# Optimizing a Trainium2 kernel written in Bass

```python
import numpy as np
import jax
import jax.numpy as jnp

def _softmax(x, axis=-1):
    return jax.nn.softmax(x, axis=axis)

def _gelu(x):
    return jax.nn.gelu(x, approximate=True)

def _silu(x):
    return jax.nn.silu(x)

def _sigmoid(x):
    return jax.nn.sigmoid(x)

def _layernorm(x, axis=-1, eps=1e-05):
    m = jnp.mean(x, axis=axis, keepdims=True)
    v = jnp.var(x, axis=axis, keepdims=True)
    return (x - m) / jnp.sqrt(v + eps)

def _scatter_add(tgt, idx, src, axis=0):
    return tgt.at[idx].add(src)

def _segment_sum(src, seg, n):
    return jax.ops.segment_sum(src, seg, n)
kernel_name = 'mk_cond_seq_d4_seqx_r8_6bc75e'

def setup_inputs(seed: int=0):
    np.random.seed(seed)
    _w = jnp.asarray

    def _rec_inputs():
        import jax
        import jax.numpy as jnp
        _rk = jax.random.key(seed)
        x = -0.0002928 + 1 * jax.random.normal(jax.random.fold_in(_rk, 1), (16, 128, 128), jnp.float32)
        _lenS = 128 - jax.random.randint(jax.random.fold_in(_rk, 7), (16,), 0, max(1, 128 // 4) + 1, jnp.int32)
        _lenS2 = 128 - jax.random.randint(jax.random.fold_in(_rk, 8), (16,), 0, max(1, 128 // 4) + 1, jnp.int32)
        cond_1024 = 0.0061147 + 1.02565 * jax.random.normal(jax.random.fold_in(_rk, 11), (16, 128), jnp.float32)
        _validS = jnp.arange(128)[None, :] < _lenS[:, None]
        _validS2 = jnp.arange(128)[None, :] < _lenS2[:, None]
        _causal = jnp.tril(jnp.ones((128, 128), dtype=bool))
        mask_BxSxSx11_ik0 = jnp.where(jnp.ones((16, 128, 128, 11), dtype=bool), 0, 1).astype(jnp.int32)
        mask_Bx1xSxS_ff0 = jnp.where(jnp.ones((16, 1, 128, 128), dtype=bool), 0.0, -1000000000.0).astype(jnp.float32)
        return (x, cond_1024, mask_BxSxSx11_ik0, mask_Bx1xSxS_ff0)
    x, cond_1024, mask_BxSxSx11_ik0, mask_Bx1xSxS_ff0 = _rec_inputs()

    def _L0_cond_setup():
        import jax, jax.numpy as jnp
        import numpy as np
        EPS = 1e-05

        def _sln(h, w, ln_g, ln_b, Wg, bg, Wb, bb):
            mu = jnp.mean(h, axis=-1, keepdims=True)
            var = jnp.mean((h - mu) ** 2, axis=-1, keepdims=True)
            ln = (h - mu) / jnp.sqrt(var + EPS) * ln_g + ln_b
            gamma = (w @ Wg.T + bg)[:, None, :]
            beta = (w @ Wb.T + bb)[:, None, :]
            return gamma * ln + beta
        key = jax.random.key(seed)
        ks = jax.random.split(key, 20)
        B, N, D = (4, 128, 128)
        F = 4 * D
        s = lambda fan: 1.0 / np.sqrt(fan)
        inp = {'hidden': jax.random.normal(ks[0], (B, N, D), jnp.float32), 'w': jax.random.normal(ks[1], (B, D), jnp.float32), 'ln_g': jnp.ones((D,), jnp.float32), 'ln_b': jnp.zeros((D,), jnp.float32), 'Wg': jax.random.normal(ks[2], (D, D), jnp.float32) * s(D), 'bg': jnp.zeros((D,), jnp.float32), 'Wb': jax.random.normal(ks[3], (D, D), jnp.float32) * s(D), 'bb': jnp.zeros((D,), jnp.float32), 'Wqkv': jax.random.normal(ks[4], (3 * D, D), jnp.float32) * s(D), 'bqkv': jnp.zeros((3 * D,), jnp.float32), 'Wp': jax.random.normal(ks[5], (D, D), jnp.float32) * s(D), 'bp': jnp.zeros((D,), jnp.float32), 'W1': jax.random.normal(ks[6], (F, D), jnp.float32) * s(D), 'b1': jnp.zeros((F,), jnp.float32), 'W2': jax.random.normal(ks[7], (D, F), jnp.float32) * s(F), 'b2': jnp.zeros((D,), jnp.float32), 'num_heads': 16}
        return inp
    _L0_cond_all = _L0_cond_setup()
    _L0_cond_in = {k: v for k, v in _L0_cond_all.items() if k in ('ln_g', 'ln_b', 'Wg', 'bg', 'Wb', 'bb', 'Wqkv', 'bqkv', 'Wp', 'bp', 'W1', 'b1', 'W2', 'b2')}
    del _L0_cond_all

    def _L1_cond_setup():
        import jax, jax.numpy as jnp
        import numpy as np
        NONGT = 20
        H = 16
        NEG = -9000000000000000.0

        def _gat_attention(self_feat, cond_adj, label_bias, Wq, bq, Wk, bk, Wout, bout):
            B, N, F = self_feat.shape
            ng = min(NONGT, N)
            dh = F // H
            kv = self_feat[:, :ng]
            qh = (self_feat @ Wq.T + bq).reshape(B, N, H, dh)
            kh = (kv @ Wk.T + bk).reshape(B, ng, H, dh)
            aff = jnp.einsum('bnhd,bmhd->bnhm', qh, kh) * (1.0 / np.sqrt(dh))
            mask = cond_adj[:, :, None, :] > 0
            aff = jnp.where(mask, aff, NEG) + label_bias[:, :, None, :]
            w = jax.nn.softmax(aff, axis=-1)
            out_t = jnp.einsum('bnhm,bmf->bnhf', w, kv)
            out = jnp.einsum('bnhf,hgf->bnhg', out_t, Wout) + bout.reshape(H, F // H)
            return out.reshape(B, N, F)

        def _forward(v, q, adj, W_self, b_self, w_bias, b_bias, Wq, bq, Wk, bk, Wout, bout):
            adj_f = adj.astype(jnp.float32)
            exp_v = v
            row_zero = exp_v.sum(-1) == 0
            q_exp = jnp.where(row_zero[..., None], 0.0, q[:, None, :])
            vcq = jnp.concatenate([exp_v, q_exp], axis=-1)
            self_feat = vcq @ W_self.T + b_self
            output = self_feat
            for d in range(2):
                A = adj_f if d == 0 else jnp.swapaxes(adj_f, 1, 2)
                A = A[:, :, :NONGT, :]
                cond = A.sum(-1)
                vb = A @ w_bias + b_bias
                output = output + _gat_attention(self_feat, cond, vb, Wq[d], bq[d], Wk[d], bk[d], Wout[d], bout[d])
            rel = jax.nn.relu(output)
            return exp_v + rel
        key = jax.random.key(seed)
        ks = jax.random.split(key, 8)
        B, N, L, F, Q = (32, 36, 11, 128, 128)
        IN = F + Q
        s = 0.02
        return {'v': jax.random.normal(ks[0], (B, N, F), jnp.float32), 'q': jax.random.normal(ks[1], (B, Q), jnp.float32), 'adj': jax.random.randint(ks[2], (B, N, N, L), 0, 2, jnp.int32), 'W_self': jax.random.normal(ks[3], (F, IN), jnp.float32) * s, 'b_self': jnp.zeros((F,), jnp.float32), 'w_bias': jax.random.normal(ks[4], (L,), jnp.float32) * s, 'b_bias': jnp.zeros((), jnp.float32), 'Wq': jax.random.normal(ks[5], (2, F, F), jnp.float32) * s, 'bq': jnp.zeros((2, F), jnp.float32), 'Wk': jax.random.normal(ks[6], (2, F, F), jnp.float32) * s, 'bk': jnp.zeros((2, F), jnp.float32), 'Wout': jax.random.normal(ks[7], (2, H, F // H, F), jnp.float32) * s, 'bout': jnp.zeros((2, F), jnp.float32)}
    _L1_cond_all = _L1_cond_setup()
    _L1_cond_in = {k: v for k, v in _L1_cond_all.items() if k in ('W_self', 'b_self', 'w_bias', 'b_bias', 'Wq', 'bq', 'Wk', 'bk', 'Wout', 'bout')}
    del _L1_cond_all

    def _L2_cond_setup():
        import jax, jax.numpy as jnp
        import numpy as np
        from jax.scipy.special import erf
        MODEL_DIM = 128
        NUM_HEADS = 16
        HEAD_DIM = 64
        FF_MULT = 4
        ROT_DIM = 32
        SCALE = HEAD_DIM ** (-0.5)
        LN_EPS = 1e-05

        def fused_gelu(x):
            return x * 0.5 * (1.0 + erf(x / 1.41421))

        def rotate_half(x):
            x1, x2 = jnp.split(x, 2, axis=-1)
            return jnp.concatenate([-x2, x1], axis=-1)

        def rope_sin_cos(seq_len, dtype=jnp.bfloat16):
            inv_freq = 1.0 / 10000.0 ** (jnp.arange(0, ROT_DIM, 2, dtype=jnp.float32) / ROT_DIM)
            t = jnp.arange(seq_len, dtype=jnp.float32)
            freqs = jnp.einsum('i,j->ij', t, inv_freq)
            emb = jnp.concatenate([freqs, freqs], axis=-1)
            sin = jnp.sin(emb)[None, None, :, :].astype(dtype)
            cos = jnp.cos(emb)[None, None, :, :].astype(dtype)
            return (sin, cos)
        key = jax.random.key(seed)
        ks = jax.random.split(key, 10)
        B, S, D = (2, 256, MODEL_DIM)
        fused = 3 * NUM_HEADS * HEAD_DIM + 2 * FF_MULT * D
        s = lambda fan_in: 1.0 / np.sqrt(fan_in)
        return {'hidden_states': jax.random.normal(ks[0], (B, S, D), jnp.float32), 'attention_mask': jnp.zeros((B, 1, S, S), jnp.float32), 'time_embeds': jax.random.normal(ks[1], (B, 1, D), jnp.float32), 'ln_w': jnp.ones((D,), jnp.float32), 'ln_b': jnp.zeros((D,), jnp.float32), 'cond_w': jax.random.uniform(ks[2], (D, 2 * D), jnp.float32, -s(D), s(D)), 'cond_b': jnp.zeros((2 * D,), jnp.float32), 'proj_in_w': jax.random.uniform(ks[3], (D, fused), jnp.float32, -s(D), s(D)), 'attn_proj_w': jax.random.uniform(ks[4], (NUM_HEADS * HEAD_DIM, D), jnp.float32, -s(D), s(D)), 'attn_proj_b': jnp.zeros((D,), jnp.float32), 'ff_proj_w': jax.random.uniform(ks[5], (FF_MULT * D, D), jnp.float32, -s(FF_MULT * D), s(FF_MULT * D)), 'ff_proj_b': jnp.zeros((D,), jnp.float32)}
    _L2_cond_all = _L2_cond_setup()
    _L2_cond_in = {k: v for k, v in _L2_cond_all.items() if k in ('ln_w', 'ln_b', 'cond_w', 'cond_b', 'proj_in_w', 'attn_proj_w', 'attn_proj_b', 'ff_proj_w', 'ff_proj_b')}
    del _L2_cond_all

    def _L3_cond_setup():
        import jax, jax.numpy as jnp
        import numpy as np
        EPS_RMS = 1e-06
        EPS_Q = 1e-05

        def _weight_quant(w):
            scale = 1.0 / jnp.clip(jnp.mean(jnp.abs(w)), EPS_Q)
            wq = jnp.clip(jnp.round(w * scale), -1.0, 1.0) / scale
            return w + jax.lax.stop_gradient(wq - w)

        def _activation_quant(x):
            scale = 127.0 / jnp.clip(jnp.max(jnp.abs(x), axis=-1, keepdims=True), EPS_Q)
            xq = jnp.clip(jnp.round(x * scale), -128.0, 127.0) / scale
            return x + jax.lax.stop_gradient(xq - x)

        def _rmsnorm(x, weight):
            inv = jax.lax.rsqrt(jnp.mean(x * x, axis=-1, keepdims=True) + EPS_RMS)
            return x * inv * weight
        key = jax.random.key(seed)
        k1, k2, k3 = jax.random.split(key, 3)
        B, S, D, CD = (8, 512, 128, 128)
        x = jax.random.normal(k1, (B, S, D), dtype=jnp.float32)
        c = jax.random.normal(k2, (B, CD), dtype=jnp.float32)
        w_proj = jax.random.normal(k3, (2 * D, CD), dtype=jnp.float32) * 0.02
        b_proj = jnp.zeros((2 * D,), dtype=jnp.float32)
        rms_weight = jnp.ones((D,), dtype=jnp.float32)
        return {'x': x, 'c': c, 'w_proj': w_proj, 'b_proj': b_proj, 'rms_weight': rms_weight}
    _L3_cond_all = _L3_cond_setup()
    _L3_cond_in = {k: v for k, v in _L3_cond_all.items() if k in ('w_proj', 'b_proj', 'rms_weight')}
    del _L3_cond_all
    return {'x': x, 'cond_1024': cond_1024, 'mask_BxSxSx11_ik0': mask_BxSxSx11_ik0, 'mask_Bx1xSxS_ff0': mask_Bx1xSxS_ff0, 'L0_cond_ln_g': _L0_cond_in['ln_g'], 'L0_cond_ln_b': _L0_cond_in['ln_b'], 'L0_cond_Wg': _L0_cond_in['Wg'], 'L0_cond_bg': _L0_cond_in['bg'], 'L0_cond_Wb': _L0_cond_in['Wb'], 'L0_cond_bb': _L0_cond_in['bb'], 'L0_cond_Wqkv': _L0_cond_in['Wqkv'], 'L0_cond_bqkv': _L0_cond_in['bqkv'], 'L0_cond_Wp': _L0_cond_in['Wp'], 'L0_cond_bp': _L0_cond_in['bp'], 'L0_cond_W1': _L0_cond_in['W1'], 'L0_cond_b1': _L0_cond_in['b1'], 'L0_cond_W2': _L0_cond_in['W2'], 'L0_cond_b2': _L0_cond_in['b2'], 'L1_cond_W_self': _L1_cond_in['W_self'], 'L1_cond_b_self': _L1_cond_in['b_self'], 'L1_cond_w_bias': _L1_cond_in['w_bias'], 'L1_cond_b_bias': _L1_cond_in['b_bias'], 'L1_cond_Wq': _L1_cond_in['Wq'], 'L1_cond_bq': _L1_cond_in['bq'], 'L1_cond_Wk': _L1_cond_in['Wk'], 'L1_cond_bk': _L1_cond_in['bk'], 'L1_cond_Wout': _L1_cond_in['Wout'], 'L1_cond_bout': _L1_cond_in['bout'], 'L2_cond_ln_w': _L2_cond_in['ln_w'], 'L2_cond_ln_b': _L2_cond_in['ln_b'], 'L2_cond_cond_w': _L2_cond_in['cond_w'], 'L2_cond_cond_b': _L2_cond_in['cond_b'], 'L2_cond_proj_in_w': _L2_cond_in['proj_in_w'], 'L2_cond_attn_proj_w': _L2_cond_in['attn_proj_w'], 'L2_cond_attn_proj_b': _L2_cond_in['attn_proj_b'], 'L2_cond_ff_proj_w': _L2_cond_in['ff_proj_w'], 'L2_cond_ff_proj_b': _L2_cond_in['ff_proj_b'], 'L3_cond_w_proj': _L3_cond_in['w_proj'], 'L3_cond_b_proj': _L3_cond_in['b_proj'], 'L3_cond_rms_weight': _L3_cond_in['rms_weight']}

def reference(x, cond_1024, mask_BxSxSx11_ik0, mask_Bx1xSxS_ff0, L0_cond_ln_g, L0_cond_ln_b, L0_cond_Wg, L0_cond_bg, L0_cond_Wb, L0_cond_bb, L0_cond_Wqkv, L0_cond_bqkv, L0_cond_Wp, L0_cond_bp, L0_cond_W1, L0_cond_b1, L0_cond_W2, L0_cond_b2, L1_cond_W_self, L1_cond_b_self, L1_cond_w_bias, L1_cond_b_bias, L1_cond_Wq, L1_cond_bq, L1_cond_Wk, L1_cond_bk, L1_cond_Wout, L1_cond_bout, L2_cond_ln_w, L2_cond_ln_b, L2_cond_cond_w, L2_cond_cond_b, L2_cond_proj_in_w, L2_cond_attn_proj_w, L2_cond_attn_proj_b, L2_cond_ff_proj_w, L2_cond_ff_proj_b, L3_cond_w_proj, L3_cond_b_proj, L3_cond_rms_weight):
    import jax
    import jax.numpy as jnp

    def _L0_cond_ref(hidden, w, ln_g, ln_b, Wg, bg, Wb, bb, Wqkv, bqkv, Wp, bp, W1, b1, W2, b2, num_heads):
        import jax, jax.numpy as jnp
        import numpy as np
        EPS = 1e-05

        def _sln(h, w, ln_g, ln_b, Wg, bg, Wb, bb):
            mu = jnp.mean(h, axis=-1, keepdims=True)
            var = jnp.mean((h - mu) ** 2, axis=-1, keepdims=True)
            ln = (h - mu) / jnp.sqrt(var + EPS) * ln_g + ln_b
            gamma = (w @ Wg.T + bg)[:, None, :]
            beta = (w @ Wb.T + bb)[:, None, :]
            return gamma * ln + beta
        B, N, D = hidden.shape
        hd = D // num_heads
        h = _sln(hidden, w, ln_g, ln_b, Wg, bg, Wb, bb)
        qkv = (h @ Wqkv.T + bqkv).reshape(B, N, num_heads, hd, 3)
        q = jnp.moveaxis(qkv[..., 0], 2, 1)
        k = jnp.moveaxis(qkv[..., 1], 2, 1)
        v = jnp.moveaxis(qkv[..., 2], 2, 1)
        energy = jnp.einsum('bhqd,bhkd->bhqk', q, k)
        att = jax.nn.softmax(energy, axis=-1) / D ** 0.5
        out = jnp.einsum('bhqk,bhkd->bhqd', att, v)
        out = jnp.moveaxis(out, 1, 2).reshape(B, N, D)
        out = out @ Wp.T + bp
        h1 = out + hidden
        h2 = _sln(h1, w, ln_g, ln_b, Wg, bg, Wb, bb)
        return h2 + h1

    def _L1_cond_ref(v, q, adj, W_self, b_self, w_bias, b_bias, Wq, bq, Wk, bk, Wout, bout):
        import jax, jax.numpy as jnp
        import numpy as np
        NONGT = 20
        H = 16
        NEG = -9000000000000000.0

        def _gat_attention(self_feat, cond_adj, label_bias, Wq, bq, Wk, bk, Wout, bout):
            B, N, F = self_feat.shape
            ng = min(NONGT, N)
            dh = F // H
            kv = self_feat[:, :ng]
            qh = (self_feat @ Wq.T + bq).reshape(B, N, H, dh)
            kh = (kv @ Wk.T + bk).reshape(B, ng, H, dh)
            aff = jnp.einsum('bnhd,bmhd->bnhm', qh, kh) * (1.0 / np.sqrt(dh))
            mask = cond_adj[:, :, None, :] > 0
            aff = jnp.where(mask, aff, NEG) + label_bias[:, :, None, :]
            w = jax.nn.softmax(aff, axis=-1)
            out_t = jnp.einsum('bnhm,bmf->bnhf', w, kv)
            out = jnp.einsum('bnhf,hgf->bnhg', out_t, Wout) + bout.reshape(H, F // H)
            return out.reshape(B, N, F)

        def _forward(v, q, adj, W_self, b_self, w_bias, b_bias, Wq, bq, Wk, bk, Wout, bout):
            adj_f = adj.astype(jnp.float32)
            exp_v = v
            row_zero = exp_v.sum(-1) == 0
            q_exp = jnp.where(row_zero[..., None], 0.0, q[:, None, :])
            vcq = jnp.concatenate([exp_v, q_exp], axis=-1)
            self_feat = vcq @ W_self.T + b_self
            output = self_feat
            for d in range(2):
                A = adj_f if d == 0 else jnp.swapaxes(adj_f, 1, 2)
                A = A[:, :, :NONGT, :]
                cond = A.sum(-1)
                vb = A @ w_bias + b_bias
                output = output + _gat_attention(self_feat, cond, vb, Wq[d], bq[d], Wk[d], bk[d], Wout[d], bout[d])
            rel = jax.nn.relu(output)
            return exp_v + rel
        return _forward(v, q, adj, W_self, b_self, w_bias, b_bias, Wq, bq, Wk, bk, Wout, bout)

    def _L2_cond_ref(hidden_states, attention_mask, time_embeds, ln_w, ln_b, cond_w, cond_b, proj_in_w, attn_proj_w, attn_proj_b, ff_proj_w, ff_proj_b):
        import jax, jax.numpy as jnp
        import numpy as np
        from jax.scipy.special import erf
        MODEL_DIM = 128
        NUM_HEADS = 16
        HEAD_DIM = 64
        FF_MULT = 4
        ROT_DIM = 32
        SCALE = HEAD_DIM ** (-0.5)
        LN_EPS = 1e-05

        def fused_gelu(x):
            return x * 0.5 * (1.0 + erf(x / 1.41421))

        def rotate_half(x):
            x1, x2 = jnp.split(x, 2, axis=-1)
            return jnp.concatenate([-x2, x1], axis=-1)

        def rope_sin_cos(seq_len, dtype=jnp.bfloat16):
            inv_freq = 1.0 / 10000.0 ** (jnp.arange(0, ROT_DIM, 2, dtype=jnp.float32) / ROT_DIM)
            t = jnp.arange(seq_len, dtype=jnp.float32)
            freqs = jnp.einsum('i,j->ij', t, inv_freq)
            emb = jnp.concatenate([freqs, freqs], axis=-1)
            sin = jnp.sin(emb)[None, None, :, :].astype(dtype)
            cos = jnp.cos(emb)[None, None, :, :].astype(dtype)
            return (sin, cos)
        B, S, D = hidden_states.shape
        mu = jnp.mean(hidden_states, axis=-1, keepdims=True)
        var = jnp.mean(jnp.square(hidden_states - mu), axis=-1, keepdims=True)
        units = (hidden_states - mu) * jax.lax.rsqrt(var + LN_EPS) * ln_w + ln_b
        sb = jax.nn.silu(time_embeds) @ cond_w + cond_b
        scale, bias = jnp.split(sb, 2, axis=-1)
        units = (1.0 + scale) * units + bias
        proj = units @ proj_in_w
        hd = NUM_HEADS * HEAD_DIM
        q, k, v, ff, ff_gate = jnp.split(proj, np.cumsum([hd, hd, hd, FF_MULT * D])[:4], axis=-1)
        split_heads = lambda x: x.reshape(B, S, NUM_HEADS, HEAD_DIM).transpose(0, 2, 1, 3)
        q, k, v = (split_heads(q), split_heads(k), split_heads(v))
        sin, cos = rope_sin_cos(S)
        q_l, q_r = (q[..., :ROT_DIM], q[..., ROT_DIM:])
        k_l, k_r = (k[..., :ROT_DIM], k[..., ROT_DIM:])
        q = jnp.concatenate([q_l * cos + rotate_half(q_l) * sin, q_r], axis=-1)
        k = jnp.concatenate([k_l * cos + rotate_half(k_l) * sin, k_r], axis=-1)
        score = jnp.einsum('bhsd,bhSd->bhsS', q * SCALE, k * SCALE) + attention_mask
        weight = jax.nn.softmax(score, axis=-1)
        attn = jnp.einsum('bhsS,bhSd->bhsd', weight, v)
        concat = attn.transpose(0, 2, 1, 3).reshape(B, S, hd)
        attn_out = concat @ attn_proj_w + attn_proj_b
        ff_out = ff * fused_gelu(ff_gate) @ ff_proj_w + ff_proj_b
        return hidden_states + attn_out + ff_out

    def _L3_cond_ref(x, c, w_proj, b_proj, rms_weight):
        import jax, jax.numpy as jnp
        import numpy as np
        EPS_RMS = 1e-06
        EPS_Q = 1e-05

        def _weight_quant(w):
            scale = 1.0 / jnp.clip(jnp.mean(jnp.abs(w)), EPS_Q)
            wq = jnp.clip(jnp.round(w * scale), -1.0, 1.0) / scale
            return w + jax.lax.stop_gradient(wq - w)

        def _activation_quant(x):
            scale = 127.0 / jnp.clip(jnp.max(jnp.abs(x), axis=-1, keepdims=True), EPS_Q)
            xq = jnp.clip(jnp.round(x * scale), -128.0, 127.0) / scale
            return x + jax.lax.stop_gradient(xq - x)

        def _rmsnorm(x, weight):
            inv = jax.lax.rsqrt(jnp.mean(x * x, axis=-1, keepdims=True) + EPS_RMS)
            return x * inv * weight
        if c.ndim == 2:
            c = c[:, None, :]
        cq = _activation_quant(c)
        wq = _weight_quant(w_proj)
        emb = jnp.einsum('btc,dc->btd', cq, wq) + b_proj
        scale, shift = jnp.split(emb, 2, axis=-1)
        xn = _rmsnorm(x, rms_weight)
        return xn * (1.0 + scale) + shift
    x = _L0_cond_ref(x, cond_1024, L0_cond_ln_g, L0_cond_ln_b, L0_cond_Wg, L0_cond_bg, L0_cond_Wb, L0_cond_bb, L0_cond_Wqkv, L0_cond_bqkv, L0_cond_Wp, L0_cond_bp, L0_cond_W1, L0_cond_b1, L0_cond_W2, L0_cond_b2, 16)
    x = _L1_cond_ref(x, cond_1024, mask_BxSxSx11_ik0, L1_cond_W_self, L1_cond_b_self, L1_cond_w_bias, L1_cond_b_bias, L1_cond_Wq, L1_cond_bq, L1_cond_Wk, L1_cond_bk, L1_cond_Wout, L1_cond_bout)
    x = _L2_cond_ref(x, mask_Bx1xSxS_ff0, cond_1024[:, None, :], L2_cond_ln_w, L2_cond_ln_b, L2_cond_cond_w, L2_cond_cond_b, L2_cond_proj_in_w, L2_cond_attn_proj_w, L2_cond_attn_proj_b, L2_cond_ff_proj_w, L2_cond_ff_proj_b)
    x = _L3_cond_ref(x, cond_1024, L3_cond_w_proj, L3_cond_b_proj, L3_cond_rms_weight)
    return x

_drawn_inputs = setup_inputs


def setup_inputs(seed=0):
    import zlib

    import numpy as np

    out = dict(_drawn_inputs(seed))
    spreads = {'L0_cond_ln_g': (1.0, 0.2),
     'L0_cond_ln_b': (0.0, 0.1),
     'L0_cond_bg': (0.0, 0.1),
     'L0_cond_bb': (0.0, 0.1),
     'L0_cond_bqkv': (0.0, 0.8),
     'L0_cond_bp': (0.0, 0.1),
     'L0_cond_b1': (0.0, 0.1),
     'L0_cond_b2': (0.0, 0.1),
     'L1_cond_b_self': (0.0, 0.1),
     'L1_cond_bq': (0.0, 0.1),
     'L1_cond_bk': (0.0, 0.1),
     'L1_cond_bout': (0.0, 0.1),
     'L2_cond_ln_w': (1.0, 0.2),
     'L2_cond_ln_b': (0.0, 0.1),
     'L2_cond_cond_b': (0.0, 0.1),
     'L2_cond_attn_proj_b': (0.0, 0.1),
     'L2_cond_ff_proj_b': (0.0, 0.1),
     'L3_cond_b_proj': (0.0, 0.1),
     'L3_cond_rms_weight': (1.0, 0.2)}
    factors = {}
    for name, (base, spread) in spreads.items():
        noise = np.random.default_rng([zlib.crc32(name.encode()), seed]).standard_normal(out[name].shape)
        drawn = base * np.exp(spread * noise) if base else spread * noise
        out[name] = jnp.asarray(drawn.astype(out[name].dtype))
    for name, factor in factors.items():
        out[name] = (out[name] * factor).astype(out[name].dtype)
    return out
```

```python
from contextlib import ExitStack

import concourse.bass as bass
from concourse import mybir

F32 = mybir.dt.float32
F32R = mybir.dt.float32r
BF16 = mybir.dt.bfloat16
I32 = mybir.dt.int32
ALU = mybir.AluOpType
ACT = mybir.ActivationFunctionType
AX = mybir.AxisListType.X

NB, S, D = 16, 128, 128
P = 128
H0, HD0 = 16, 8
G = 4
NC0 = H0 // G
NG, NL = 20, 11
HC = 6
NC1 = 3
H1P = HC * NC1
GM = 4
GN = S // GM
H2, HD2, ROT = 16, 64, 32
FF = 4 * D
W2P = 3 * H2 * HD2 // NB
EPS = 1e-5
NEG = -9000000000000000.0
BIG_ROUND = 12582912.0


def columns(*pieces):
    at, out = 0, {}
    for name, width in pieces:
        out[name] = (at, at + width)
        at += width
    return out, at


W0_COLS, W0_N = columns(("q", NC0 * P), ("k", NC0 * P), ("v", D))
W1_COLS, W1_N = columns(("wp0", D), ("self", D), ("q", 2 * D), ("k", 2 * D), ("out", 2 * H1P * HD0))
WC_COLS, WC_N = columns(("gb", 2 * D), ("self_q", D), ("sb", 2 * D), ("proj", 2 * D))
ROW_COLS, ROW_N = columns(("gb0", 2 * D), ("ln_g0", D), ("ln_b0", D), ("cond_b", 2 * D), ("ln_w2", D),
                          ("ln_b2", D), ("b_proj", 2 * D), ("rms_w", D))
BC_COLS, BC_N = columns(("bv0", D), ("bp0", D), ("b_self", D), ("bout", 2 * D), ("attn_b", D), ("ff_b", D),
                        ("w_bias", NL), ("b_bias", 1))
COL_COLS, COL_N = columns(("bq1", 2), ("bk1", 2), ("part_q", 1), ("part_k", 1))
CST_COLS, CST_N = columns(("ident", P), ("bd_k", H0 * NG), ("bd_v", NC1 * HC * HD0), ("cos", ROT), ("sin", ROT), ("sel4", NC0), ("sel8", H2 // 2))


def need(engine, sem, value):
    if isinstance(value, int) and value <= 0:
        return
    engine.wait_ge(sem, value)


def slots(engine, slot, first, last, total):
    for t in range(first):
        slot(t, t % 2)
    with engine.Fori(first // 2, last // 2) as i:
        for u in range(2):
            slot(2 * i + u, u)
    for t in range(last, total):
        slot(t, t % 2)


def one(b):
    return slice(b, b + 1) if isinstance(b, int) else bass.ds(b, 1)


def live(b):
    return not isinstance(b, int) or 0 <= b < NB


def build(nc, x, cond_t, cond_r, w0, bias_qk0, w1, wc, rows, bc, cols, cst_d, adj, w2, attn_w, ff_w, mask, mask_t, out):
    ctx = ExitStack()
    with ctx:
        def sb(name, shape, dt=F32, where=ctx):
            return where.enter_context(nc.sbuf_tensor(name, shape, dt))

        def sem(name):
            return ctx.enter_context(nc.semaphore(name))

        bank = [ctx.enter_context(nc.psum_tensor(f"bank{i}", [P, 512], F32)) for i in range(8)]

        X = sb("X", [P, NB, D])
        bc_sb = sb("bc_sb", [P, BC_N])
        cols_sb = sb("cols_sb", [P, COL_N])
        cst_sb = sb("cst_sb", [P, CST_N])
        carrier = sb("carrier", [P, 1])
        identB = sb("identB", [P, P], BF16)
        sel0 = sb("sel0", [P, NC0, P], BF16)
        eps_c = sb("eps_c", [P, 1])
        neg_half = sb("neg_half", [P, NB])
        AB0T = sb("AB0T", [P, 2, NB])
        AB2T = sb("AB2T", [P, 2, NB])

        w1_sb = sb("w1_sb", [P, W1_N])
        w2h = sb("w2h", [P, 3 * H2 * HD2], F32R)
        w2l = sb("w2l", [P, 3 * H2 * HD2], F32R)
        w_ff = sb("w_ff", [P, 2 * FF])
        w_at = sb("w_at", [P, H2 * HD2 // P, D])
        w_fo = sb("w_fo", [P, FF // P, D])

        def bcv(name):
            a, b = BC_COLS[name]
            return bc_sb[:, a:b]

        def cst(name):
            a, b = CST_COLS[name]
            return cst_sb[:, a:b]

        ident = cst("ident")

        early = ExitStack()
        l0 = early
        AB0 = sb("AB0", [P, NB, 2 * D], F32, l0)
        w0_sb = sb("w0_sb", [P, W0_N], F32, l0)
        bqk_raw = sb("bqk_raw", [NC0, 2 * P], F32, l0)
        bqk_part = sb("bqk_part", [NC0, 3, 2 * P], BF16, l0)
        bqk_rest = sb("bqk_rest", [NC0, 2, 2 * P], F32, l0)
        bqk = sb("bqk", [3 * NC0, 2 * P], BF16, l0)
        sel12 = sb("sel12", [3 * NC0, NC0, S], BF16, l0)
        mean0 = sb("mean0", [P, NB, 2], F32, l0)
        rstd0 = sb("rstd0", [P, NB], F32, l0)
        xn = sb("xn", [P, D], F32, l0)
        ut = sb("ut", [P, D], F32, l0)
        rnd = sb("rnd", [P, 2, NC0 * P], F32R, l0)
        pack = sb("pack", [P, 2, 2, NC0, S], F32R, l0)
        V0 = sb("V0", [P, 2, H0, HD0 + 1], F32, l0)
        m0 = sb("m0", [P, G, NC0], F32, l0)
        nm0 = sb("nm0", [P, P], BF16, l0)
        mT0 = sb("mT0", [P, S], BF16, l0)
        P0 = sb("P0", [P, 2, G * S], F32, l0)
        rc0 = sb("rc0", [P, H0], F32, l0)
        at0 = sb("at0", [P, D], F32, l0)
        at0T = sb("at0T", [P, D], F32, l0)
        xb0 = sb("xb0", [P, D], F32, l0)
        h1 = sb("h1", [P, 2, D], F32, l0)
        st0 = sb("st0", [P, 6], F32, l0)
        mv0 = sb("mv0", [P, 2, 2], F32, l0)
        ve0 = sb("ve0", [P, 1], F32, l0)
        rs0 = sb("rs0", [P, 2, 1], F32, l0)
        hb0 = sb("hb0", [P, 2, D], F32, l0)
        tn0 = sb("tn0", [P, D], F32, l0)

        l1 = early
        QP1 = sb("QP1", [P, NB, D], F32, l1)
        adj0 = sb("adj0", [P, NB, NG * NL], I32, l1)
        adj1 = sb("adj1", [GM * NG, NB, GN * NL], I32, l1)
        labF0 = sb("labF0", [P, NG * NL], F32, l1)
        labF1 = sb("labF1", [GM * NG, GN * NL], F32, l1)
        lab0 = sb("lab0", [P, NG * NL], F32, l1)
        lab1 = sb("lab1", [GM * NG, GN * NL], F32, l1)
        cnt0 = sb("cnt0", [P, NB, NG], F32, l1)
        cnt1 = sb("cnt1", [GM * NG, NB, GN], F32, l1)
        vb0 = sb("vb0", [P, NB, NG], F32, l1)
        vb1 = sb("vb1", [GM * NG, NB, GN], F32, l1)
        w2raw = sb("w2raw", [P, 3 * H2 * HD2], F32, early)

        raw = ExitStack()
        siluT = sb("siluT", [P, NB], F32, raw)
        cabs = sb("cabs", [NB, D], F32, raw)
        wabs = sb("wabs", [P, 2 * D], F32, raw)
        onesP = sb("onesP", [P, P], F32, raw)
        sb2 = sb("sb2", [NB, 2 * D], F32, raw)
        R2 = sb("R2", [NB, 2 * D], F32, raw)
        R3 = sb("R3", [NB, 2 * D], F32, raw)
        emb3 = sb("emb3", [NB, 2 * D], F32, raw)
        cq = sb("cq", [NB, D], F32, raw)
        cq_s = sb("cq_s", [NB, 3], F32, raw)
        wq = sb("wq", [P, 2 * D], F32, raw)
        wq_s = sb("wq_s", [P, 3], F32, raw)
        cqT = sb("cqT", [P, NB], F32, raw)
        condT = sb("condT", [P, NB], F32, raw)
        condR = sb("condR", [NB, D], F32, raw)
        wc_sb = sb("wc_sb", [P, WC_N], F32, raw)
        rows_sb = sb("rows_sb", [NB, ROW_N], F32, raw)
        gb0 = sb("gb0", [NB, 2 * D], F32, raw)
        R0 = sb("R0", [NB, 2 * D], F32, raw)
        st_all = sb("st_all", [P, NB, 6], F32, raw)

        raw.close()

        Bc = sb("Bc", [P, NB, 2, NG], F32, l1)
        xs = sb("xs", [P, D], F32, l1)
        rsum = sb("rsum", [P, 1], F32, l1)
        nz = sb("nz", [P, 1], F32, l1)
        xT1 = sb("xT1", [P, S], F32, l1)
        cpart = sb("cpart", [P, D], F32, l1)
        selfTok = sb("selfTok", [P, 2, D], F32, l1)
        selfT = sb("selfT", [P, S], F32, l1)
        selfR = sb("selfR", [P, HC, NG], F32, l1)
        qT1 = sb("qT1", [P, 2, 2, S], F32, l1)
        kbd = sb("kbd", [P, 2, 2, H0 * NG], F32, l1)
        VW = sb("VW", [HC * NG, 2, 2, H1P, HD0 + 1], F32, l1)
        aff = sb("aff", [P, 2, H0 * NG], F32, l1)
        mx1 = sb("mx1", [P, 2, H0], F32, l1)
        ex1 = sb("ex1", [P, 2, H1P * NG], F32, l1)
        exT = sb("exT", [HC * NG, 2, NC1 * S], F32, l1)
        rc1 = sb("rc1", [P, 2, H0], F32, l1)
        on1 = sb("on1", [P, 2, D], F32, l1)
        sum1 = sb("sum1", [P, 3, D], F32, l1)
        bout1 = sb("bout1", [P, D], F32, l1)
        qp_r = sb("qp_r", [NB, D], F32, l1)

        early.close()

        HC2 = H2 * HD2 // P
        AB3 = sb("AB3", [P, NB, 2 * D])
        maskN = sb("maskN", [P, NB, S])
        maskT = sb("maskT", [P, NB, S])
        sel2 = sb("sel2", [P, HC2, P], BF16)
        st2 = sb("st2", [P, 6])
        mv2 = sb("mv2", [P, 2])
        ve2 = sb("ve2", [P, 1])
        rs2 = sb("rs2", [P, 1])
        xn2 = sb("xn2", [P, D])
        uT2 = sb("uT2", [P, 2, S])
        uTh = sb("uTh", [P, 2, S], F32R)
        uTl = sb("uTl", [P, 2, S], F32R)
        qkt = sb("qkt", [P, 2, 8 * HD2])
        rcos = sb("rcos", [P, 8, ROT])
        rsin = sb("rsin", [P, 8, ROT])
        qkT = sb("qkT", [P, 2, 2, HC2, S])
        qkB = sb("qkB", [P, 2, HC2, S], BF16)
        V2 = sb("V2", [P, 2, H2, HD2 + 1])
        mask_b = sb("mask_b", [P, S])
        junk = sb("junk", [P, S])
        m2 = sb("m2", [P, 2, HC2])
        mr2 = sb("mr2", [P, 2, 2, HC2])
        nm2 = sb("nm2", [P, P], BF16)
        mT2 = sb("mT2", [P, S], BF16)
        P2 = sb("P2", [P, 2, G * S])
        rc2 = sb("rc2", [P, 2, G])
        O2 = sb("O2", [P, HC2, 2, HD2])
        OT2 = sb("OT2", [P, HC2, S])
        gel = sb("gel", [P, FF // P, S])
        ffT = sb("ffT", [P, 2, FF // P, S])
        xb2 = sb("xb2", [P, D])
        bsum2 = sb("bsum2", [P, D])
        x3 = sb("x3", [P, D])
        sq3 = sb("sq3", [P, D])
        ss3 = sb("ss3", [P, 1])
        ms3 = sb("ms3", [P, 1])
        rs3 = sb("rs3", [P, 1])
        y3 = sb("y3", [P, D])

        scr0 = nc.dram_tensor("scr0", (NB, 2 * D), F32, kind="Internal").ap()
        scr3 = nc.dram_tensor("scr3", (NB, 2 * D), F32, kind="Internal").ap()
        scr1 = nc.dram_tensor("scr1", (NB, D), F32, kind="Internal").ap()

        def w1c(name):
            a, b = W1_COLS[name]
            return w1_sb[:, a:b]

        def row(name):
            a, b = ROW_COLS[name]
            return rows_sb[:, a:b]

        def w0c(name):
            a, b = W0_COLS[name]
            return w0_sb[:, a:b]

        def wcc(name):
            a, b = WC_COLS[name]
            return wc_sb[:, a:b]

        d_x = [sem(f"d_x{n}") for n in range(4)]
        d_cond, d_w0, d_bc, d_w1 = sem("d_cond"), sem("d_w0"), sem("d_bc"), sem("d_w1")
        d_scr0, d_ab0, d_bqk = sem("d_scr0"), sem("d_ab0"), sem("d_bqk")
        s_const = sem("s_const")
        s_idr = sem("s_idr")
        s_gb0, s_R0, s_R0T, s_AB0T = sem("s_gb0"), sem("s_R0"), sem("s_R0T"), sem("s_AB0T")
        s_st, s_mean0, s_ve, s_rstd0 = sem("s_st"), sem("s_mean0"), sem("s_ve"), sem("s_rstd0")
        s_bq = sem("s_bq")
        d_out = sem("d_out")
        s_qp, s_qpr, d_scr1, d_qp = sem("s_qp"), sem("s_qpr"), sem("d_scr1"), sem("d_qp")
        d_adj = sem("d_adj")
        d_w2, d_wo, d_mask, d_scr3, d_ab3 = sem("d_w2"), sem("d_wo"), sem("d_mask"), sem("d_scr3"), sem("d_ab3")
        s_act = sem("s_act")
        s_q = sem("s_q")
        s_p = sem("s_p")
        s_cqT, s_R2, s_R2T, s_R3 = sem("s_cqT"), sem("s_R2"), sem("s_R2T"), sem("s_R3")
        s_one = sem("s_one")

        a_xn = sem("a_xn")
        a_xnT = sem("a_xnT")
        a_u = sem("a_u")
        a_qk = sem("a_qk")
        a_v = sem("a_v")
        a_rnd = sem("a_rnd")
        a_pack = sem("a_pack")
        a_V = sem("a_V")
        a_S = sem("a_S")
        a_max = sem("a_max")
        a_nm = sem("a_nm")
        a_mT = sem("a_mT")
        a_mTs = sem("a_mTs")
        a_ST = sem("a_ST")
        a_P = sem("a_P")
        a_PV = sem("a_PV")
        a_rc = sem("a_rc")
        a_at = sem("a_at")
        a_atT = sem("a_atT")
        a_atS = sem("a_atS")
        a_o = sem("a_o")
        a_xb = sem("a_xb")
        a_h1 = sem("a_h1")
        a_bn = sem("a_bn")
        a_ve = sem("a_ve")
        a_rs = sem("a_rs")
        a_hb = sem("a_hb")
        a_tn = sem("a_tn")
        a_x1 = sem("a_x1")

        g_flt = sem("g_flt")
        g_lab = sem("g_lab")
        g_cnt = sem("g_cnt")
        g_vb = sem("g_vb")
        g_bc = sem("g_bc")
        g_bcT = sem("g_bcT")
        g_pad = sem("g_pad")

        b_xs = sem("b_xs")
        b_rs = sem("b_rs")
        b_nz = sem("b_nz")
        b_cp = sem("b_cp")
        b_xT = sem("b_xT")
        b_xTs = sem("b_xTs")
        b_sf = sem("b_sf")
        b_self = sem("b_self")
        b_sT = sem("b_sT")
        b_sTs = sem("b_sTs")
        b_q = sem("b_q")
        b_qs = sem("b_qs")
        b_kv = sem("b_kv")
        b_kbd = sem("b_kbd")
        b_VW = sem("b_VW")
        b_S = sem("b_S")
        b_aff = sem("b_aff")
        b_mx = sem("b_mx")
        b_sub = sem("b_sub")
        b_ex = sem("b_ex")
        b_eT = sem("b_eT")
        b_eTs = sem("b_eTs")
        b_PV = sem("b_PV")
        b_rc = sem("b_rc")
        b_on = sem("b_on")
        b_sum = sem("b_sum")
        b_x2 = sem("b_x2")

        e_h = sem("e_h")
        e_l = sem("e_l")

        c_const = sem("c_const")
        c_bn = sem("c_bn")
        c_ve = sem("c_ve")
        c_rs = sem("c_rs")
        c_xn = sem("c_xn")
        c_xT = sem("c_xT")
        c_u = sem("c_u")
        c_ul = sem("c_ul")
        c_pj = sem("c_pj")
        c_cp = sem("c_cp")
        c_rope = sem("c_rope")
        c_rot = sem("c_rot")
        c_T = sem("c_T")
        c_Ts = sem("c_Ts")
        c_B = sem("c_B")
        c_V = sem("c_V")
        c_gel = sem("c_gel")
        c_ff = sem("c_ff")
        c_G = sem("c_G")
        c_mk = sem("c_mk")
        c_jk = sem("c_jk")
        c_nm = sem("c_nm")
        c_mT = sem("c_mT")
        c_mTs = sem("c_mTs")
        c_ST = sem("c_ST")
        c_SM = sem("c_SM")
        c_P = sem("c_P")
        c_PV = sem("c_PV")
        c_rc = sem("c_rc")
        c_O = sem("c_O")
        c_OT = sem("c_OT")
        c_OTs = sem("c_OTs")
        c_o = sem("c_o")
        c_xb = sem("c_xb")
        c_x3 = sem("c_x3")
        c_sq = sem("c_sq")
        c_ss = sem("c_ss")
        c_ms = sem("c_ms")
        c_r3 = sem("c_r3")
        c_y = sem("c_y")
        c_out = sem("c_out")

        block = ctx.enter_context(nc.Block())

        @block.sync
        def _(sp):
            sp.dma_start(condT[:, :], cond_t).then_inc(d_cond, 16)
            sp.dma_start(condR[:, :], cond_r).then_inc(d_cond, 16)
            sp.dma_start(wc_sb[:, :], wc).then_inc(d_cond, 16)
            sp.dma_start(rows_sb[:, :], rows.to_broadcast([NB, ROW_N])).then_inc(d_cond, 16)
            sp.dma_start(cst_sb[:, :], cst_d).then_inc(d_bc, 16)
            sp.dma_start(w0_sb[:, :], w0).then_inc(d_w0, 16)
            sp.dma_start(bqk_raw[:, :], bias_qk0).then_inc(d_w0, 16)
            x_tok = x.rearrange("b t d -> t b d")
            for n in range(4):
                sp.dma_start(X[:, 4 * n:4 * n + 4, :], x_tok[:, 4 * n:4 * n + 4, :]).then_inc(d_x[n], 16)
            sp.dma_start(bc_sb[:, :], bc.to_broadcast([P, BC_N])).then_inc(d_bc, 16)
            sp.dma_start(cols_sb[:, :], cols).then_inc(d_bc, 16)
            sp.wait_ge(s_bq, 5)
            for n in range(3):
                sp.dma_start(bqk[NC0 * n:NC0 * (n + 1), :], bqk_part[:, n, :]).then_inc(d_bqk, 16)
            sp.wait_ge(s_R0, 3)
            sp.dma_start(scr0, R0[:, :]).then_inc(d_scr0, 16)
            sp.wait_ge(d_scr0, 16)
            sp.dma_start(AB0[:, :, :], scr0.rearrange("(o b) d -> o b d", o=1).to_broadcast([P, NB, 2 * D]))\
                .then_inc(d_ab0, 16)
            sp.dma_start(w1_sb[:, :], w1).then_inc(d_w1, 16)
            for n in range(NB // GM):
                sp.dma_start(adj0[:, GM * n:GM * (n + 1), :],
                             adj[GM * n:GM * (n + 1), :, 0:NG, :].rearrange("b n m l -> n b (m l)")).then_inc(d_adj, 16)
                for b in range(GM):
                    sp.dma_start(adj1[NG * b:NG * (b + 1), GM * n:GM * (n + 1), :].rearrange("p a c -> p (a c)"),
                                 adj[GM * n + b, 0:NG, :, :].rearrange("m n l -> m (n l)")).then_inc(d_adj, 16)
            sp.wait_ge(s_qpr, 1)
            sp.dma_start(scr1, qp_r[:, :]).then_inc(d_scr1, 16)
            sp.wait_ge(d_scr1, 16)
            sp.dma_start(QP1[:, :, :], scr1.rearrange("(o b) d -> o b d", o=1).to_broadcast([P, NB, D]))\
                .then_inc(d_qp, 16)
            sp.wait_ge(s_R3, 2)
            sp.dma_start(scr3, R3[:, :]).then_inc(d_scr3, 16)
            sp.wait_ge(d_scr3, 16)
            n2 = 3 * H2 * HD2
            sp.dma_start(w2raw[:, :], w2[:, 0:n2]).then_inc(d_w2, 16)
            sp.dma_start(w_ff[:, :], w2[:, n2:n2 + 2 * FF]).then_inc(d_wo, 16)
            sp.dma_start(w_at[:, :, :], attn_w.rearrange("(c p) n -> p c n", p=P)).then_inc(d_wo, 16)
            sp.dma_start(w_fo[:, :, :], ff_w.rearrange("(c p) n -> p c n", p=P)).then_inc(d_wo, 16)
            sp.wait_ge(b_x2, NB)
            sp.dma_start(AB3[:, :, :], scr3.rearrange("(o b) d -> o b d", o=1).to_broadcast([P, NB, 2 * D]))\
                .then_inc(d_ab3, 16)
            sp.dma_start(maskN[:, :, :], mask.rearrange("b q k -> q b k")).then_inc(d_mask, 16)
            sp.dma_start(maskT[:, :, :], mask_t.rearrange("b k q -> k b q")).then_inc(d_mask, 16)
            sp.wait_ge(c_out, 1)
            with sp.Fori(0, NB) as b:
                sp.wait_ge(c_out, b + 1)
                sp.dma_start(out[bass.ds(b, 1), :, :].rearrange("b t d -> t b d"), X[:, bass.ds(b, 1), :])\
                    .then_inc(d_out, 16)
            sp.wait_ge(d_out, 16 * NB)

        @block.tensor
        def _(pe):
            pe.wait_ge(d_cond, 64)
            pe.matmul(bank[7][0:NB, 0:2 * D], condT[:, :], wcc("gb"), start=True, stop=True).then_inc(s_gb0, 1)
            pe.matmul(bank[5][0:NB, 0:D], condT[:, :], wcc("self_q"), start=True, stop=True).then_inc(s_qp, 1)
            pe.wait_ge(s_act, 1)
            pe.matmul(bank[4][0:NB, 0:2 * D], siluT[:, :], wcc("sb"), start=True, stop=True).then_inc(s_p, 1)
            pe.wait_ge(s_R0, 3)
            pe.wait_ge(d_bc, 48)
            for n in range(2):
                last = pe.transpose(bank[6][:, n * NB:(n + 1) * NB], R0[:, n * D:(n + 1) * D], ident[0:NB, 0:NB])
            last.then_inc(s_R0T, 1)
            pe.wait_ge(s_one, 1)
            pe.wait_ge(s_q, 1)
            pe.matmul(bank[3][:, 0:1], onesP[:, :], wq_s[:, 0:1], start=True, stop=True).then_inc(s_p, 1)
            pe.wait_ge(s_q, 16)
            pe.transpose(bank[5][:, 0:NB], cq[:, :], ident[0:NB, 0:NB]).then_inc(s_p, 1)
            pe.wait_ge(s_R2, 3)
            for n in range(2):
                last = pe.transpose(bank[2][:, n * NB:(n + 1) * NB], R2[:, n * D:(n + 1) * D], ident[0:NB, 0:NB])
            last.then_inc(s_R2T, 1)
            pe.wait_ge(s_cqT, 1)
            pe.matmul(bank[3][0:NB, 0:2 * D], cqT[:, :], wq[:, :], start=True, stop=True).then_inc(s_p, 1)
            pe.wait_ge(s_cqT, 2)
            pe.wait_ge(s_R3, 2)
            pe.wait_ge(d_w0, 32)
            pe.wait_ge(d_bqk, 48)
            pe.wait_ge(s_const, 7)
            pe.wait_ge(s_idr, 1)
            pe.wait_ge(s_AB0T, 1)

            def l0_slot(t, u):
                f, a = t, t - 1
                front, att = live(f), live(a)
                v = 1 - u

                def scores(r):
                    rows_r = slice(32 * r, 32 * r + 32)
                    need(pe, a_pack, 2 * f + 2)
                    need(pe, a_max, NC0 * f + r)
                    for c in range(NC0):
                        last = pe.matmul(bank[3][:, c * S:(c + 1) * S], pack[rows_r, u, 0, c, :],
                                         pack[rows_r, u, 1, c, :], start=True, stop=True)
                    last.then_inc(a_S, 1)

                def scores_t(r):
                    rows_r = slice(32 * r, 32 * r + 32)
                    need(pe, a_P, NC0 * a + r - 1)
                    if r == 0:
                        need(pe, a_mTs, a + 1)
                    for c in range(NC0):
                        dst = bank[4 + r % 2][:, c * S:(c + 1) * S]
                        pe.matmul(dst, pack[rows_r, v, 1, c, :], pack[rows_r, v, 0, c, :], start=True, stop=False)
                        last = pe.matmul(dst, sel0[32 * r:32 * r + 8, c, :], mT0[32 * r:32 * r + 8, :],
                                         start=False, stop=True)
                    last.then_inc(a_ST, 1)

                def values(r):
                    need(pe, a_P, NC0 * a + r + 1)
                    if r == 0:
                        need(pe, a_V, a + 1)
                        need(pe, a_at, a)
                    for c in range(NC0):
                        h = G * c + r
                        last = pe.matmul(bank[6][:, h * (HD0 + 1):(h + 1) * (HD0 + 1)],
                                         P0[:, r % 2, c * S:(c + 1) * S], V0[:, v, h, :], start=True, stop=True)
                    last.then_inc(a_PV, 1)

                if att:
                    scores_t(0)
                if front:
                    need(pe, a_xn, f + 1)
                    need(pe, a_h1, f - 1)
                    pe.transpose(bank[0][:, 0:S], xn[:, :], ident).then_inc(a_xnT, 1)
                if att:
                    scores_t(1)
                if front:
                    need(pe, a_u, f + 1)
                    for n, name in enumerate(("q", "k")):
                        need(pe, a_pack, 2 * f - 1 + n)
                        pe.matmul(bank[1 + n][:, :], bqk[:, n * P:(n + 1) * P],
                                  sel12[:, :, :].rearrange("p c s -> p (c s)"), start=True, stop=False)
                        for c in range(NC0):
                            last = pe.matmul(bank[1 + n][:, c * S:(c + 1) * S], w0c(name)[:, c * P:(c + 1) * P],
                                             ut[:, :], start=False, stop=(c == NC0 - 1))
                        last.then_inc(a_qk, 1)
                        if att and n == 0:
                            values(0)
                            scores_t(2)
                    need(pe, a_mTs, f)
                    pe.matmul(bank[7][:, 0:D], ut[:, :], w0c("v"), start=True, stop=True).then_inc(a_v, 1)
                elif att:
                    values(0)
                    scores_t(2)
                if att:
                    values(1)
                    scores_t(3)
                if front:
                    scores(0)
                if att:
                    values(2)
                if front:
                    scores(1)
                if att:
                    values(3)
                if front:
                    scores(2)
                    scores(3)
                if att:
                    need(pe, a_at, a + 1)
                    need(pe, a_u, f if not isinstance(f, int) else min(f + 1, NB))
                    pe.transpose(bank[0][:, 128:256], at0[:, :], ident).then_inc(a_atT, 1)
                if front:
                    need(pe, a_nm, 2 * f + 2)
                    need(pe, a_V, f + 1)
                    pe.matmul(bank[7][:, 128:256], nm0[:, :], identB[:, :], start=True, stop=True)\
                        .then_inc(a_mT, 1)
                if att:
                    need(pe, a_atS, a + 1)
                    pe.matmul(bank[0][:, 256:384], at0T[:, :], w1_sb[:, W1_COLS["wp0"][0]:W1_COLS["wp0"][1]],
                              start=True, stop=True).then_inc(a_o, 1)

            pe.wait_ge(d_w1, 16)
            slots(pe, l0_slot, 4, NB, NB + 1)
            pe.wait_ge(g_bc, 4)
            for n in range(NB // GM):
                last = pe.transpose(bank[1][:, n * GM * NG:(n + 1) * GM * NG],
                                    vb1[:, GM * n:GM * (n + 1), :].rearrange("p a c -> p (a c)"),
                                    ident[0:GM * NG, 0:GM * NG])
            last.then_inc(g_bcT, 1)
            pe.wait_ge(g_bc, 5)
            pe.wait_ge(a_h1, NB)

            def l1_slot(t, u):
                f, a = t, t - 1
                front, att = live(f), live(a)
                v = 1 - u
                if att:
                    for d in range(2):
                        need(pe, b_qs, 2 * a + 2)
                        need(pe, b_kbd, 2 * a + 2)
                        need(pe, b_aff, 2 * a - 1 + d)
                        pe.matmul(bank[3 + d][:, 0:H0 * NG], qT1[:, v, d, :], kbd[:, v, d, :], start=True,
                                  stop=True).then_inc(b_S, 1)
                if front:
                    need(pe, b_xs, f + 1)
                    need(pe, b_sTs, 2 * f)
                    pe.transpose(bank[0][:, 0:S], xs[:, :], ident).then_inc(b_xT, 1)
                    need(pe, b_xTs, f + 1)
                    pe.matmul(bank[0][:, 128:256], xT1[:, :], w1c("self"), start=True, stop=True).then_inc(b_sf, 1)
                if att:
                    weighted(0, a, v)
                if front:
                    need(pe, b_self, f + 1)
                    pe.transpose(bank[0][:, 256:384], selfTok[:, u, :], ident).then_inc(b_sT, 1)
                    need(pe, b_sTs, 2 * f + 2)
                    need(pe, b_VW, f)
                    for d in range(2):
                        pe.matmul(bank[2][:, 288 + NG * d:288 + NG * (d + 1)], w1c("k")[:, d * D:(d + 1) * D],
                                  selfT[:, 0:NG], start=True, stop=True)
                    pe.matmul(bank[2][0:HC * NG, 0:288], selfR[:, :, :].rearrange("p r m -> p (r m)"), w1c("out"),
                              start=True, stop=True).then_inc(b_kv, 1)
                    need(pe, b_qs, 2 * f)
                    for d in range(2):
                        last = pe.matmul(bank[1][:, d * S:(d + 1) * S], w1c("q")[:, d * D:(d + 1) * D],
                                         selfT[:, :], start=True, stop=True)
                    last.then_inc(b_q, 1)
                if att:
                    weighted(1, a, v)

            def weighted(d, a, v):
                need(pe, b_ex, 2 * a + 1 + d)
                need(pe, b_eTs, 2 * a - 1 + d)
                for c in range(NC1):
                    last = pe.transpose(bank[5 + d][0:HC * NG, c * S:(c + 1) * S],
                                        ex1[:, d, c * HC * NG:(c + 1) * HC * NG], ident)
                last.then_inc(b_eT, 1)
                need(pe, b_eTs, 2 * a + 1 + d)
                if d == 0:
                    need(pe, b_VW, a + 1)
                    need(pe, b_on, 2 * a)
                else:
                    need(pe, b_on, 2 * a + 1)
                for c in range(NC1):
                    w = HC * (HD0 + 1)
                    last = pe.matmul(bank[7][:, (NC1 * d + c) * w:(NC1 * d + c + 1) * w],
                                     exT[:, d, c * S:(c + 1) * S],
                                     VW[:, v, d, c * HC:(c + 1) * HC, :].rearrange("p h d -> p (h d)"),
                                     start=True, stop=True)
                last.then_inc(b_PV, 1)

            slots(pe, l1_slot, 2, NB, NB + 1)
            pe.wait_ge(b_x2, NB)
            pe.wait_ge(e_l, NB)
            pe.wait_ge(d_wo, 48)
            pe.wait_ge(c_const, 5)

            def l2_slot(t, u):
                g, f, a = t, t - 1, t - 2
                lead, front, att = live(g), live(f), live(a)
                v = 1 - u

                def project(j):
                    n = 8 * f + j
                    if j == 0:
                        need(pe, c_ul, f + 1)
                    if j == 0:
                        need(pe, c_gel, f)
                    elif j == 1:
                        need(pe, c_ff, f)
                    elif j <= 5:
                        need(pe, c_cp, 4 * f + j - 1)
                    else:
                        need(pe, c_V, 2 * f + j - 5)
                    dst = bank[1 + j % 2]
                    if j < 6:
                        c0 = (0, 1024, 512, 1536, 2048, 2560)[j]
                        cs = slice(c0, c0 + 512)
                        pe.matmul(dst[:, :], uTh[:, v, :], w2h[:, cs], start=True, stop=False)
                        pe.matmul(dst[:, :], uTh[:, v, :], w2l[:, cs], start=False, stop=False)
                        last = pe.matmul(dst[:, :], uTl[:, v, :], w2h[:, cs], start=False, stop=True)
                    else:
                        c0 = FF if j == 6 else 0
                        for c in range(FF // P):
                            last = pe.matmul(dst[:, c * S:(c + 1) * S], w_ff[:, c0 + c * P:c0 + (c + 1) * P],
                                             uT2[:, v, :], start=True, stop=True)
                    last.then_inc(c_pj, 1)

                def turn(j):
                    need(pe, c_rot, 4 * f + j + 1)
                    if j == 0:
                        need(pe, c_OTs, 2 * (f - 1))
                    else:
                        need(pe, c_Ts, 4 * f + j)
                    for c in range(4):
                        last = pe.transpose(bank[3][:, c * S:(c + 1) * S], qkt[:, j % 2, c * P:(c + 1) * P], ident)
                    last.then_inc(c_T, 1)

                def rough(r):
                    h0, c0 = 64 * (r % 2), 4 * (r // 2)
                    need(pe, c_B, 4 * f + 2 * (r // 2) + 2)
                    need(pe, c_jk, 16 * f + 4 * r)
                    for c in range(4):
                        last = pe.matmul(bank[7][:, c * S:(c + 1) * S], qkB[h0:h0 + 64, 0, c0 + c, :],
                                         qkB[h0:h0 + 64, 1, c0 + c, :], start=True, stop=True)
                    last.then_inc(c_G, 1)

                def scores_t(r):
                    h0, c0 = 64 * (r % 2), 4 * (r // 2)
                    need(pe, c_SM, 4 * a + r - 1)
                    if r == 0:
                        need(pe, c_mTs, a + 1)
                    for c in range(4):
                        dst = bank[4 + r % 2][:, c * S:(c + 1) * S]
                        pe.matmul(dst, qkT[h0:h0 + 64, u, 1, c0 + c, :], qkT[h0:h0 + 64, u, 0, c0 + c, :],
                                  start=True, stop=False)
                        last = pe.matmul(dst, sel2[h0:h0 + 24, c0 + c, :], mT2[h0:h0 + 24, :],
                                         start=False, stop=True)
                    last.then_inc(c_ST, 1)

                def values(r):
                    half, c0 = r % 2, 4 * (r // 2)
                    need(pe, c_P, 4 * a + r + 1)
                    need(pe, c_O, 4 * a + r)
                    if r == 0:
                        need(pe, c_V, 2 * a + 2)
                        need(pe, c_x3, a)
                    for c in range(4):
                        last = pe.matmul(bank[6][:, c * (HD2 + 1):(c + 1) * (HD2 + 1)],
                                         P2[:, r % 2, c * S:(c + 1) * S], V2[:, u, 2 * (c0 + c) + half, :],
                                         start=True, stop=True)
                    last.then_inc(c_PV, 1)

                if att:
                    scores_t(0)
                if front:
                    project(0)
                    project(1)
                if att:
                    scores_t(1)
                    values(0)
                if front:
                    project(2)
                    turn(0)
                if att:
                    scores_t(2)
                    values(1)
                if front:
                    project(3)
                    turn(1)
                if att:
                    scores_t(3)
                    values(2)
                if lead:
                    need(pe, c_xn, g + 1)
                    need(pe, c_mTs, f)
                    pe.transpose(bank[0][:, 0:S], xn2[:, :], ident).then_inc(c_xT, 1)
                if front:
                    project(4)
                    turn(2)
                    rough(0)
                    project(5)
                if att:
                    values(3)
                if front:
                    rough(1)
                    turn(3)
                    project(6)
                    rough(2)
                    project(7)
                    rough(3)
                if att:
                    for n in range(2):
                        need(pe, c_O, 4 * a + 2 * n + 2)
                        if n == 0:
                            need(pe, c_Ts, 4 * min(f + 1, NB) if isinstance(f, int) else 4 * f + 4)
                        else:
                            need(pe, c_OTs, 2 * a + 1)
                        for c in range(4):
                            last = pe.transpose(bank[3][:, c * S:(c + 1) * S],
                                                O2[:, 4 * n + c, :, :].rearrange("p h d -> p (h d)"), ident)
                        last.then_inc(c_OT, 1)
                if front:
                    need(pe, c_nm, 5 * f + 5)
                    need(pe, c_ul, min(g + 1, NB) if isinstance(g, int) else g + 1)
                    pe.matmul(bank[0][:, 128:256], nm2[:, :], identB[:, :], start=True, stop=True)\
                        .then_inc(c_mT, 1)
                if att:
                    need(pe, c_OTs, 2 * a + 2)
                    need(pe, c_ff, a + 1)
                    for c in range(FF // P):
                        pe.matmul(bank[6][:, 384:512], ffT[:, u, c, :], w_fo[:, c, :], start=(c == 0), stop=False)
                    for c in range(HC2):
                        last = pe.matmul(bank[6][:, 384:512], OT2[:, c, :], w_at[:, c, :], start=False,
                                         stop=(c == HC2 - 1))
                    last.then_inc(c_o, 1)

            slots(pe, l2_slot, 4, NB, NB + 2)

        @block.vector
        def _(dve):
            dve.wait_ge(s_gb0, 1)
            dve.wait_ge(d_cond, 64)
            dve.tensor_tensor(gb0[:, :], bank[7][0:NB, 0:2 * D], row("gb0"), ALU.add).then_inc(s_R0, 1)
            dve.wait_ge(s_R0, 1)
            dve.tensor_tensor(R0[:, D:2 * D], gb0[:, 0:D], row("ln_b0"), ALU.mult).then_inc(s_R0, 1)
            dve.tensor_tensor(R0[:, 0:D], gb0[:, 0:D], row("ln_g0"), ALU.mult)
            dve.wait_ge(s_R0, 2)
            dve.tensor_tensor(R0[:, D:2 * D], R0[:, D:2 * D], gb0[:, D:2 * D], ALU.add).then_inc(s_R0, 1)
            dve.wait_ge(s_qp, 1)
            dve.tensor_copy(qp_r[:, :], bank[5][0:NB, 0:D]).then_inc(s_qpr, 1)
            for b in range(NB):
                if b % 4 == 0:
                    dve.wait_ge(d_x[b // 4], 16)
                dve.bn_stats(st_all[:, b, :], X[:, b, :]).then_inc(s_st, 1)
            for b in range(NB):
                dve.wait_ge(s_st, b + 1)
                dve.bn_aggr(mean0[:, b, :], st_all[:, b, :]).then_inc(s_mean0, 1)
            dve.wait_ge(d_w0, 32)
            rest = bqk_raw[:, :]
            for n in range(3):
                dve.tensor_copy(bqk_part[:, n, :], rest).then_inc(s_bq, 1)
                if n < 2:
                    dve.wait_ge(s_bq, 2 * n + 1)
                    dve.tensor_tensor(bqk_rest[:, n, :], rest, bqk_part[:, n, :], ALU.subtract).then_inc(s_bq, 1)
                    dve.wait_ge(s_bq, 2 * n + 2)
                    rest = bqk_rest[:, n, :]
            dve.wait_ge(s_p, 1)
            dve.tensor_tensor(sb2[:, :], bank[4][0:NB, 0:2 * D], row("cond_b"), ALU.add).then_inc(s_R2, 1)
            dve.wait_ge(s_R2, 1)
            dve.scalar_tensor_tensor(out=R2[:, D:2 * D], in0=sb2[:, 0:D], scalar=1.0, in1=row("ln_b2"),
                                     op0=ALU.add, op1=ALU.mult).then_inc(s_R2, 1)
            dve.scalar_tensor_tensor(out=R2[:, 0:D], in0=sb2[:, 0:D], scalar=1.0, in1=row("ln_w2"),
                                     op0=ALU.add, op1=ALU.mult)
            dve.wait_ge(s_R2, 2)
            dve.tensor_tensor(R2[:, D:2 * D], R2[:, D:2 * D], sb2[:, D:2 * D], ALU.add).then_inc(s_R2, 1)
            steps = iter(range(1, 100))

            def step(instruction):
                k = next(steps)
                instruction.then_inc(s_q, 1)
                dve.wait_ge(s_q, k)

            dve.wait_ge(s_act, 3)
            step(dve.tensor_reduce(wq_s[:, 0:1], wabs[:, :], AX, ALU.add))
            step(dve.tensor_reduce(cq_s[:, 0:1], cabs[:, :], AX, ALU.max))
            step(dve.tensor_scalar(cq_s[:, 0:1], cq_s[:, 0:1], EPS, None, ALU.max))
            step(dve.tensor_scalar(cq_s[:, 2:3], cq_s[:, 0:1], 1.0 / 127.0, None, ALU.mult))
            step(dve.reciprocal(cq_s[:, 1:2], cq_s[:, 2:3]))
            step(dve.tensor_scalar(cq[:, :], condR[:, :], cq_s[:, 1:2], None, ALU.mult))
            step(dve.tensor_scalar(cq[:, :], cq[:, :], BIG_ROUND, None, ALU.add))
            step(dve.tensor_scalar(cq[:, :], cq[:, :], BIG_ROUND, 127.0, ALU.subtract, ALU.min))
            step(dve.tensor_scalar(cq[:, :], cq[:, :], -128.0, cq_s[:, 2:3], ALU.max, ALU.mult))
            step(dve.tensor_tensor(cq[:, :], cq[:, :], condR[:, :], ALU.subtract))
            dve.wait_ge(s_p, 2)
            step(dve.tensor_scalar(wq_s[:, 1:2], bank[3][:, 0:1], 1.0 / (2 * D * D), EPS, ALU.mult, ALU.max))
            step(dve.reciprocal(wq_s[:, 2:3], wq_s[:, 1:2]))
            step(dve.tensor_scalar(wq[:, :], wcc("proj"), wq_s[:, 2:3], None, ALU.mult))
            step(dve.tensor_scalar(wq[:, :], wq[:, :], BIG_ROUND, None, ALU.add))
            step(dve.tensor_scalar(wq[:, :], wq[:, :], BIG_ROUND, 1.0, ALU.subtract, ALU.min))
            step(dve.tensor_tensor(cq[:, :], cq[:, :], condR[:, :], ALU.add))
            step(dve.tensor_scalar(wq[:, :], wq[:, :], -1.0, wq_s[:, 1:2], ALU.max, ALU.mult))
            step(dve.tensor_tensor(wq[:, :], wq[:, :], wcc("proj"), ALU.subtract))
            step(dve.tensor_tensor(wq[:, :], wq[:, :], wcc("proj"), ALU.add))
            dve.wait_ge(s_p, 3)
            dve.tensor_copy(cqT[:, :], bank[5][:, 0:NB]).then_inc(s_cqT, 1)
            dve.wait_ge(s_R2T, 1)
            dve.tensor_copy(AB2T[:, :, :], bank[2][:, 0:2 * NB].rearrange("p (n b) -> p n b", n=2)).then_inc(s_cqT, 1)
            dve.wait_ge(s_p, 4)
            dve.tensor_tensor(emb3[:, :], bank[3][0:NB, 0:2 * D], row("b_proj"), ALU.add).then_inc(s_R3, 1)
            dve.wait_ge(s_R3, 1)
            dve.tensor_copy(R3[:, D:2 * D], emb3[:, D:2 * D])
            dve.scalar_tensor_tensor(out=R3[:, 0:D], in0=emb3[:, 0:D], scalar=1.0, in1=row("rms_w"), op0=ALU.add,
                                     op1=ALU.mult).then_inc(s_R3, 1)
            dve.wait_ge(s_mean0, NB)
            dve.wait_ge(s_rstd0, 1)

            def l0_slot(t, u):
                f, a, e = t, t - 1, t - 2
                v = 1 - u

                def maxima(r):
                    need(dve, a_S, NC0 * f + r + 1)
                    need(dve, a_nm, 2 * f)
                    dve.tensor_reduce(m0[:, r, :], bank[3][:, :].rearrange("p (c k) -> p c k", c=NC0),
                                      AX, ALU.max).then_inc(a_max, 1)

                if live(f):
                    need(dve, a_xnT, f)
                    dve.tensor_scalar(xn[:, :], X[:, f, :], mean0[:, f, 0:1], rstd0[:, one(f)],
                                      ALU.subtract, ALU.mult).then_inc(a_xn, 1)
                if live(e):
                    need(dve, a_rs, e + 1)
                    need(dve, a_hb, e + 1)
                    need(dve, a_x1, e)
                    dve.scalar_tensor_tensor(out=tn0[:, :], in0=h1[:, u, :], scalar=mv0[:, u, 0:1],
                                             in1=AB0[:, e, 0:D], op0=ALU.subtract, op1=ALU.mult).then_inc(a_tn, 1)
                if live(e):
                    need(dve, a_tn, e + 1)
                    dve.scalar_tensor_tensor(out=X[:, e, :], in0=tn0[:, :], scalar=rs0[:, u, :],
                                             in1=hb0[:, u, :], op0=ALU.mult, op1=ALU.add).then_inc(a_x1, 1)
                if live(f):
                    need(dve, a_ST, NC0 * (f - 1))
                    for n in range(2):
                        need(dve, a_rnd, 2 * f + 1 + n)
                        dve.tensor_tensor(pack[:, u, n, :, :].rearrange("p c s -> p (c s)"), bank[1 + n][:, :],
                                          rnd[:, n, :], ALU.subtract).then_inc(a_pack, 1)
                    need(dve, a_v, f + 1)
                    need(dve, a_PV, NC0 * (f - 1))
                    dve.tensor_tensor(V0[:, u, :, 0:HD0], bank[7][:, 0:D].rearrange("p (h d) -> p h d", h=H0),
                                      bcv("bv0").rearrange("p (h d) -> p h d", h=H0), ALU.add).then_inc(a_V, 1)
                    maxima(0)
                    maxima(1)
                if live(a):
                    need(dve, a_PV, NC0 * a + NC0)
                    O = bank[6][:, 0:H0 * (HD0 + 1)].rearrange("p (h d) -> p h d", h=H0)
                    dve.reciprocal(rc0[:, :], O[:, :, HD0]).then_inc(a_rc, 1)
                if live(f):
                    maxima(2)
                if live(a):
                    need(dve, a_rc, a + 1)
                    need(dve, a_atT, a)
                    dve.scalar_tensor_tensor(out=at0[:, :].rearrange("p (h d) -> p h d", h=H0), in0=O[:, :, 0:HD0],
                                             scalar=1.0 / D ** 0.5,
                                             in1=rc0[:, :].unsqueeze(2).to_broadcast([P, H0, HD0]),
                                             op0=ALU.mult, op1=ALU.mult).then_inc(a_at, 1)
                if live(a):
                    for n, (flt, lab, cnt, vb) in enumerate(((labF0, lab0, cnt0, vb0), (labF1, lab1, cnt1, vb1))):
                        need(dve, g_flt, 2 * a + 1 + n)
                        dve.tensor_reduce(cnt[:, a, :], flt[:, :].rearrange("p (m l) -> p m l", l=NL),
                                          AX, ALU.add).then_inc(g_cnt, 1)
                        need(dve, g_lab, 2 * a + 1 + n)
                        dve.tensor_reduce(vb[:, a, :], lab[:, :].rearrange("p (m l) -> p m l", l=NL),
                                          AX, ALU.add).then_inc(g_vb, 1)
                if live(f):
                    maxima(3)
                    need(dve, a_max, NC0 * f + NC0)
                    need(dve, a_mT, f)
                    cols0 = nm0[:, :].rearrange("p (r c) -> p r c", r=G)
                    dve.tensor_scalar(cols0[:, :, 0:NC0], m0[:, :, :], -1.0, None, ALU.mult).then_inc(a_nm, 1)
                    need(dve, a_nm, 2 * f + 1)
                    dve.scalar_tensor_tensor(out=cols0[:, :, NC0:2 * NC0], in0=m0[:, :, :], scalar=-1.0,
                                             in1=cols0[:, :, 0:NC0], op0=ALU.mult, op1=ALU.subtract)\
                        .then_inc(a_nm, 1)
                if live(a):
                    need(dve, a_o, a + 1)
                    need(dve, a_xb, a + 1)
                    need(dve, a_x1, a - 1)
                    need(dve, a_hb, a - 1)
                    dve.tensor_tensor(h1[:, v, :], bank[0][:, 256:384], xb0[:, :], ALU.add).then_inc(a_h1, 1)
                    need(dve, a_h1, a + 1)
                    dve.bn_stats(st0[:, :], h1[:, v, :]).then_inc(a_bn, 1)
                    need(dve, a_bn, 2 * a + 1)
                    need(dve, a_rs, a - 1)
                    dve.memset(carrier[:, :], 0.0)
                    dve.bn_aggr(mv0[:, v, :], st0[:, :]).then_inc(a_bn, 1)

            dve.wait_ge(d_ab0, 16)
            dve.wait_ge(s_const, 7)
            slots(dve, l0_slot, 4, NB, NB + 2)
            dve.wait_ge(g_cnt, 2 * NB)
            dve.wait_ge(g_vb, 2 * NB)
            for cnt, vb in ((cnt0, vb0), (cnt1, vb1)):
                dve.tensor_scalar(cnt[:, :, :], cnt[:, :, :], 0.0, NEG, ALU.is_le, ALU.mult).then_inc(g_bc, 1)
            dve.wait_ge(g_bc, 2)
            bias1 = bcv("b_bias")
            dve.scalar_tensor_tensor(out=Bc[:, :, 0, :], in0=vb0[:, :, :], scalar=bias1, in1=cnt0[:, :, :],
                                     op0=ALU.add, op1=ALU.add).then_inc(g_bc, 1)
            dve.scalar_tensor_tensor(out=vb1[:, :, :], in0=vb1[:, :, :], scalar=bias1[0:GM * NG, :],
                                     in1=cnt1[:, :, :], op0=ALU.add, op1=ALU.add).then_inc(g_bc, 1)
            dve.wait_ge(g_bcT, 1)
            dve.tensor_copy(Bc[:, :, 1, :], bank[1][:, 0:NB * NG].rearrange("p (b m) -> p b m", m=NG))\
                .then_inc(g_bc, 1)
            dve.tensor_tensor(bout1[:, :], bcv("bout")[:, 0:D], bcv("bout")[:, D:2 * D], ALU.add).then_inc(g_bc, 1)
            dve.wait_ge(g_bc, 6)
            dve.wait_ge(a_x1, NB)
            dve.wait_ge(d_qp, 16)
            dve.wait_ge(g_pad, 3)

            def l1_slot(t, u):
                f, a = t, t - 1
                front, att = live(f), live(a)
                v = 1 - u

                def affinity(d):
                    need(dve, b_S, 2 * a + 1 + d)
                    need(dve, b_sub, 2 * a - 1 + d)
                    dve.scalar_tensor_tensor(
                        out=aff[:, d, :].rearrange("p (h m) -> p h m", m=NG),
                        in0=bank[3 + d][:, 0:H0 * NG].rearrange("p (h m) -> p h m", m=NG), scalar=1.0 / HD0 ** 0.5,
                        in1=Bc[:, a, d, :].unsqueeze(1).to_broadcast([P, H0, NG]), op0=ALU.mult, op1=ALU.add)\
                        .then_inc(b_aff, 1)
                    need(dve, b_aff, 2 * a + 1 + d)
                    dve.tensor_reduce(mx1[:, d, :], aff[:, d, :].rearrange("p (h m) -> p h m", m=NG), AX,
                                      ALU.max).then_inc(b_mx, 1)

                def normalised(d):
                    O = bank[7][:, NC1 * d * HC * (HD0 + 1):(NC1 * d * HC + H0) * (HD0 + 1)]\
                        .rearrange("p (h d) -> p h d", h=H0)
                    need(dve, b_PV, 2 * a + 1 + d)
                    dve.reciprocal(rc1[:, d, :], O[:, :, HD0]).then_inc(b_rc, 1)
                    need(dve, b_rc, 2 * a + 1 + d)
                    need(dve, b_sum, 3 * a)
                    dve.tensor_tensor(on1[:, d, :].rearrange("p (h d) -> p h d", h=H0), O[:, :, 0:HD0],
                                      rc1[:, d, :].unsqueeze(2).to_broadcast([P, H0, HD0]), ALU.mult)\
                        .then_inc(b_on, 1)

                if front:
                    need(dve, b_xT, f)
                    dve.tensor_copy(xs[:, :], X[:, f, :]).then_inc(b_xs, 1)
                if att:
                    affinity(0)
                if front:
                    need(dve, b_xs, f + 1)
                    dve.tensor_reduce(rsum[:, :], xs[:, :], AX, ALU.add).then_inc(b_rs, 1)
                    need(dve, b_rs, f + 1)
                    dve.tensor_scalar(nz[:, :], rsum[:, :], 0.0, None, ALU.not_equal).then_inc(b_nz, 1)
                    need(dve, b_nz, f + 1)
                    need(dve, b_self, f)
                    dve.scalar_tensor_tensor(out=cpart[:, :], in0=QP1[:, f, :], scalar=nz[:, :], in1=bcv("b_self"),
                                             op0=ALU.mult, op1=ALU.add).then_inc(b_cp, 1)
                    need(dve, b_sf, f + 1)
                    need(dve, b_cp, f + 1)
                    need(dve, b_sum, 3 * (f - 1))
                    dve.tensor_tensor(selfTok[:, u, :], cpart[:, :], bank[0][:, 128:256], ALU.add)\
                        .then_inc(b_self, 1)
                if att:
                    affinity(1)
                if front:
                    need(dve, b_kv, f + 1)
                    need(dve, b_S, 2 * (f - 1))
                    for d in range(2):
                        c0 = COL_COLS["bk1"][0] + d
                        dve.scalar_tensor_tensor(
                            out=kbd[:, u, d, :].rearrange("p (h m) -> p h m", m=NG),
                            in0=bank[2][:, 288 + NG * d:288 + NG * (d + 1)].unsqueeze(1)
                            .to_broadcast([P, H0, NG]), scalar=cols_sb[:, c0:c0 + 1],
                            in1=cst("bd_k").rearrange("p (h m) -> p h m", m=NG), op0=ALU.add, op1=ALU.mult)\
                            .then_inc(b_kbd, 1)
                    need(dve, b_PV, 2 * (f - 1))
                    dve.tensor_tensor(VW[:, u, :, :, 0:HD0],
                                      bank[2][0:HC * NG, 0:288].rearrange("p (e h d) -> p e h d", e=2, d=HD0),
                                      cst("bd_v")[0:HC * NG, :].rearrange("p (h d) -> p h d", d=HD0).unsqueeze(1)
                                      .to_broadcast([HC * NG, 2, H1P, HD0]), ALU.mult).then_inc(b_VW, 1)
                if att:
                    normalised(0)
                    dve.tensor_tensor(sum1[:, 0, :], selfTok[:, v, :], bout1[:, :], ALU.add).then_inc(b_sum, 1)
                    normalised(1)
                    need(dve, b_on, 2 * a + 2)
                    need(dve, b_sum, 3 * a + 1)
                    dve.tensor_tensor(sum1[:, 1, :], sum1[:, 0, :], on1[:, 0, :], ALU.add).then_inc(b_sum, 1)
                    need(dve, b_sum, 3 * a + 2)
                    dve.tensor_tensor(sum1[:, 2, :], sum1[:, 1, :], on1[:, 1, :], ALU.add).then_inc(b_sum, 1)
                    need(dve, b_sum, 3 * a + 3)
                    dve.scalar_tensor_tensor(out=X[:, a, :], in0=sum1[:, 2, :], scalar=0.0, in1=X[:, a, :],
                                             op0=ALU.max, op1=ALU.add).then_inc(b_x2, 1)

            slots(dve, l1_slot, 2, NB, NB + 1)
            dve.wait_ge(b_x2, NB)
            dve.wait_ge(e_l, NB)
            dve.memset(nm2[:, :], 0.0).then_inc(c_const, 1)
            dve.tensor_tensor(bsum2[:, :], bcv("attn_b"), bcv("ff_b"), ALU.add).then_inc(c_const, 1)
            dve.wait_ge(c_const, 5)
            dve.wait_ge(d_mask, 32)
            dve.wait_ge(d_ab3, 16)
            inv_s = 1.41421 / 2.0 ** 0.5

            def l2_slot(t, u):
                g, f, a, e = t, t - 1, t - 2, t - 3
                lead, front, att, tail = live(g), live(f), live(a), live(e)
                v = 1 - u

                def masked(r):
                    need(dve, c_ST, 4 * a + r + 1)
                    need(dve, c_PV, 4 * a + r - 1)
                    dve.tensor_tensor(P2[:, r % 2, :].rearrange("p (h q) -> p h q", h=G),
                                      bank[4 + r % 2][:, :].rearrange("p (h q) -> p h q", h=G),
                                      maskT[:, one(a), :].to_broadcast([P, G, S]), ALU.add).then_inc(c_SM, 1)

                def normalised(r):
                    half, c0 = r % 2, 4 * (r // 2)
                    O = bank[6][:, 0:G * (HD2 + 1)].rearrange("p (h d) -> p h d", h=G)
                    need(dve, c_PV, 4 * a + r + 1)
                    dve.reciprocal(rc2[:, r % 2, :], O[:, :, HD2]).then_inc(c_rc, 1)
                    need(dve, c_rc, 4 * a + r + 1)
                    need(dve, c_OT, 2 * a)
                    dve.tensor_tensor(O2[:, c0:c0 + G, half, :], O[:, :, 0:HD2],
                                      rc2[:, r % 2, :].unsqueeze(2).to_broadcast([P, G, HD2]), ALU.mult)\
                        .then_inc(c_O, 1)

                def rotate(j):
                    src = qkt[:, j % 2, :].rearrange("p (h d) -> p h d", d=HD2)
                    need(dve, c_cp, 4 * f + j + 1)
                    need(dve, c_rot, 4 * f + j)
                    dve.tensor_tensor(rcos[:, :, :], src[:, :, 0:ROT],
                                      cst("cos").unsqueeze(1).to_broadcast([P, 8, ROT]), ALU.mult)\
                        .then_inc(c_rope, 1)
                    for n in range(2):
                        x0, x1 = (1 - n) * ROT // 2, n * ROT // 2
                        last = dve.tensor_tensor(rsin[:, :, x1:x1 + ROT // 2], src[:, :, x0:x0 + ROT // 2],
                                                 cst("sin")[:, x1:x1 + ROT // 2].unsqueeze(1)
                                                 .to_broadcast([P, 8, ROT // 2]), ALU.mult)
                    last.then_inc(c_rope, 1)

                def rounded(j):
                    need(dve, c_Ts, 4 * f + j + 1)
                    need(dve, c_G, 4 * f)
                    dve.tensor_copy(qkB[:, j % 2, 4 * (j // 2):4 * (j // 2) + 4, :],
                                    qkT[:, v, j % 2, 4 * (j // 2):4 * (j // 2) + 4, :]).then_inc(c_B, 1)

                def maxima(r):
                    half, c0 = r % 2, 4 * (r // 2)
                    need(dve, c_G, 4 * f + r + 1)
                    for c in range(4):
                        n = 16 * f + 4 * r + c
                        need(dve, c_jk, n)
                        if r == 0 and c == 0:
                            need(dve, c_mk, f + 1)
                            need(dve, c_nm, 5 * f)
                        dve.memset(carrier[:, :], 0.0)
                        dve.tensor_tensor_reduce(junk[:, :], bank[7][:, c * S:(c + 1) * S], mask_b[:, :],
                                                 1.0, -3e38, ALU.add, ALU.max, m2[:, half, c0 + c:c0 + c + 1])\
                            .then_inc(c_jk, 1)

                if tail:
                    need(dve, c_r3, e + 1)
                    dve.scalar_tensor_tensor(out=y3[:, :], in0=x3[:, :], scalar=rs3[:, :], in1=AB3[:, e, 0:D],
                                             op0=ALU.mult, op1=ALU.mult).then_inc(c_y, 1)
                    need(dve, c_y, e + 1)
                    dve.tensor_tensor(X[:, e, :], y3[:, :], AB3[:, e, D:2 * D], ALU.add).then_inc(c_out, 1)
                if att:
                    masked(0)
                if front:
                    rotate(0)
                    rotate(1)
                if att:
                    masked(1)
                    normalised(0)
                if front:
                    rotate(2)
                    rounded(0)
                if att:
                    masked(2)
                    normalised(1)
                if front:
                    rotate(3)
                    rounded(1)
                if lead:
                    dve.bn_stats(st2[:, :], X[:, g, :]).then_inc(c_bn, 1)
                    need(dve, c_bn, 2 * g + 1)
                    need(dve, c_ve, g)
                    need(dve, c_xn, g)
                    dve.memset(carrier[:, :], 0.0)
                    dve.bn_aggr(mv2[:, :], st2[:, :]).then_inc(c_bn, 1)
                if att:
                    masked(3)
                    normalised(2)
                if lead:
                    need(dve, c_bn, 2 * g + 2)
                    need(dve, c_rs, g + 1)
                    need(dve, c_xT, g)
                    dve.tensor_scalar(xn2[:, :], X[:, g, :], mv2[:, 0:1], rs2[:, :], ALU.subtract, ALU.mult)\
                        .then_inc(c_xn, 1)
                if front:
                    need(dve, c_jk, 16 * f)
                    dve.tensor_copy(mask_b[:, :], maskN[:, f, :]).then_inc(c_mk, 1)
                    rounded(2)
                    maxima(0)
                if att:
                    normalised(3)
                if front:
                    maxima(1)
                    rounded(3)
                if lead:
                    need(dve, c_u, 2 * g + 2)
                    need(dve, c_pj, 8 * (g - 1))
                    dve.tensor_tensor(uTl[:, u, :], uT2[:, u, :], uTh[:, u, :], ALU.subtract).then_inc(c_ul, 1)
                if front:
                    maxima(2)
                    need(dve, c_gel, f + 1)
                    need(dve, c_pj, 8 * f + 8)
                    need(dve, c_o, f - 1)
                    dve.scalar_tensor_tensor(out=ffT[:, v, :, :].rearrange("p c s -> p (c s)"), in0=bank[2][:, :],
                                             scalar=inv_s, in1=gel[:, :, :].rearrange("p c s -> p (c s)"),
                                             op0=ALU.mult, op1=ALU.mult).then_inc(c_ff, 1)
                    maxima(3)
                    parts = nm2[:, :].rearrange("p (h n) -> p h n", h=2)
                    need(dve, c_jk, 16 * f + 16)
                    need(dve, c_mT, f)
                    dve.tensor_scalar(parts[:, :, 0:8], m2[:, :, :], -1.0, None, ALU.mult).then_inc(c_nm, 1)
                    need(dve, c_nm, 5 * f + 1)
                    dve.scalar_tensor_tensor(out=mr2[:, 0, :, :], in0=m2[:, :, :], scalar=-1.0,
                                             in1=parts[:, :, 0:8], op0=ALU.mult, op1=ALU.subtract).then_inc(c_nm, 1)
                    need(dve, c_nm, 5 * f + 2)
                    dve.tensor_copy(parts[:, :, 8:16], mr2[:, 0, :, :]).then_inc(c_nm, 1)
                    need(dve, c_nm, 5 * f + 3)
                    dve.tensor_tensor(mr2[:, 1, :, :], mr2[:, 0, :, :], parts[:, :, 8:16], ALU.subtract)\
                        .then_inc(c_nm, 1)
                    need(dve, c_nm, 5 * f + 4)
                    dve.tensor_copy(parts[:, :, 16:24], mr2[:, 1, :, :]).then_inc(c_nm, 1)
                if att:
                    need(dve, c_o, a + 1)
                    need(dve, c_xb, a + 1)
                    need(dve, c_y, a)
                    need(dve, c_sq, a)
                    dve.tensor_tensor(x3[:, :], bank[6][:, 384:512], xb2[:, :], ALU.add).then_inc(c_x3, 1)
                    need(dve, c_sq, a + 1)
                    dve.tensor_reduce(ss3[:, :], sq3[:, :], AX, ALU.add).then_inc(c_ss, 1)
                    need(dve, c_ss, a + 1)
                    dve.tensor_scalar(ms3[:, :], ss3[:, :], 1.0 / D, 1e-6, ALU.mult, ALU.add).then_inc(c_ms, 1)

            slots(dve, l2_slot, 4, NB, NB + 3)

        @block.scalar
        def _(act):
            act.wait_ge(d_cond, 64)
            act.activation(siluT[:, :], condT[:, :], ACT.Silu).then_inc(s_act, 1)
            act.activation(cabs[:, :], condR[:, :], ACT.Abs).then_inc(s_act, 1)
            act.activation(wabs[:, :], wcc("proj"), ACT.Abs).then_inc(s_act, 1)
            act.wait_ge(d_bc, 48)
            act.activation(identB[:, :], ident, ACT.Copy).then_inc(s_idr, 1)
            act.wait_ge(s_R0T, 1)
            act.activation(AB0T[:, :, :], bank[6][:, 0:2 * NB].rearrange("p (n b) -> p n b", n=2), ACT.Copy)\
                .then_inc(s_AB0T, 1)
            act.wait_ge(s_AB0T, 1)

            def l0_slot(t, u):
                f, a = t, t - 1

                def exps(j):
                    need(act, a_ST, NC0 * a + j + 1)
                    need(act, a_PV, NC0 * a + j - 1)
                    act.activation(P0[:, j % 2, :], bank[4 + j % 2][:, :], ACT.Exp).then_inc(a_P, 1)

                def rounded(n):
                    need(act, a_qk, 2 * f + 1 + n)
                    need(act, a_pack, 2 * f - 1 + n)
                    c0 = COL_COLS[("part_q", "part_k")[n]][0]
                    act.activation(rnd[:, n, :], bank[1 + n][:, :], ACT.Copy, scale=cols_sb[:, c0:c0 + 1])\
                        .then_inc(a_rnd, 1)

                if live(a):
                    exps(0)
                    if isinstance(a, int) and a == 0:
                        act.wait_ge(d_adj, 16 * (NB // GM) * (GM + 1))
                    need(act, g_cnt, 2 * a)
                    need(act, g_lab, 2 * a)
                    act.activation(labF0[:, :], adj0[:, a, :], ACT.Copy).then_inc(g_flt, 1)
                    act.activation(labF1[:, :], adj1[:, a, :], ACT.Copy).then_inc(g_flt, 1)
                if live(f):
                    need(act, a_xnT, f + 1)
                    need(act, a_v, f)
                    act.activation(ut[:, :], bank[0][:, 0:S], ACT.Identity, bias=AB0T[:, 1, one(f)],
                                   scale=AB0T[:, 0, one(f)]).then_inc(a_u, 1)
                if live(a):
                    exps(1)
                if live(f):
                    rounded(0)
                if live(a):
                    exps(2)
                if live(f):
                    rounded(1)
                if live(a):
                    exps(3)
                    need(act, a_atT, a + 1)
                    need(act, a_o, a)
                    act.activation(at0T[:, :], bank[0][:, 128:256], ACT.Copy).then_inc(a_atS, 1)
                if live(f):
                    need(act, a_mT, f + 1)
                    need(act, a_ST, NC0 * f)
                    act.activation(mT0[:, :], bank[7][:, 128:256], ACT.Copy).then_inc(a_mTs, 1)

            slots(act, l0_slot, 4, NB, NB + 1)
            def l1_slot(t, u):
                f, a = t, t - 1
                front, att = live(f), live(a)

                def exps(d):
                    need(act, b_sub, 2 * a + 1 + d)
                    need(act, b_eT, 2 * a - 1 + d)
                    act.activation(ex1[:, d, 0:H0 * NG], aff[:, d, :], ACT.Exp).then_inc(b_ex, 1)

                def exps_t(d):
                    need(act, b_eT, 2 * a + 1 + d)
                    need(act, b_PV, 2 * a - 1 + d)
                    act.activation(exT[:, d, :], bank[5 + d][0:HC * NG, 0:NC1 * S], ACT.Copy).then_inc(b_eTs, 1)

                if front:
                    need(act, b_xT, f + 1)
                    need(act, b_sf, f)
                    act.activation(xT1[:, :], bank[0][:, 0:S], ACT.Copy).then_inc(b_xTs, 1)
                if att:
                    exps(0)
                    exps_t(0)
                if front:
                    need(act, b_sT, f + 1)
                    need(act, b_q, f)
                    act.activation(selfT[:, :], bank[0][:, 256:384], ACT.Copy).then_inc(b_sTs, 1)
                    act.activation(selfR[:, :, :],
                                   bank[0][:, 256:256 + NG].unsqueeze(1).to_broadcast([P, HC, NG]), ACT.Copy)\
                        .then_inc(b_sTs, 1)
                if att:
                    exps(1)
                if front:
                    need(act, b_q, f + 1)
                    need(act, b_S, 2 * (f - 1))
                    for d in range(2):
                        c0 = COL_COLS["bq1"][0] + d
                        act.activation(qT1[:, u, d, :], bank[1][:, d * S:(d + 1) * S], ACT.Identity,
                                       bias=cols_sb[:, c0:c0 + 1]).then_inc(b_qs, 1)
                if att:
                    exps_t(1)
                if front:
                    cs = bass.ds(f * W2P, W2P)
                    act.activation(w2h[:, cs], w2raw[:, cs], ACT.Copy).then_inc(e_h, 1)

            act.wait_ge(d_w2, 16)
            slots(act, l1_slot, 2, NB, NB + 1)
            act.wait_ge(b_x2, NB)
            act.wait_ge(s_cqT, 2)

            def l2_slot(t, u):
                g, f, a = t, t - 1, t - 2
                lead, front, att = live(g), live(f), live(a)
                v = 1 - u

                def exps(r):
                    need(act, c_SM, 4 * a + r + 1)
                    act.activation(P2[:, r % 2, :], P2[:, r % 2, :], ACT.Exp).then_inc(c_P, 1)

                def taken(j):
                    need(act, c_pj, 8 * f + j + 1)
                    need(act, c_T, 4 * f + j - 1)
                    act.activation(qkt[:, j % 2, :], bank[1 + j % 2][:, :], ACT.Copy, scale=HD2 ** -0.5)\
                        .then_inc(c_cp, 1)

                def turned(j):
                    need(act, c_T, 4 * f + j + 1)
                    need(act, c_ST, 4 * (f - 1))
                    act.activation(qkT[:, v, j % 2, 4 * (j // 2):4 * (j // 2) + 4, :],
                                   bank[3][:, :].rearrange("p (c s) -> p c s", s=S), ACT.Copy).then_inc(c_Ts, 1)

                def val(n):
                    need(act, c_pj, 8 * f + 5 + n)
                    need(act, c_PV, 4 * (f - 1))
                    act.activation(V2[:, v, 8 * n:8 * n + 8, 0:HD2],
                                   bank[1 + n][:, :].rearrange("p (h d) -> p h d", d=HD2), ACT.Copy).then_inc(c_V, 1)

                if att:
                    exps(0)
                if front:
                    taken(0)
                    taken(1)
                if att:
                    exps(1)
                if front:
                    turned(0)
                    taken(2)
                if att:
                    exps(2)
                if front:
                    turned(1)
                    taken(3)
                if att:
                    exps(3)
                if lead:
                    need(act, c_xT, g + 1)
                    need(act, c_pj, 8 * (g - 1))
                    need(act, c_ul, g - 1)
                    act.activation(uT2[:, u, :], bank[0][:, 0:S], ACT.Identity, bias=AB2T[:, 1, one(g)],
                                   scale=AB2T[:, 0, one(g)]).then_inc(c_u, 1)
                    act.activation(uTh[:, u, :], bank[0][:, 0:S], ACT.Identity, bias=AB2T[:, 1, one(g)],
                                   scale=AB2T[:, 0, one(g)]).then_inc(c_u, 1)
                if front:
                    turned(2)
                    val(0)
                    val(1)
                    turned(3)
                    need(act, c_pj, 8 * f + 7)
                    need(act, c_ff, f)
                    act.activation(gel[:, :, :].rearrange("p c s -> p (c s)"), bank[1][:, :], ACT.Gelu,
                                   scale=2.0 ** 0.5 / 1.41421).then_inc(c_gel, 1)
                if att:
                    for n in range(2):
                        need(act, c_OT, 2 * a + n + 1)
                        need(act, c_o, a)
                        act.activation(OT2[:, 4 * n:4 * n + 4, :], bank[3][:, :].rearrange("p (c s) -> p c s", s=S),
                                       ACT.Copy).then_inc(c_OTs, 1)
                if front:
                    need(act, c_mT, f + 1)
                    need(act, c_ST, 4 * f)
                    act.activation(mT2[:, :], bank[0][:, 128:256], ACT.Copy).then_inc(c_mTs, 1)
                if att:
                    need(act, c_x3, a + 1)
                    need(act, c_ss, a)
                    act.activation(sq3[:, :], x3[:, :], ACT.Square).then_inc(c_sq, 1)

            slots(act, l2_slot, 4, NB, NB + 2)

        @block.gpsimd
        def _(pool):
            pool.memset(onesP[:, :], 1.0).then_inc(s_one, 1)
            pool.memset(eps_c[:, :], EPS).then_inc(s_const, 1)
            pool.memset(neg_half[:, :], -0.5).then_inc(s_const, 1)
            pool.memset(nm0[:, :], 0.0).then_inc(s_const, 1)
            pool.memset(V0[:, 0, :, HD0], 1.0).then_inc(s_const, 1)
            pool.memset(V0[:, 1, :, HD0], 1.0).then_inc(s_const, 1)
            pool.wait_ge(s_const, 5)
            pool.wait_ge(s_mean0, NB)
            pool.tensor_tensor(rstd0[:, :], mean0[:, :, 1], eps_c[:, :].to_broadcast([P, NB]), ALU.add)\
                .then_inc(s_ve, 1)
            pool.wait_ge(s_ve, 1)
            pool.tensor_tensor(rstd0[:, :], rstd0[:, :], neg_half[:, :], ALU.pow).then_inc(s_rstd0, 1)
            pool.wait_ge(d_bc, 48)
            pool.tensor_copy(sel12[:, :, :], cst("sel4")[0:3 * NC0, :].unsqueeze(2).to_broadcast([3 * NC0, NC0, S]))\
                .then_inc(s_const, 1)
            pool.tensor_copy(sel0[:, :, :], cst("sel4").unsqueeze(2).to_broadcast([P, NC0, P]))\
                .then_inc(s_const, 1)
            pool.wait_ge(d_ab0, 16)
            w_lab = bcv("w_bias")

            def l0_slot(t, u):
                a, v = t - 1, 1 - u
                if live(a):
                    need(pool, a_h1, a)
                    pool.tensor_tensor(xb0[:, :], X[:, a, :], bcv("bp0"), ALU.add).then_inc(a_xb, 1)
                    for n, (flt, lab, parts, m) in enumerate(((labF0, lab0, P, NG), (labF1, lab1, GM * NG, GN))):
                        need(pool, g_flt, 2 * a + 1 + n)
                        need(pool, g_vb, 2 * a - 1 + n)
                        pool.tensor_tensor(lab[:, :].rearrange("p (m l) -> p m l", l=NL),
                                           flt[:, :].rearrange("p (m l) -> p m l", l=NL),
                                           w_lab[0:parts, :].unsqueeze(1).to_broadcast([parts, m, NL]),
                                           ALU.mult).then_inc(g_lab, 1)
                    need(pool, a_bn, 2 * a + 2)
                    pool.tensor_tensor(ve0[:, :], mv0[:, v, 1:2], eps_c[:, :], ALU.add).then_inc(a_ve, 1)
                    need(pool, a_ve, a + 1)
                    need(pool, a_x1, a - 1)
                    pool.tensor_tensor(rs0[:, v, :], ve0[:, :], neg_half[:, 0:1], ALU.pow).then_inc(a_rs, 1)
                    pool.tensor_tensor(hb0[:, v, :], h1[:, v, :], AB0[:, a, D:2 * D], ALU.add).then_inc(a_hb, 1)

            slots(pool, l0_slot, 4, NB, NB + 1)
            pool.wait_ge(a_x1, NB)
            pool.memset(ex1[:, :, H0 * NG:H1P * NG], 0.0).then_inc(g_pad, 1)
            for n in range(2):
                pool.tensor_copy(VW[:, n, :, :, HD0],
                                 cst("bd_v")[0:HC * NG, :].rearrange("p (h d) -> p h d", d=HD0)[:, :, 0].unsqueeze(1)
                                 .to_broadcast([HC * NG, 2, H1P])).then_inc(g_pad, 1)

            def l1_slot(t, u):
                a = t - 1
                if live(a):
                    for d in range(2):
                        need(pool, b_mx, 2 * a + 1 + d)
                        need(pool, b_ex, 2 * a - 1 + d)
                        pool.tensor_tensor(aff[:, d, :].rearrange("p (h m) -> p h m", m=NG),
                                           aff[:, d, :].rearrange("p (h m) -> p h m", m=NG),
                                           mx1[:, d, :].unsqueeze(2).to_broadcast([P, H0, NG]), ALU.subtract)\
                            .then_inc(b_sub, 1)

                if live(t):
                    cs = bass.ds(t * W2P, W2P)
                    need(pool, e_h, t + 1)
                    pool.tensor_tensor(w2l[:, cs], w2raw[:, cs], w2h[:, cs].bitcast(F32), ALU.subtract)\
                        .then_inc(e_l, 1)

            slots(pool, l1_slot, 2, NB, NB + 1)
            pool.wait_ge(b_x2, NB)
            pool.memset(V2[:, 0, :, HD2], 1.0).then_inc(c_const, 1)
            pool.memset(V2[:, 1, :, HD2], 1.0).then_inc(c_const, 1)
            pool.tensor_copy(sel2[:, :, :], cst("sel8").unsqueeze(2).to_broadcast([P, HC2, P])).then_inc(c_const, 1)
            pool.wait_ge(c_const, 5)

            def l2_slot(t, u):
                g, f, a, e = t, t - 1, t - 2, t - 3
                lead, front, att, tail = live(g), live(f), live(a), live(e)

                def rotated(j):
                    need(pool, c_rope, 8 * f + 2 * j + 2)
                    pool.tensor_tensor(qkt[:, j % 2, :].rearrange("p (h d) -> p h d", d=HD2)[:, :, 0:ROT],
                                       rcos[:, :, :], rsin[:, :, :], ALU.add).then_inc(c_rot, 1)

                if tail:
                    need(pool, c_ms, e + 1)
                    need(pool, c_y, e)
                    pool.tensor_tensor(rs3[:, :], ms3[:, :], neg_half[:, 0:1], ALU.pow).then_inc(c_r3, 1)
                if front:
                    rotated(0)
                    rotated(1)
                    rotated(2)
                    rotated(3)
                if lead:
                    need(pool, c_bn, 2 * g + 2)
                    pool.tensor_tensor(ve2[:, :], mv2[:, 1:2], eps_c[:, :], ALU.add).then_inc(c_ve, 1)
                    need(pool, c_ve, g + 1)
                    need(pool, c_xn, g)
                    pool.tensor_tensor(rs2[:, :], ve2[:, :], neg_half[:, 0:1], ALU.pow).then_inc(c_rs, 1)
                if att:
                    need(pool, c_x3, a)
                    pool.tensor_tensor(xb2[:, :], X[:, a, :], bsum2[:, :], ALU.add).then_inc(c_xb, 1)

            slots(pool, l2_slot, 4, NB, NB + 3)


def bf16_rounded(table):
    import numpy as np
    bits = table.astype(np.float32).view(np.uint32)
    return ((bits + 0x7FFF + (bits >> 16 & 1)) & 0xFFFF0000).astype(np.uint32).view(np.float32)


def laid_out(inputs):
    import numpy as np
    g = {k: np.ascontiguousarray(v) for k, v in inputs.items()}

    def per_head(t):
        return np.ascontiguousarray(g["L0_cond_Wqkv"].reshape(H0, HD0, 3, D)[:, :, t]), \
            np.ascontiguousarray(g["L0_cond_bqkv"].reshape(H0, HD0, 3)[:, :, t])

    def packed(w):
        return np.repeat(w.reshape(H0, 1, HD0, -1), 4, axis=1).reshape(H0 * 4 * HD0, -1)

    (wq, bq), (wk, bk), (wv, bv) = (per_head(t) for t in range(3))
    w0 = np.concatenate([packed(wq).T, packed(wk).T, wv.reshape(D, D).T], axis=1)
    bias_qk0 = np.concatenate([packed(bq[..., None]).reshape(NC0, P), packed(bk[..., None]).reshape(NC0, P)], axis=1)
    w_self = g["L1_cond_W_self"]
    wout = g["L1_cond_Wout"].reshape(2, D, D)
    pad = np.zeros((2, (H1P - H0) * HD0, D), np.float32)
    wout = np.concatenate([wout, pad], axis=1)
    w1 = np.concatenate([g["L0_cond_Wp"].T, w_self[:, :D].T, g["L1_cond_Wq"][0].T, g["L1_cond_Wq"][1].T,
                         g["L1_cond_Wk"][0].T, g["L1_cond_Wk"][1].T, wout[0].T, wout[1].T], axis=1)
    wc = np.concatenate([g["L0_cond_Wg"].T, g["L0_cond_Wb"].T, w_self[:, D:].T, g["L2_cond_cond_w"],
                         g["L3_cond_w_proj"].T], axis=1)
    rows = np.concatenate([g[k].reshape(-1) for k in (
        "L0_cond_bg", "L0_cond_bb", "L0_cond_ln_g", "L0_cond_ln_b", "L2_cond_cond_b", "L2_cond_ln_w",
        "L2_cond_ln_b", "L3_cond_b_proj", "L3_cond_rms_weight")])[None]
    bc = np.concatenate([bv.reshape(-1)] + [g[k].reshape(-1) for k in (
        "L0_cond_bp", "L1_cond_b_self", "L1_cond_bout", "L2_cond_attn_proj_b", "L2_cond_ff_proj_b",
        "L1_cond_w_bias", "L1_cond_b_bias")])[None]
    part = np.arange(P) % 32 // HD0
    part_q, part_k = np.array([0, 1, 0, 1], np.float32)[part], np.array([0, 0, 1, 1], np.float32)[part]
    cols = np.stack([*g["L1_cond_bq"], *g["L1_cond_bk"], part_q, part_k], axis=1)
    bd_k = (np.arange(P)[:, None] // HD0 == np.arange(H0 * NG)[None] // NG).astype(np.float32)
    bd_v = (np.arange(P)[:, None] // NG == np.arange(HC * HD0)[None] // HD0).astype(np.float32)
    inv_freq = np.float32(1.0) / np.float32(10000.0) ** (np.arange(0, ROT, 2, dtype=np.float32) / np.float32(ROT))
    freqs = np.arange(S, dtype=np.float32)[:, None] * inv_freq[None]
    cos, sin = bf16_rounded(np.cos(freqs)), bf16_rounded(np.sin(freqs))
    cst = np.concatenate([np.eye(P, dtype=np.float32), bd_k, np.tile(bd_v, (1, NC1)), cos, cos, -sin, sin,
                          (np.arange(P)[:, None] % NC0 == np.arange(NC0)[None]).astype(np.float32),
                          (np.arange(P)[:, None] % 8 == np.arange(8)[None]).astype(np.float32)], axis=1)
    return {
        "x": g["x"], "cond_t": g["cond_1024"].T, "cond_r": g["cond_1024"], "w0": w0, "bias_qk0": bias_qk0,
        "w1": w1, "wc": wc, "rows": rows, "bc": bc, "cols": cols, "cst_d": cst, "adj": g["mask_BxSxSx11_ik0"],
        "w2": g["L2_cond_proj_in_w"],
        "attn_w": g["L2_cond_attn_proj_w"], "ff_w": g["L2_cond_ff_proj_w"],
        "mask": g["mask_Bx1xSxS_ff0"].reshape(NB, S, S),
        "mask_t": g["mask_Bx1xSxS_ff0"].reshape(NB, S, S).transpose(0, 2, 1),
    }


def kernel(**inputs):
    import numpy as np
    import concourse.bacc as bacc
    from concourse.bass_utils import run_bass_kernel_spmd

    nc = bacc.Bacc("TRN2", target_bir_lowering=False, num_devices=1)
    arrays, args = {}, {}
    for name, a in laid_out(inputs).items():
        a = np.ascontiguousarray(a)
        arrays[f"in_{name}"] = a
        args[name] = nc.dram_tensor(f"in_{name}", a.shape, mybir.dt.from_np(a.dtype), kind="ExternalInput").ap()
    args["out"] = nc.dram_tensor("out_0", (NB, S, D), F32, kind="ExternalOutput").ap()
    build(nc, **args)
    got = run_bass_kernel_spmd(nc, [arrays], core_ids=[0])
    return got.results[0]["out_0"]
```

```python
from contextlib import ExitStack

import concourse.bass as bass
from concourse import mybir

F32 = mybir.dt.float32
F32R = mybir.dt.float32r
BF16 = mybir.dt.bfloat16
I32 = mybir.dt.int32
ALU = mybir.AluOpType
ACT = mybir.ActivationFunctionType
AX = mybir.AxisListType.X

NB, S, D = 16, 128, 128
P = 128
H0, HD0 = 16, 8
VW0 = 32
G = 4
NC0 = H0 // G
NG, NL = 20, 11
HC = 6
NC1 = 3
H1P = HC * NC1
GM = 4
GN = S // GM
H2, HD2, ROT = 16, 64, 32
FF = 4 * D
W2P = 3 * H2 * HD2 // NB
EPS = 1e-5
NEG = -9000000000000000.0
BIG_ROUND = 12582912.0

START, WARM = 12, 12
BUSY, DRAIN = 4, 8
LEAP, FILL = 12, 4
LEAD, LIFT = 5, 5
TAIL, HOLD = 2, 2


def columns(*pieces):
    at, out = 0, {}
    for name, width in pieces:
        out[name] = (at, at + width)
        at += width
    return out, at


W0_COLS, W0_N = columns(("q", NC0 * P), ("k", NC0 * P), ("v", D))
W1_COLS, W1_N = columns(("wp0", D), ("self", D), ("q", 2 * D), ("k", 2 * D), ("out", 2 * H1P * HD0))
WC_COLS, WC_N = columns(("gb", 2 * D), ("self_q", D), ("sb", 2 * D), ("proj", 2 * D))
ROW_COLS, ROW_N = columns(("gb0", 2 * D), ("ln_g0", D), ("ln_b0", D), ("cond_b", 2 * D), ("ln_w2", D),
                          ("ln_b2", D), ("b_proj", 2 * D), ("rms_w", D))
BC_COLS, BC_N = columns(("bv0", D), ("bp0", D), ("b_self", D), ("bout", 2 * D), ("attn_b", D), ("ff_b", D),
                        ("w_bias", NL), ("b_bias", 1))
COL_COLS, COL_N = columns(("bq1", 2), ("bk1", 2), ("part_q", 1), ("part_k", 1))
CST_COLS, CST_N = columns(("ident", P), ("bd_k", H0 * NG), ("bd_v", NC1 * HC * HD0), ("cos", ROT), ("sin", ROT), ("sel4", NC0), ("sel8", H2 // 2))


def need(engine, sem, value):
    if isinstance(value, int) and value <= 0:
        return
    engine.wait_ge(sem, value)


def slots(engine, slot, first, last, total, begin=0):
    for t in range(begin, first):
        slot(t, t % 2)
    with engine.Fori(first // 2, last // 2) as i:
        for u in range(2):
            slot(2 * i + u, u)
    for t in range(last, total):
        slot(t, t % 2)


def one(b):
    return slice(b, b + 1) if isinstance(b, int) else bass.ds(b, 1)


def live(b):
    return not isinstance(b, int) or 0 <= b < NB


def build(nc, x, cond_t, cond_r, w0, bias_qk0, w1, wc, rows, bc, cols, cst_d, adj, w2, attn_w, ff_w, mask, mask_t, out):
    ctx = ExitStack()
    with ctx:
        def sb(name, shape, dt=F32, where=ctx):
            return where.enter_context(nc.sbuf_tensor(name, shape, dt))

        def sem(name):
            return ctx.enter_context(nc.semaphore(name))

        bank = [ctx.enter_context(nc.psum_tensor(f"bank{i}", [P, 512], F32)) for i in range(8)]

        X = sb("X", [P, NB, D])
        bc_sb = sb("bc_sb", [P, BC_N])
        cols_sb = sb("cols_sb", [P, COL_N])
        cst_sb = sb("cst_sb", [P, CST_N])
        carrier = sb("carrier", [P, 1])
        identB = sb("identB", [P, P], BF16)
        sel0 = sb("sel0", [P, NC0, P], BF16)
        eps_c = sb("eps_c", [P, 1])
        neg_half = sb("neg_half", [P, NB])
        AB0T = sb("AB0T", [P, 2, NB])
        AB2T = sb("AB2T", [P, 2, NB])

        w1_sb = sb("w1_sb", [P, W1_N])
        w2h = sb("w2h", [P, 3 * H2 * HD2], F32R)
        w2l = sb("w2l", [P, 3 * H2 * HD2], F32R)
        w_ff = sb("w_ff", [P, 2 * FF])
        w_at = sb("w_at", [P, H2 * HD2 // P, D])
        w_fo = sb("w_fo", [P, FF // P, D])

        def bcv(name):
            a, b = BC_COLS[name]
            return bc_sb[:, a:b]

        def cst(name):
            a, b = CST_COLS[name]
            return cst_sb[:, a:b]

        ident = cst("ident")

        early = ExitStack()
        l0 = early
        AB0 = sb("AB0", [P, NB, 2 * D], F32, l0)
        w0_sb = sb("w0_sb", [P, W0_N], F32, l0)
        bqk_raw = sb("bqk_raw", [NC0, 2 * P], F32, l0)
        bqk_part = sb("bqk_part", [NC0, 3, 2 * P], BF16, l0)
        bqk_rest = sb("bqk_rest", [NC0, 2, 2 * P], F32, l0)
        bqk = sb("bqk", [3 * NC0, 2 * P], BF16, l0)
        sel12 = sb("sel12", [3 * NC0, NC0, S], BF16, l0)
        mean0 = sb("mean0", [P, NB, 2], F32, l0)
        rstd0 = sb("rstd0", [P, NB], F32, l0)
        xn = sb("xn", [P, D], F32, l0)
        ut = sb("ut", [P, D], F32, l0)
        rnd = sb("rnd", [P, 2, NC0 * P], F32R, l0)
        pack = sb("pack", [P, 2, 2, NC0, S], F32R, l0)
        V0 = sb("V0", [P, 2, H0, VW0], F32, l0)
        m0 = sb("m0", [P, G, NC0], F32, l0)
        nm0 = sb("nm0", [P, P], BF16, l0)
        mT0 = sb("mT0", [P, S], BF16, l0)
        P0 = sb("P0", [P, 2, G * S], F32, l0)
        rc0 = sb("rc0", [P, H0], F32, l0)
        at0 = sb("at0", [P, D], F32, l0)
        at0T = sb("at0T", [P, D], F32, l0)
        xb0 = sb("xb0", [P, D], F32, l0)
        h1 = sb("h1", [P, 2, D], F32, l0)
        st0 = sb("st0", [P, 6], F32, l0)
        mv0 = sb("mv0", [P, 2, 2], F32, l0)
        ve0 = sb("ve0", [P, 1], F32, l0)
        rs0 = sb("rs0", [P, 2, 1], F32, l0)
        hb0 = sb("hb0", [P, 2, D], F32, l0)
        tn0 = sb("tn0", [P, D], F32, l0)

        l1 = early
        QP1 = sb("QP1", [P, NB, D], F32, l1)
        adj0 = sb("adj0", [P, NB, NG * NL], I32, l1)
        adj1 = sb("adj1", [GM * NG, NB, GN * NL], I32, l1)
        labF0 = sb("labF0", [P, NG * NL], F32, l1)
        labF1 = sb("labF1", [GM * NG, GN * NL], F32, l1)
        lab0 = sb("lab0", [P, NG * NL], F32, l1)
        lab1 = sb("lab1", [GM * NG, GN * NL], F32, l1)
        cnt0 = sb("cnt0", [P, NB, NG], F32, l1)
        cnt1 = sb("cnt1", [GM * NG, NB, GN], F32, l1)
        vb0 = sb("vb0", [P, NB, NG], F32, l1)
        vb1 = sb("vb1", [GM * NG, NB, GN], F32, l1)
        w2raw = sb("w2raw", [P, 3 * H2 * HD2], F32, early)

        raw = ExitStack()
        siluT = sb("siluT", [P, NB], F32, raw)
        cabs = sb("cabs", [NB, D], F32, raw)
        wabs = sb("wabs", [P, 2 * D], F32, raw)
        onesP = sb("onesP", [P, P], F32, raw)
        sb2 = sb("sb2", [NB, 2 * D], F32, raw)
        R2 = sb("R2", [NB, 2 * D], F32, raw)
        R3 = sb("R3", [NB, 2 * D], F32, raw)
        emb3 = sb("emb3", [NB, 2 * D], F32, raw)
        cq = sb("cq", [NB, D], F32, raw)
        cq_s = sb("cq_s", [NB, 3], F32, raw)
        wq = sb("wq", [P, 2 * D], F32, raw)
        wq_s = sb("wq_s", [P, 3], F32, raw)
        cqT = sb("cqT", [P, NB], F32, raw)
        condT = sb("condT", [P, NB], F32, raw)
        condR = sb("condR", [NB, D], F32, raw)
        wc_sb = sb("wc_sb", [P, WC_N], F32, raw)
        rows_sb = sb("rows_sb", [NB, ROW_N], F32, raw)
        gb0 = sb("gb0", [NB, 2 * D], F32, raw)
        R0 = sb("R0", [NB, 2 * D], F32, raw)
        st_all = sb("st_all", [P, NB, 6], F32, raw)

        raw.close()

        Bc = sb("Bc", [P, NB, 2, NG], F32, l1)
        xs = sb("xs", [P, D], F32, l1)
        rsum = sb("rsum", [P, 1], F32, l1)
        nz = sb("nz", [P, 1], F32, l1)
        xT1 = sb("xT1", [P, S], F32, l1)
        cpart = sb("cpart", [P, D], F32, l1)
        selfTok = sb("selfTok", [P, D], F32, l1)
        selfB = QP1
        selfT = sb("selfT", [P, 2, S], F32, l1)
        selfR = sb("selfR", [P, 2, HC, NG], F32, l1)
        qT1 = sb("qT1", [P, 2, 2, S], F32, l1)
        kT1 = sb("kT1", [P, 2, NG], F32, l1)
        kbd = sb("kbd", [P, 2, 2, H0 * NG], F32, l1)
        VW = sb("VW", [HC * NG, 2, 2, H1P, HD0 + 1], F32, l1)
        aff = sb("aff", [P, 2, H0 * NG], F32, l1)
        mx1 = sb("mx1", [P, 2, H0], F32, l1)
        ex1 = sb("ex1", [P, 2, H1P * NG], F32, l1)
        exT = sb("exT", [HC * NG, 2, NC1 * S], F32, l1)
        rc1 = sb("rc1", [P, 2, H0], F32, l1)
        on1 = sb("on1", [P, 2, D], F32, l1)
        sum1 = sb("sum1", [P, 2, D], F32, l1)
        bout1 = sb("bout1", [P, D], F32, l1)
        qp_r = sb("qp_r", [NB, D], F32, l1)

        early.close()

        HC2 = H2 * HD2 // P
        sel2 = sb("sel2", [P, HC2, P], BF16)
        st2 = sb("st2", [P, 6])
        mv2 = sb("mv2", [P, 2])
        ve2 = sb("ve2", [P, 1])
        rs2 = sb("rs2", [P, 1])
        xn2 = sb("xn2", [P, D])
        uT2 = sb("uT2", [P, 2, S])
        uTh = sb("uTh", [P, 2, S], F32R)
        uTl = sb("uTl", [P, 2, S], F32R)
        V2 = sb("V2", [P, 2, H2, HD2 + 1])
        nm2 = sb("nm2", [P, P], BF16)
        bsum2 = sb("bsum2", [P, D])
        AB3 = sb("AB3", [P, NB, 2 * D])
        maskN = sb("maskN", [P, NB, S])
        maskT = sb("maskT", [P, NB, S])
        qkt = sb("qkt", [P, 2, 8 * HD2])
        rcos = sb("rcos", [P, 8, ROT])
        rsin = sb("rsin", [P, 8, ROT])
        qkT = sb("qkT", [P, 2, 2, HC2, S])
        qkB = sb("qkB", [P, 2, HC2, S], BF16)
        mask_b = sb("mask_b", [P, S])
        junk = sb("junk", [P, 4, S])
        m2 = sb("m2", [P, 2, HC2])
        mr2 = sb("mr2", [P, 2, 2, HC2])
        mT2 = sb("mT2", [P, S], BF16)
        P2 = sb("P2", [P, 2, G * S])
        rc2 = sb("rc2", [P, 2, G])
        O2 = sb("O2", [P, HC2, 2, HD2])
        OT2 = sb("OT2", [P, HC2, S])
        gel = sb("gel", [P, FF // P, S])
        ffT = sb("ffT", [P, 2, FF // P, S])
        xb2 = sb("xb2", [P, D])
        x3 = sb("x3", [P, D])
        tab = sb("tab", [P, 1])
        sq3 = sb("sq3", [P, D])
        ss3 = sb("ss3", [P, 1])
        ms3 = sb("ms3", [P, 1])
        rs3 = sb("rs3", [P, 1])
        y3 = sb("y3", [P, D])

        scr0 = nc.dram_tensor("scr0", (NB, 2 * D), F32, kind="Internal").ap()
        scr3 = nc.dram_tensor("scr3", (NB, 2 * D), F32, kind="Internal").ap()
        scr1 = nc.dram_tensor("scr1", (NB, D), F32, kind="Internal").ap()

        def w1c(name):
            a, b = W1_COLS[name]
            return w1_sb[:, a:b]

        def row(name):
            a, b = ROW_COLS[name]
            return rows_sb[:, a:b]

        def w0c(name):
            a, b = W0_COLS[name]
            return w0_sb[:, a:b]

        def wcc(name):
            a, b = WC_COLS[name]
            return wc_sb[:, a:b]

        d_x = [sem(f"d_x{n}") for n in range(4)]
        d_cond, d_cst, d_w0, d_bc, d_w1 = sem("d_cond"), sem("d_cst"), sem("d_w0"), sem("d_bc"), sem("d_w1")
        d_scr0, d_ab0, d_bqk = sem("d_scr0"), sem("d_ab0"), sem("d_bqk")
        s_const = sem("s_const")
        s_sel = sem("s_sel")
        s_gb0, s_R0, s_R0T, s_AB0T = sem("s_gb0"), sem("s_R0"), sem("s_R0T"), sem("s_AB0T")
        s_st, s_mean0, s_ve, s_rstd0 = sem("s_st"), sem("s_mean0"), sem("s_ve"), sem("s_rstd0")
        s_bq = sem("s_bq")
        d_out = sem("d_out")
        s_qp, s_qpr, d_scr1, d_qp = sem("s_qp"), sem("s_qpr"), sem("d_scr1"), sem("d_qp")
        d_adj = sem("d_adj")
        d_w2, d_wo, d_mn, d_mt = sem("d_w2"), sem("d_wo"), sem("d_mn"), sem("d_mt")
        d_scr3, d_ab3 = sem("d_scr3"), sem("d_ab3")
        s_act = sem("s_act")
        s_q = sem("s_q")
        s_p = sem("s_p")
        s_cqT, s_R2, s_R2T, s_R3 = sem("s_cqT"), sem("s_R2"), sem("s_R2T"), sem("s_R3")
        s_one = sem("s_one")

        a_xn = sem("a_xn")
        a_xnT = sem("a_xnT")
        a_u = sem("a_u")
        a_qk = sem("a_qk")
        a_v = sem("a_v")
        a_rnd = sem("a_rnd")
        a_pack = sem("a_pack")
        a_V = sem("a_V")
        a_S = sem("a_S")
        a_max = sem("a_max")
        a_nm = sem("a_nm")
        a_mT = sem("a_mT")
        a_mTs = sem("a_mTs")
        a_ST = sem("a_ST")
        a_P = sem("a_P")
        a_PV = sem("a_PV")
        a_rc = sem("a_rc")
        a_at = sem("a_at")
        a_atT = sem("a_atT")
        a_atS = sem("a_atS")
        a_o = sem("a_o")
        a_xb = sem("a_xb")
        a_h1 = sem("a_h1")
        a_bn = sem("a_bn")
        a_ve = sem("a_ve")
        a_rs = sem("a_rs")
        a_hb = sem("a_hb")
        a_tn = sem("a_tn")
        a_x1 = sem("a_x1")

        g_flt = sem("g_flt")
        g_lab = sem("g_lab")
        g_cnt = sem("g_cnt")
        g_vb = sem("g_vb")
        g_bc = sem("g_bc")
        g_bcT = sem("g_bcT")
        g_pad = sem("g_pad")

        b_xs = sem("b_xs")
        b_rs = sem("b_rs")
        b_nz = sem("b_nz")
        b_cp = sem("b_cp")
        b_xT = sem("b_xT")
        b_xTs = sem("b_xTs")
        b_sf = sem("b_sf")
        b_self = sem("b_self")
        b_sT = sem("b_sT")
        b_sTs = sem("b_sTs")
        b_q = sem("b_q")
        b_qs = sem("b_qs")
        b_kv = sem("b_kv")
        b_kT = sem("b_kT")
        b_kbd = sem("b_kbd")
        b_VW = sem("b_VW")
        b_S = sem("b_S")
        b_aff = sem("b_aff")
        b_mx = sem("b_mx")
        b_sub = sem("b_sub")
        b_ex = sem("b_ex")
        b_eT = sem("b_eT")
        b_eTs = sem("b_eTs")
        b_PV = sem("b_PV")
        b_rc = sem("b_rc")
        b_on = sem("b_on")
        b_sB = sem("b_sB")
        b_sum = sem("b_sum")
        b_x2 = sem("b_x2")

        e_h = sem("e_h")
        e_l = sem("e_l")

        c_const = sem("c_const")
        c_bn = sem("c_bn")
        c_ve = sem("c_ve")
        c_rs = sem("c_rs")
        c_xn = sem("c_xn")
        c_xT = sem("c_xT")
        c_u = sem("c_u")
        c_ul = sem("c_ul")
        c_pj = sem("c_pj")
        c_cp = sem("c_cp")
        c_rope = sem("c_rope")
        c_rot = sem("c_rot")
        c_T = sem("c_T")
        c_Ts = sem("c_Ts")
        c_B = sem("c_B")
        c_V = sem("c_V")
        c_gel = sem("c_gel")
        c_ff = sem("c_ff")
        c_G = sem("c_G")
        c_mk = sem("c_mk")
        c_jk = sem("c_jk")
        c_nm = sem("c_nm")
        c_mT = sem("c_mT")
        c_mTs = sem("c_mTs")
        c_ST = sem("c_ST")
        c_SM = sem("c_SM")
        c_P = sem("c_P")
        c_PV = sem("c_PV")
        c_rc = sem("c_rc")
        c_O = sem("c_O")
        c_OT = sem("c_OT")
        c_OTs = sem("c_OTs")
        c_tab = sem("c_tab")
        c_o = sem("c_o")
        c_xb = sem("c_xb")
        c_x3 = sem("c_x3")
        c_sq = sem("c_sq")
        c_ss = sem("c_ss")
        c_ms = sem("c_ms")
        c_r3 = sem("c_r3")
        c_y = sem("c_y")
        c_out = sem("c_out")

        block = ctx.enter_context(nc.Block())

        @block.sync
        def _(sp):
            sp.dma_start(condT[:, :], cond_t).then_inc(d_cond, 16)
            sp.dma_start(condR[:, :], cond_r).then_inc(d_cond, 16)
            sp.dma_start(wc_sb[:, :], wc).then_inc(d_cond, 16)
            sp.dma_start(rows_sb[:, :], rows.to_broadcast([NB, ROW_N])).then_inc(d_cond, 16)
            sp.dma_start(cst_sb[:, :], cst_d).then_inc(d_cst, 16)
            sp.dma_start(w0_sb[:, :], w0).then_inc(d_w0, 16)
            sp.dma_start(bqk_raw[:, :], bias_qk0).then_inc(d_w0, 16)
            x_tok = x.rearrange("b t d -> t b d")
            for n in range(4):
                sp.dma_start(X[:, 4 * n:4 * n + 4, :], x_tok[:, 4 * n:4 * n + 4, :]).then_inc(d_x[n], 16)
                if n == 0:
                    sp.dma_start(bc_sb[:, :], bc.to_broadcast([P, BC_N])).then_inc(d_bc, 16)
                    sp.dma_start(cols_sb[:, :], cols).then_inc(d_bc, 16)
            sp.wait_ge(s_bq, 5)
            for n in range(3):
                sp.dma_start(bqk[NC0 * n:NC0 * (n + 1), :], bqk_part[:, n, :]).then_inc(d_bqk, 16)
            sp.wait_ge(s_R0, 3)
            sp.dma_start(scr0, R0[:, :]).then_inc(d_scr0, 16)
            sp.wait_ge(d_scr0, 16)
            sp.dma_start(AB0[:, :, :], scr0.rearrange("(o b) d -> o b d", o=1).to_broadcast([P, NB, 2 * D]))\
                .then_inc(d_ab0, 16)
            sp.dma_start(w1_sb[:, :], w1).then_inc(d_w1, 16)
            for n in range(NB // GM):
                sp.dma_start(adj0[:, GM * n:GM * (n + 1), :],
                             adj[GM * n:GM * (n + 1), :, 0:NG, :].rearrange("b n m l -> n b (m l)")).then_inc(d_adj, 16)
                for b in range(GM):
                    sp.dma_start(adj1[NG * b:NG * (b + 1), GM * n:GM * (n + 1), :].rearrange("p a c -> p (a c)"),
                                 adj[GM * n + b, 0:NG, :, :].rearrange("m n l -> m (n l)")).then_inc(d_adj, 16)
            sp.wait_ge(s_qpr, 1)
            sp.dma_start(scr1, qp_r[:, :]).then_inc(d_scr1, 16)
            sp.wait_ge(d_scr1, 16)
            sp.dma_start(QP1[:, :, :], scr1.rearrange("(o b) d -> o b d", o=1).to_broadcast([P, NB, D]))\
                .then_inc(d_qp, 16)
            n2 = 3 * H2 * HD2
            sp.dma_start(w2raw[:, :], w2[:, 0:n2]).then_inc(d_w2, 16)
            sp.dma_start(w_ff[:, :], w2[:, n2:n2 + 2 * FF]).then_inc(d_wo, 16)
            sp.dma_start(w_at[:, :, :], attn_w.rearrange("(c p) n -> p c n", p=P)).then_inc(d_wo, 16)
            sp.dma_start(w_fo[:, :, :], ff_w.rearrange("(c p) n -> p c n", p=P)).then_inc(d_wo, 16)
            sp.wait_ge(s_R3, 2)
            sp.dma_start(scr3, R3[:, :]).then_inc(d_scr3, 16)
            sp.wait_ge(d_scr3, 16)
            sp.wait_ge(b_x2, NB)
            sp.dma_start(maskN[:, :, :], mask.rearrange("b q k -> q b k")).then_inc(d_mn, 16)
            sp.dma_start(maskT[:, :, :], mask_t.rearrange("b k q -> k b q")).then_inc(d_mt, 16)
            sp.dma_start(AB3[:, :, :], scr3.rearrange("(o b) d -> o b d", o=1).to_broadcast([P, NB, 2 * D]))\
                .then_inc(d_ab3, 16)
            sp.wait_ge(c_out, 1)
            with sp.Fori(0, NB) as b:
                sp.wait_ge(c_out, b + 1)
                sp.dma_start(out[bass.ds(b, 1), :, :].rearrange("b t d -> t b d"), X[:, bass.ds(b, 1), :])\
                    .then_inc(d_out, 16)
            sp.wait_ge(d_out, 16 * NB)

        @block.tensor
        def _(pe):
            def busy(n, into):
                for _ in range(n):
                    pe.matmul(into[:, :], identB[:, :], sel0[:, :, :].rearrange("p c s -> p (c s)"), start=True,
                              stop=True)

            pe.wait_ge(d_cond, 64)
            pe.matmul(bank[7][0:NB, 0:2 * D], condT[:, :], wcc("gb"), start=True, stop=True).then_inc(s_gb0, 1)
            pe.matmul(bank[5][0:NB, 0:D], condT[:, :], wcc("self_q"), start=True, stop=True).then_inc(s_qp, 1)
            pe.wait_ge(s_act, 1)
            pe.matmul(bank[4][0:NB, 0:2 * D], siluT[:, :], wcc("sb"), start=True, stop=True).then_inc(s_p, 1)
            pe.wait_ge(s_R0, 3)
            pe.wait_ge(d_cst, 16)
            for n in range(2):
                last = pe.transpose(bank[6][:, n * NB:(n + 1) * NB], R0[:, n * D:(n + 1) * D], ident[0:NB, 0:NB])
            last.then_inc(s_R0T, 1)
            pe.wait_ge(s_sel, 3)
            busy(START, bank[2])
            pe.wait_ge(s_one, 1)
            pe.wait_ge(s_q, 1)
            pe.matmul(bank[3][:, 0:1], onesP[:, :], wq_s[:, 0:1], start=True, stop=True).then_inc(s_p, 1)
            pe.wait_ge(d_w0, 32)
            pe.wait_ge(d_bqk, 48)
            pe.wait_ge(s_AB0T, 1)

            def l0_slot(t, u):
                g, f, e = t, t - 1, t - 2
                front, att, end = live(g), live(f), live(e)
                v = 1 - u

                def wide(c):
                    return min(c + 2, NC0)

                def scores(r):
                    rows_r = slice(32 * r, 32 * r + 32)
                    if r == 0:
                        need(pe, a_pack, 2 * f + 2)
                        need(pe, a_P, NC0 * f)
                    if r == 3:
                        need(pe, a_max, NC0 * f + 1)
                    for c in range(NC0):
                        w = wide(c)
                        last = pe.matmul(bank[3 + r % 3][:, c * S:w * S], pack[rows_r, v, 0, c, :],
                                         pack[rows_r, v, 1, c:w, :].rearrange("p c s -> p (c s)"),
                                         start=True, stop=True)
                    last.then_inc(a_S, 1)

                def scores_t(r):
                    rows_r = slice(32 * r, 32 * r + 32)
                    if r == 0:
                        need(pe, a_mTs, f + 1)
                    if r == 3:
                        need(pe, a_P, NC0 * f + 1)
                    for c in range(NC0):
                        w, dst = wide(c), bank[3 + (r + 1) % 3]
                        pe.matmul(dst[:, c * S:w * S], pack[rows_r, v, 1, c, :],
                                  pack[rows_r, v, 0, c:w, :].rearrange("p c s -> p (c s)"), start=True, stop=False)
                        last = pe.matmul(dst[:, c * S:(c + 1) * S], sel0[32 * r:32 * r + 8, c, :], mT0[32 * r:32 * r + 8, :],
                                         start=False, stop=True)
                    last.then_inc(a_ST, 1)

                def values(r):
                    need(pe, a_P, NC0 * f + r + 1)
                    if r == 0:
                        need(pe, a_V, f + 1)
                        need(pe, a_at, f)
                    for c in range(NC0):
                        n = G * r + c
                        w = min(n + 4, H0)
                        last = pe.matmul(bank[6][:, n * VW0:w * VW0], P0[:, r % 2, c * S:(c + 1) * S],
                                         V0[:, v, n:w, :].rearrange("p h d -> p (h d)"), start=True, stop=True)
                    last.then_inc(a_PV, 1)

                def bias(n):
                    need(pe, a_pack, 2 * g - 1 + n)
                    pe.matmul(bank[1 + n][:, :], bqk[:, n * P:(n + 1) * P],
                              sel12[:, :, :].rearrange("p c s -> p (c s)"), start=True, stop=False)

                def project(n, c):
                    last = pe.matmul(bank[1 + n][:, c * S:(c + 1) * S], w0c("qk"[n])[:, c * P:(c + 1) * P],
                                     ut[:, :], start=False, stop=(c == NC0 - 1))
                    if c == NC0 - 1:
                        last.then_inc(a_qk, 1)

                if att:
                    scores(0)
                    scores(1)
                if front:
                    need(pe, a_xn, g + 1)
                    need(pe, a_h1, g - 2)
                    pe.transpose(bank[0][:, 0:S], xn[:, :], ident).then_inc(a_xnT, 1)
                if att:
                    scores(2)
                if end:
                    need(pe, a_at, e + 1)
                    need(pe, a_mTs, e + 1)
                    pe.transpose(bank[7][:, 256:384], at0[:, :], ident).then_inc(a_atT, 1)
                if att:
                    scores(3)
                if front:
                    need(pe, a_u, g + 1)
                    bias(0)
                if end:
                    if isinstance(e, int) and e == 0:
                        pe.wait_ge(d_w1, 16)
                    need(pe, a_atS, e + 1)
                    pe.matmul(bank[0][:, 256:384], at0T[:, :], w1_sb[:, W1_COLS["wp0"][0]:W1_COLS["wp0"][1]],
                              start=True, stop=True).then_inc(a_o, 1)
                if front:
                    need(pe, a_mTs, g - 1)
                    pe.matmul(bank[7][:, 0:D], ut[:, :], w0c("v"), start=True, stop=True).then_inc(a_v, 1)
                    for c in range(NC0):
                        project(0, c)
                if front:
                    need(pe, a_pack, 2 * g)
                    busy(BUSY, bank[2])
                elif att:
                    busy(DRAIN, bank[2])
                if att:
                    need(pe, a_nm, 2 * f + 2)
                    need(pe, a_V, min(g + 1, NB) if isinstance(g, int) else g + 1)
                    pe.matmul(bank[7][:, 128:256], nm0[:, :], identB[:, :], start=True, stop=True)\
                        .then_inc(a_mT, 1)
                if front:
                    bias(1)
                    project(1, 0)
                if att:
                    scores_t(0)
                if front:
                    project(1, 1)
                if att:
                    scores_t(1)
                if front:
                    project(1, 2)
                if att:
                    values(0)
                if front:
                    project(1, 3)
                if att:
                    scores_t(2)
                    values(1)
                    if isinstance(g, int) and g == 2:
                        pe.wait_ge(a_h1, 1)
                        pe.wait_ge(s_q, 16)
                        pe.wait_ge(s_R2, 3)
                        pe.transpose(bank[0][:, 0:NB], cq[:, :], ident[0:NB, 0:NB]).then_inc(s_p, 1)
                        for n in range(2):
                            last = pe.transpose(bank[0][:, (n + 1) * NB:(n + 2) * NB], R2[:, n * D:(n + 1) * D],
                                                ident[0:NB, 0:NB])
                        last.then_inc(s_R2T, 1)
                    if isinstance(g, int) and g == 3:
                        pe.wait_ge(a_h1, 2)
                        pe.matmul(bank[0][0:NB, 0:2 * D], cqT[:, :], wq[:, :], start=True, stop=True).then_inc(s_p, 1)
                    scores_t(3)
                    values(2)
                    values(3)
                if isinstance(g, int) and g == 0:
                    pe.wait_ge(s_q, 2)
                    pe.wait_ge(s_R2, 1)
                    busy(WARM, bank[6])
                if isinstance(g, int) and g == 2:
                    pe.wait_ge(s_cqT, 2)
                if isinstance(g, int) and g == 3:
                    pe.wait_ge(s_R3, 1)

            slots(pe, l0_slot, 4, NB - 2, NB + 2)
            pe.wait_ge(a_h1, NB)
            pe.wait_ge(a_at, NB)
            busy(LEAP, bank[2])

            def l1_slot(t, u):
                g, f, a, e = t, t - 1, t - 2, t - 3
                v = 1 - u

                def weighted(d):
                    need(pe, b_eTs, 2 * e + 1 + d)
                    if d == 0:
                        if isinstance(e, int) and e == 0:
                            pe.wait_ge(g_bc, 6)
                        need(pe, b_VW, e + 1)
                        need(pe, b_on, e)
                    w = HC * (HD0 + 1)
                    for c in range(NC1):
                        n = min(c + 2, NC1)
                        last = pe.matmul(bank[7][:, (NC1 * d + c) * w:(NC1 * d + n) * w],
                                         exT[:, d, c * S:(c + 1) * S],
                                         VW[:, v, d, c * HC:n * HC, :].rearrange("p h d -> p (h d)"),
                                         start=True, stop=True)
                    last.then_inc(b_PV, 1)

                if isinstance(t, int) and t == 1:
                    pe.wait_ge(g_bc, 5)
                    for n in range(NB // GM):
                        last = pe.transpose(bank[7][:, n * GM * NG:(n + 1) * GM * NG],
                                            vb1[:, GM * n:GM * (n + 1), :].rearrange("p a c -> p (a c)"),
                                            ident[0:GM * NG, 0:GM * NG])
                    last.then_inc(g_bcT, 1)
                if live(a):
                    for d in range(2):
                        need(pe, b_qs, 2 * a + 2)
                        need(pe, b_kbd, 2 * a + 1 + d)
                        need(pe, b_aff, 2 * a - 1 + d)
                        pe.matmul(bank[3 + d][:, 0:H0 * NG], qT1[:, u, d, :], kbd[:, u, d, :], start=True,
                                  stop=True).then_inc(b_S, 1)
                if live(g):
                    need(pe, b_xs, g + 1)
                    need(pe, b_sTs, 2 * g)
                    pe.transpose(bank[0][:, 0:S], xs[:, :], ident).then_inc(b_xT, 1)
                if live(e):
                    for d in range(2):
                        need(pe, b_ex, 2 * e + 1 + d)
                        need(pe, b_eTs, 2 * e - 1 + d)
                        for c in range(NC1):
                            last = pe.transpose(bank[5 + d][0:HC * NG, c * S:(c + 1) * S],
                                                ex1[:, d, c * HC * NG:(c + 1) * HC * NG], ident)
                        last.then_inc(b_eT, 1)
                if live(f):
                    need(pe, b_sTs, 2 * f + 2)
                    need(pe, b_qs, 2 * f)
                    for d in range(2):
                        pe.matmul(bank[1][:, 256 + NG * d:256 + NG * (d + 1)], w1c("k")[:, d * D:(d + 1) * D],
                                  selfT[:, v, 0:NG], start=True, stop=True)
                    for d in range(2):
                        last = pe.matmul(bank[1][:, d * S:(d + 1) * S], w1c("q")[:, d * D:(d + 1) * D],
                                         selfT[:, v, :], start=True, stop=True)
                    last.then_inc(b_q, 1)
                if live(g):
                    if not live(e):
                        busy(FILL, bank[6])
                    need(pe, b_xTs, g + 1)
                    pe.matmul(bank[0][:, 128:256], xT1[:, :], w1c("self"), start=True, stop=True).then_inc(b_sf, 1)
                if isinstance(t, int) and t == NB + 1:
                    centred_t(0)
                if live(e):
                    weighted(0)
                    weighted(1)
                if live(g):
                    need(pe, b_self, g + 1)
                    pe.transpose(bank[0][:, 256:384], selfTok[:, :], ident).then_inc(b_sT, 1)
                if live(f):
                    need(pe, b_VW, f)
                    pe.matmul(bank[2][0:HC * NG, 0:288], selfR[:, v, :, :].rearrange("p r m -> p (r m)"),
                              w1c("out"), start=True, stop=True).then_inc(b_kv, 1)

            def centred_t(g):
                need(pe, c_xn, g + 1)
                need(pe, c_x3, g - 2)
                pe.transpose(bank[0][:, 0:S], xn2[:, :], ident).then_inc(c_xT, 1)

            slots(pe, l1_slot, 4, NB, NB + 3)
            busy(LEAD, bank[1])
            pe.wait_ge(b_x2, NB)
            pe.wait_ge(e_l, NB)
            pe.wait_ge(d_wo, 48)

            def l2_slot(t, u):
                g, f, a = t, t - 1, t - 2
                lead, front, att = live(g), live(f), live(a)
                v = 1 - u

                def project(j):
                    n = 8 * f + j
                    if j == 0:
                        need(pe, c_ul, f + 1)
                    if j == 0:
                        need(pe, c_gel, f)
                    elif j == 1:
                        need(pe, c_ff, f)
                    elif j <= 5:
                        need(pe, c_cp, 4 * f + j - 1)
                    else:
                        need(pe, c_V, 2 * f + j - 5)
                    dst = bank[1 + j % 2]
                    if j < 6:
                        c0 = (0, 1024, 512, 1536, 2048, 2560)[j]
                        cs = slice(c0, c0 + 512)
                        pe.matmul(dst[:, :], uTh[:, v, :], w2h[:, cs], start=True, stop=False)
                        pe.matmul(dst[:, :], uTh[:, v, :], w2l[:, cs], start=False, stop=False)
                        last = pe.matmul(dst[:, :], uTl[:, v, :], w2h[:, cs], start=False, stop=True)
                    else:
                        c0 = FF if j == 6 else 0
                        for c in range(FF // P):
                            last = pe.matmul(dst[:, c * S:(c + 1) * S], w_ff[:, c0 + c * P:c0 + (c + 1) * P],
                                             uT2[:, v, :], start=True, stop=True)
                    last.then_inc(c_pj, 1)

                def turn(j):
                    need(pe, c_rot, 4 * f + j + 1)
                    if j == 0:
                        need(pe, c_OTs, 2 * (f - 1))
                    else:
                        need(pe, c_Ts, 4 * f + j)
                    for c in range(4):
                        last = pe.transpose(bank[3][:, c * S:(c + 1) * S], qkt[:, j % 2, c * P:(c + 1) * P], ident)
                    last.then_inc(c_T, 1)

                def rough(r):
                    h0, c0 = 64 * (r % 2), 4 * (r // 2)
                    need(pe, c_B, 4 * f + 2 * (r // 2) + 2)
                    if r == 0:
                        need(pe, c_mTs, f)
                    elif r == 1:
                        need(pe, c_SM, 4 * a + 3)
                    else:
                        need(pe, c_jk, 16 * f + 4 * (r - 1))
                    for c in range(4):
                        last = pe.matmul(bank[7 - 3 * (r % 2)][:, c * S:(c + 1) * S], qkB[h0:h0 + 64, 0, c0 + c, :],
                                         qkB[h0:h0 + 64, 1, c0 + c, :], start=True, stop=True)
                    last.then_inc(c_G, 1)

                def scores_t(r):
                    h0, c0 = 64 * (r % 2), 4 * (r // 2)
                    need(pe, c_SM, 4 * a + r - 1)
                    if isinstance(a, int) and a == 0 and r == 0:
                        pe.wait_ge(c_const, 5)
                    if r == 0:
                        need(pe, c_mTs, a + 1)
                    for c in range(4):
                        dst = bank[4 + r % 2][:, c * S:(c + 1) * S]
                        pe.matmul(dst, qkT[h0:h0 + 64, u, 1, c0 + c, :], qkT[h0:h0 + 64, u, 0, c0 + c, :],
                                  start=True, stop=False)
                        last = pe.matmul(dst, sel2[h0:h0 + 24, c0 + c, :], mT2[h0:h0 + 24, :],
                                         start=False, stop=True)
                    last.then_inc(c_ST, 1)

                def values(r):
                    half, c0 = r % 2, 4 * (r // 2)
                    need(pe, c_P, 4 * a + r + 1)
                    need(pe, c_O, 4 * a + r)
                    if r == 0:
                        need(pe, c_V, 2 * a + 2)
                    for c in range(4):
                        last = pe.matmul(bank[6][:, c * (HD2 + 1):(c + 1) * (HD2 + 1)],
                                         P2[:, r % 2, c * S:(c + 1) * S], V2[:, u, 2 * (c0 + c) + half, :],
                                         start=True, stop=True)
                    last.then_inc(c_PV, 1)

                def results_t(n):
                    need(pe, c_O, 4 * a + 2 * n + 2)
                    if n == 1:
                        need(pe, c_OTs, 2 * a + 1)
                    elif front:
                        need(pe, c_Ts, 4 * f + 4)
                    for c in range(4):
                        last = pe.transpose(bank[3][:, c * S:(c + 1) * S],
                                            O2[:, 4 * n + c, :, :].rearrange("p h d -> p (h d)"), ident)
                    last.then_inc(c_OT, 1)

                if front:
                    project(0)
                elif att:
                    busy(TAIL, bank[1])
                if att:
                    scores_t(0)
                if front:
                    project(1)
                if att:
                    scores_t(1)
                if front:
                    if not att:
                        busy(LIFT, bank[5])
                    turn(0)
                elif att:
                    busy(HOLD, bank[1])
                if att:
                    values(0)
                if front:
                    project(2)
                if att:
                    scores_t(2)
                if front:
                    turn(1)
                elif att:
                    busy(HOLD, bank[1])
                if att:
                    values(1)
                if front:
                    project(3)
                if att:
                    scores_t(3)
                if front:
                    turn(2)
                elif att:
                    busy(HOLD, bank[1])
                if att:
                    values(2)
                if front:
                    rough(0)
                    project(4)
                    turn(3)
                if att:
                    values(3)
                if front:
                    project(5)
                    rough(1)
                if att:
                    results_t(0)
                if lead:
                    centred_t(g)
                if front:
                    project(6)
                    rough(2)
                if att:
                    results_t(1)
                if front:
                    rough(3)
                    project(7)
                if att:
                    need(pe, c_u, 2 * min(g + 1, NB) if isinstance(g, int) else 2 * g + 2)
                    need(pe, c_x3, a)
                    for c in range(HC2):
                        if c == HC2 // 2:
                            need(pe, c_OTs, 2 * a + 2)
                        pe.matmul(bank[0][:, 384:512], OT2[:, c, :], w_at[:, c, :], start=(c == 0), stop=False)
                    need(pe, c_ff, a + 1)
                    for c in range(FF // P):
                        last = pe.matmul(bank[0][:, 384:512], ffT[:, u, c, :], w_fo[:, c, :], start=False,
                                         stop=(c == FF // P - 1))
                    last.then_inc(c_o, 1)
                if front:
                    if not att:
                        busy(WARM, bank[5])
                    need(pe, c_nm, 5 * f + 5)
                    pe.matmul(bank[7][:, 0:128], nm2[:, :], identB[:, :], start=True, stop=True)\
                        .then_inc(c_mT, 1)

            slots(pe, l2_slot, 4, NB, NB + 2, begin=1)

        @block.vector
        def _(dve):
            dve.wait_ge(s_gb0, 1)
            dve.wait_ge(d_cond, 64)
            dve.tensor_tensor(gb0[:, :], bank[7][0:NB, 0:2 * D], row("gb0"), ALU.add).then_inc(s_R0, 1)
            dve.wait_ge(s_R0, 1)
            dve.tensor_tensor(R0[:, D:2 * D], gb0[:, 0:D], row("ln_b0"), ALU.mult).then_inc(s_R0, 1)
            dve.tensor_tensor(R0[:, 0:D], gb0[:, 0:D], row("ln_g0"), ALU.mult)
            dve.wait_ge(s_R0, 2)
            dve.tensor_tensor(R0[:, D:2 * D], R0[:, D:2 * D], gb0[:, D:2 * D], ALU.add).then_inc(s_R0, 1)
            dve.wait_ge(s_qp, 1)
            dve.tensor_copy(qp_r[:, :], bank[5][0:NB, 0:D]).then_inc(s_qpr, 1)
            dve.wait_ge(d_w0, 32)
            rest = bqk_raw[:, :]
            for n in range(3):
                dve.tensor_copy(bqk_part[:, n, :], rest).then_inc(s_bq, 1)
                if n < 2:
                    dve.wait_ge(s_bq, 2 * n + 1)
                    dve.tensor_tensor(bqk_rest[:, n, :], rest, bqk_part[:, n, :], ALU.subtract).then_inc(s_bq, 1)
                    dve.wait_ge(s_bq, 2 * n + 2)
                    rest = bqk_rest[:, n, :]
            dve.wait_ge(d_x[0], 16)
            dve.bn_stats(st_all[:, 0, :], X[:, 0, :]).then_inc(s_st, 1)
            dve.wait_ge(s_st, 1)
            dve.bn_aggr(mean0[:, 0, :], st_all[:, 0, :]).then_inc(s_mean0, 1)
            steps = iter(range(1, 100))

            def step(instruction):
                k = next(steps)
                instruction.then_inc(s_q, 1)
                dve.wait_ge(s_q, k)

            dve.wait_ge(s_act, 3)
            step(dve.tensor_reduce(wq_s[:, 0:1], wabs[:, :], AX, ALU.add))
            dve.wait_ge(s_p, 1)
            dve.tensor_tensor(sb2[:, :], bank[4][0:NB, 0:2 * D], row("cond_b"), ALU.add).then_inc(s_R2, 1)

            def input_of(n):
                need(dve, a_xnT, n)
                dve.tensor_scalar(xn[:, :], X[:, n, :], mean0[:, n, 0:1], rstd0[:, one(n)],
                                  ALU.subtract, ALU.mult).then_inc(a_xn, 1)

            dve.wait_ge(s_rstd0, 1)
            input_of(0)
            for b in range(1, NB):
                if b % 4 == 0:
                    dve.wait_ge(d_x[b // 4], 16)
                dve.bn_stats(st_all[:, b, :], X[:, b, :]).then_inc(s_st, 1)
            for b in range(1, NB):
                dve.wait_ge(s_st, b + 1)
                dve.bn_aggr(mean0[:, b, :], st_all[:, b, :]).then_inc(s_mean0, 1)
            dve.wait_ge(s_p, 2)
            step(dve.tensor_scalar(wq_s[:, 1:2], bank[3][:, 0:1], 1.0 / (2 * D * D), EPS, ALU.mult, ALU.max))
            dve.wait_ge(s_const, 5)
            dve.wait_ge(d_bc, 32)

            def second_setup():
                dve.wait_ge(s_R2, 1)
                dve.scalar_tensor_tensor(out=R2[:, D:2 * D], in0=sb2[:, 0:D], scalar=1.0, in1=row("ln_b2"),
                                         op0=ALU.add, op1=ALU.mult).then_inc(s_R2, 1)
                dve.scalar_tensor_tensor(out=R2[:, 0:D], in0=sb2[:, 0:D], scalar=1.0, in1=row("ln_w2"),
                                         op0=ALU.add, op1=ALU.mult)
                dve.wait_ge(s_R2, 2)
                dve.tensor_tensor(R2[:, D:2 * D], R2[:, D:2 * D], sb2[:, D:2 * D], ALU.add).then_inc(s_R2, 1)
                step(dve.tensor_reduce(cq_s[:, 0:1], cabs[:, :], AX, ALU.max))
                step(dve.tensor_scalar(cq_s[:, 0:1], cq_s[:, 0:1], EPS, None, ALU.max))
                step(dve.tensor_scalar(cq_s[:, 2:3], cq_s[:, 0:1], 1.0 / 127.0, None, ALU.mult))
                step(dve.reciprocal(cq_s[:, 1:2], cq_s[:, 2:3]))
                step(dve.tensor_scalar(cq[:, :], condR[:, :], cq_s[:, 1:2], None, ALU.mult))
                step(dve.tensor_scalar(cq[:, :], cq[:, :], BIG_ROUND, None, ALU.add))
                step(dve.tensor_scalar(cq[:, :], cq[:, :], BIG_ROUND, 127.0, ALU.subtract, ALU.min))
                step(dve.tensor_scalar(cq[:, :], cq[:, :], -128.0, cq_s[:, 2:3], ALU.max, ALU.mult))
                step(dve.tensor_tensor(cq[:, :], cq[:, :], condR[:, :], ALU.subtract))
                step(dve.reciprocal(wq_s[:, 2:3], wq_s[:, 1:2]))
                step(dve.tensor_scalar(wq[:, :], wcc("proj"), wq_s[:, 2:3], None, ALU.mult))
                step(dve.tensor_scalar(wq[:, :], wq[:, :], BIG_ROUND, None, ALU.add))
                step(dve.tensor_scalar(wq[:, :], wq[:, :], BIG_ROUND, 1.0, ALU.subtract, ALU.min))
                step(dve.tensor_tensor(cq[:, :], cq[:, :], condR[:, :], ALU.add))
                step(dve.tensor_scalar(wq[:, :], wq[:, :], -1.0, wq_s[:, 1:2], ALU.max, ALU.mult))
                step(dve.tensor_tensor(wq[:, :], wq[:, :], wcc("proj"), ALU.subtract))
                step(dve.tensor_tensor(wq[:, :], wq[:, :], wcc("proj"), ALU.add))

            def l0_slot(t, u):
                g, f, e, z = t, t - 1, t - 2, t - 3
                v = 1 - u

                def maxima(r):
                    need(dve, a_S, NC0 * f + r + 1)
                    if r == 0:
                        need(dve, a_nm, 2 * f)
                    dve.tensor_reduce(m0[:, r, :], bank[3 + r % 3][:, :].rearrange("p (c k) -> p c k", c=NC0),
                                      AX, ALU.max).then_inc(a_max, 1)

                def packed(n):
                    need(dve, a_rnd, 2 * g + 1 + n)
                    need(dve, a_ST, NC0 * (g - 1))
                    dve.tensor_tensor(pack[:, u, n, :, :].rearrange("p c s -> p (c s)"), bank[1 + n][:, :],
                                      rnd[:, n, :], ALU.subtract).then_inc(a_pack, 1)

                if live(f):
                    maxima(0)
                    maxima(1)
                if live(z):
                    if isinstance(z, int) and z == 0:
                        dve.wait_ge(d_ab0, 16)
                    need(dve, a_rs, z + 1)
                    need(dve, a_x1, z)
                    dve.scalar_tensor_tensor(out=tn0[:, :], in0=h1[:, v, :], scalar=mv0[:, v, 0:1],
                                             in1=AB0[:, z, 0:D], op0=ALU.subtract, op1=ALU.mult).then_inc(a_tn, 1)
                if live(f):
                    maxima(2)
                    maxima(3)
                    need(dve, a_max, NC0 * f + NC0)
                    need(dve, a_mT, f)
                    cols0 = nm0[:, :].rearrange("p (r c) -> p r c", r=G)
                    dve.tensor_scalar(cols0[:, :, 0:NC0], m0[:, :, :], -1.0, None, ALU.mult).then_inc(a_nm, 1)
                    need(dve, a_nm, 2 * f + 1)
                    dve.scalar_tensor_tensor(out=cols0[:, :, NC0:2 * NC0], in0=m0[:, :, :], scalar=-1.0,
                                             in1=cols0[:, :, 0:NC0], op0=ALU.mult, op1=ALU.subtract)\
                        .then_inc(a_nm, 1)
                if live(e):
                    need(dve, a_o, e + 1)
                    need(dve, a_xb, e + 1)
                    need(dve, a_x1, e - 1)
                    need(dve, a_hb, e - 1)
                    dve.tensor_tensor(h1[:, u, :], bank[0][:, 256:384], xb0[:, :], ALU.add).then_inc(a_h1, 1)
                if live(g):
                    need(dve, a_v, g + 1)
                    need(dve, a_PV, NC0 * (g - 1))
                    dve.tensor_tensor(V0[:, u, :, 0:HD0], bank[7][:, 0:D].rearrange("p (h d) -> p h d", h=H0),
                                      bcv("bv0").rearrange("p (h d) -> p h d", h=H0), ALU.add).then_inc(a_V, 1)
                    packed(0)
                if live(z):
                    need(dve, a_tn, z + 1)
                    need(dve, a_hb, z + 1)
                    dve.scalar_tensor_tensor(out=X[:, z, :], in0=tn0[:, :], scalar=rs0[:, v, :],
                                             in1=hb0[:, v, :], op0=ALU.mult, op1=ALU.add).then_inc(a_x1, 1)
                if live(e):
                    need(dve, a_h1, e + 1)
                    dve.bn_stats(st0[:, :], h1[:, u, :]).then_inc(a_bn, 1)
                if live(e):
                    need(dve, a_bn, 2 * e + 1)
                    need(dve, a_rs, e - 1)
                    dve.memset(carrier[:, :], 0.0)
                    dve.bn_aggr(mv0[:, u, :], st0[:, :]).then_inc(a_bn, 1)
                if live(e):
                    for n, (flt, lab, cnt, vb) in enumerate(((labF0, lab0, cnt0, vb0), (labF1, lab1, cnt1, vb1))):
                        need(dve, g_flt, 2 * e + 1 + n)
                        dve.tensor_reduce(cnt[:, e, :], flt[:, :].rearrange("p (m l) -> p m l", l=NL),
                                          AX, ALU.add).then_inc(g_cnt, 1)
                        need(dve, g_lab, 2 * e + 1 + n)
                        dve.tensor_reduce(vb[:, e, :], lab[:, :].rearrange("p (m l) -> p m l", l=NL),
                                          AX, ALU.add).then_inc(g_vb, 1)
                if live(g + 1):
                    if isinstance(g, int) and g == 0:
                        dve.wait_ge(s_rstd0, 2)
                    input_of(g + 1)
                if live(g):
                    packed(1)
                if isinstance(t, int) and t == 1:
                    second_setup()
                if isinstance(t, int) and t == 2:
                    dve.wait_ge(s_p, 3)
                    dve.wait_ge(s_R2T, 1)
                    dve.tensor_copy(cqT[:, :], bank[0][:, 0:NB]).then_inc(s_cqT, 1)
                    dve.tensor_copy(AB2T[:, :, :], bank[0][:, NB:3 * NB].rearrange("p (n b) -> p n b", n=2))\
                        .then_inc(s_cqT, 1)
                if isinstance(t, int) and t == 3:
                    dve.wait_ge(s_p, 4)
                    dve.tensor_tensor(emb3[:, :], bank[0][0:NB, 0:2 * D], row("b_proj"), ALU.add).then_inc(s_R3, 1)
                    dve.wait_ge(s_R3, 1)
                    dve.tensor_copy(R3[:, D:2 * D], emb3[:, D:2 * D])
                    dve.scalar_tensor_tensor(out=R3[:, 0:D], in0=emb3[:, 0:D], scalar=1.0, in1=row("rms_w"),
                                             op0=ALU.add, op1=ALU.mult).then_inc(s_R3, 1)
                if live(f):
                    need(dve, a_PV, NC0 * f + NC0)
                    O = bank[6][:, 0:H0 * VW0].rearrange("p (h d) -> p h d", h=H0)
                    dve.reciprocal(rc0[:, :], O[:, :, HD0]).then_inc(a_rc, 1)
                    need(dve, a_rc, f + 1)
                    need(dve, a_atT, f)
                    dve.scalar_tensor_tensor(out=at0[:, :].rearrange("p (h d) -> p h d", h=H0), in0=O[:, :, 0:HD0],
                                             scalar=1.0 / D ** 0.5,
                                             in1=rc0[:, :].unsqueeze(2).to_broadcast([P, H0, HD0]),
                                             op0=ALU.mult, op1=ALU.mult).then_inc(a_at, 1)

            slots(dve, l0_slot, 4, NB - 2, NB + 3)
            dve.tensor_tensor(bout1[:, :], bcv("bout")[:, 0:D], bcv("bout")[:, D:2 * D], ALU.add).then_inc(g_bc, 1)
            dve.wait_ge(a_x1, NB)
            dve.wait_ge(d_qp, 16)
            dve.wait_ge(d_scr3, 16)

            def additive():
                dve.wait_ge(g_cnt, 2 * NB)
                dve.wait_ge(g_vb, 2 * NB)
                for cnt in (cnt0, cnt1):
                    dve.tensor_scalar(cnt[:, :, :], cnt[:, :, :], 0.0, NEG, ALU.is_le, ALU.mult).then_inc(g_bc, 1)
                dve.wait_ge(g_bc, 3)
                bias1 = bcv("b_bias")
                dve.scalar_tensor_tensor(out=Bc[:, :, 0, :], in0=vb0[:, :, :], scalar=bias1, in1=cnt0[:, :, :],
                                         op0=ALU.add, op1=ALU.add).then_inc(g_bc, 1)
                dve.scalar_tensor_tensor(out=vb1[:, :, :], in0=vb1[:, :, :], scalar=bias1[0:GM * NG, :],
                                         in1=cnt1[:, :, :], op0=ALU.add, op1=ALU.add).then_inc(g_bc, 1)

            def staged(n):
                need(dve, b_xT, n)
                need(dve, b_rs, n)
                dve.tensor_copy(xs[:, :], X[:, n, :]).then_inc(b_xs, 1)

            def l1_slot(t, u):
                g, f, a, e = t, t - 1, t - 2, t - 3
                v = 1 - u

                def affinity(d):
                    need(dve, b_S, 2 * a + 1 + d)
                    need(dve, b_ex, 2 * a - 1 + d)
                    dve.scalar_tensor_tensor(
                        out=aff[:, d, :].rearrange("p (h m) -> p h m", m=NG),
                        in0=bank[3 + d][:, 0:H0 * NG].rearrange("p (h m) -> p h m", m=NG), scalar=1.0 / HD0 ** 0.5,
                        in1=Bc[:, a, d, :].unsqueeze(1).to_broadcast([P, H0, NG]), op0=ALU.mult, op1=ALU.add)\
                        .then_inc(b_aff, 1)

                def maximum(d):
                    need(dve, b_aff, 2 * a + 1 + d)
                    dve.tensor_reduce(mx1[:, d, :], aff[:, d, :].rearrange("p (h m) -> p h m", m=NG), AX,
                                      ALU.max).then_inc(b_mx, 1)

                O = bank[7][:, 0:2 * H1P * (HD0 + 1)].rearrange("p (e h d) -> p e h d", e=2, d=HD0 + 1)[:, :, 0:H0, :]
                if isinstance(t, int) and t == 0:
                    staged(0)
                if live(a):
                    affinity(0)
                if live(g):
                    need(dve, b_xs, g + 1)
                    dve.tensor_reduce(rsum[:, :], xs[:, :], AX, ALU.add).then_inc(b_rs, 1)
                if live(a):
                    maximum(0)
                if live(g):
                    need(dve, b_rs, g + 1)
                    dve.tensor_scalar(nz[:, :], rsum[:, :], 0.0, None, ALU.not_equal).then_inc(b_nz, 1)
                if live(a):
                    affinity(1)
                if live(g):
                    need(dve, b_nz, g + 1)
                    need(dve, b_self, g)
                    dve.scalar_tensor_tensor(out=cpart[:, :], in0=QP1[:, g, :], scalar=nz[:, :], in1=bcv("b_self"),
                                             op0=ALU.mult, op1=ALU.add).then_inc(b_cp, 1)
                if live(a):
                    maximum(1)
                if live(g):
                    need(dve, b_sf, g + 1)
                    need(dve, b_cp, g + 1)
                    need(dve, b_sB, g)
                    need(dve, b_sT, g)
                    dve.tensor_tensor(selfTok[:, :], cpart[:, :], bank[0][:, 128:256], ALU.add)\
                        .then_inc(b_self, 1)
                if live(g + 1):
                    staged(g + 1)
                if isinstance(t, int) and t == 0:
                    additive()
                if isinstance(t, int) and t == 1:
                    dve.wait_ge(g_bcT, 1)
                    dve.tensor_copy(Bc[:, :, 1, :], bank[7][:, 0:NB * NG].rearrange("p (b m) -> p b m", m=NG))\
                        .then_inc(g_bc, 1)
                if isinstance(t, int) and t == 1:
                    dve.wait_ge(g_bc, 6)
                if isinstance(t, int) and t == NB:
                    statistics(0)
                    aggregated(0)
                if isinstance(t, int) and t == NB + 1:
                    centred(0)
                if isinstance(t, int) and t == NB + 2:
                    units_low(0, 0)
                if live(e):
                    need(dve, b_PV, 2 * e + 2)
                    dve.reciprocal(rc1[:, :, :], O[:, :, :, HD0]).then_inc(b_rc, 1)
                if live(e):
                    need(dve, b_rc, e + 1)
                    dve.tensor_tensor(on1[:, :, :].rearrange("p e (h d) -> p e h d", h=H0), O[:, :, :, 0:HD0],
                                      rc1[:, :, :].unsqueeze(3).to_broadcast([P, 2, H0, HD0]), ALU.mult)\
                        .then_inc(b_on, 1)
                    need(dve, b_on, e + 1)
                    need(dve, b_sB, e + 1)
                    dve.tensor_tensor(sum1[:, 0, :], on1[:, 0, :], selfB[:, e, :], ALU.add).then_inc(b_sum, 1)
                    need(dve, b_sum, 2 * e + 1)
                    dve.tensor_tensor(sum1[:, 1, :], sum1[:, 0, :], on1[:, 1, :], ALU.add).then_inc(b_sum, 1)
                if live(f):
                    if isinstance(f, int) and f == 0:
                        dve.wait_ge(g_pad, 3)
                    need(dve, b_kv, f + 1)
                    need(dve, b_PV, 2 * (f - 1))
                    dve.tensor_tensor(VW[:, v, :, :, 0:HD0],
                                      bank[2][0:HC * NG, 0:288].rearrange("p (e h d) -> p e h d", e=2, d=HD0),
                                      cst("bd_v")[0:HC * NG, :].rearrange("p (h d) -> p h d", d=HD0).unsqueeze(1)
                                      .to_broadcast([HC * NG, 2, H1P, HD0]), ALU.mult).then_inc(b_VW, 1)
                if live(e):
                    need(dve, b_sum, 2 * e + 2)
                    dve.scalar_tensor_tensor(out=X[:, e, :], in0=sum1[:, 1, :], scalar=0.0, in1=X[:, e, :],
                                             op0=ALU.max, op1=ALU.add).then_inc(b_x2, 1)

            def statistics(g):
                dve.bn_stats(st2[:, :], X[:, g, :]).then_inc(c_bn, 1)

            def aggregated(g):
                need(dve, c_bn, 2 * g + 1)
                need(dve, c_ve, g)
                need(dve, c_xn, g)
                dve.memset(carrier[:, :], 0.0)
                dve.bn_aggr(mv2[:, :], st2[:, :]).then_inc(c_bn, 1)

            def centred(g):
                need(dve, c_bn, 2 * g + 2)
                need(dve, c_rs, g + 1)
                need(dve, c_xT, g)
                dve.tensor_scalar(xn2[:, :], X[:, g, :], mv2[:, 0:1], rs2[:, :], ALU.subtract, ALU.mult)\
                    .then_inc(c_xn, 1)

            def units_low(g, u):
                need(dve, c_u, 2 * g + 2)
                need(dve, c_pj, 8 * (g - 1))
                dve.tensor_tensor(uTl[:, u, :], uT2[:, u, :], uTh[:, u, :], ALU.subtract).then_inc(c_ul, 1)

            slots(dve, l1_slot, 4, NB - 2, NB + 3)
            dve.wait_ge(b_x2, NB)
            dve.wait_ge(e_l, NB)
            dve.memset(nm2[:, :], 0.0).then_inc(c_const, 1)
            dve.tensor_tensor(bsum2[:, :], bcv("attn_b"), bcv("ff_b"), ALU.add).then_inc(c_const, 1)
            inv_s = 1.41421 / 2.0 ** 0.5

            def l2_slot(t, u):
                g, f, a, e = t, t - 1, t - 2, t - 3
                lead, front, att, tail = live(g), live(f), live(a), live(e)
                v = 1 - u

                def masked(r):
                    if isinstance(a, int) and a == 0 and r == 0:
                        dve.wait_ge(d_mt, 16)
                    need(dve, c_ST, 4 * a + r + 1)
                    need(dve, c_PV, 4 * a + r - 1)
                    dve.tensor_tensor(P2[:, r % 2, :].rearrange("p (h q) -> p h q", h=G),
                                      bank[4 + r % 2][:, :].rearrange("p (h q) -> p h q", h=G),
                                      maskT[:, one(a), :].to_broadcast([P, G, S]), ALU.add).then_inc(c_SM, 1)

                def normalised(r):
                    half, c0 = r % 2, 4 * (r // 2)
                    O = bank[6][:, 0:G * (HD2 + 1)].rearrange("p (h d) -> p h d", h=G)
                    need(dve, c_PV, 4 * a + r + 1)
                    dve.reciprocal(rc2[:, r % 2, :], O[:, :, HD2]).then_inc(c_rc, 1)
                    need(dve, c_rc, 4 * a + r + 1)
                    need(dve, c_OT, 2 * a)
                    dve.tensor_tensor(O2[:, c0:c0 + G, half, :], O[:, :, 0:HD2],
                                      rc2[:, r % 2, :].unsqueeze(2).to_broadcast([P, G, HD2]), ALU.mult)\
                        .then_inc(c_O, 1)

                def rotate(j):
                    src = qkt[:, j % 2, :].rearrange("p (h d) -> p h d", d=HD2)
                    need(dve, c_cp, 4 * f + j + 1)
                    need(dve, c_rot, 4 * f + j)
                    dve.tensor_tensor(rcos[:, :, :], src[:, :, 0:ROT],
                                      cst("cos").unsqueeze(1).to_broadcast([P, 8, ROT]), ALU.mult)\
                        .then_inc(c_rope, 1)
                    for n in range(2):
                        x0, x1 = (1 - n) * ROT // 2, n * ROT // 2
                        last = dve.tensor_tensor(rsin[:, :, x1:x1 + ROT // 2], src[:, :, x0:x0 + ROT // 2],
                                                 cst("sin")[:, x1:x1 + ROT // 2].unsqueeze(1)
                                                 .to_broadcast([P, 8, ROT // 2]), ALU.mult)
                    last.then_inc(c_rope, 1)

                def rounded(j):
                    need(dve, c_Ts, 4 * f + j + 1)
                    need(dve, c_G, 4 * f)
                    dve.tensor_copy(qkB[:, j % 2, 4 * (j // 2):4 * (j // 2) + 4, :],
                                    qkT[:, v, j % 2, 4 * (j // 2):4 * (j // 2) + 4, :]).then_inc(c_B, 1)

                def maxima(r):
                    half, c0 = r % 2, 4 * (r // 2)
                    need(dve, c_G, 4 * f + r + 1)
                    if r == 0:
                        need(dve, c_mk, f + 1)
                        need(dve, c_nm, 5 * f)
                    need(dve, c_jk, 16 * f + 4 * r)
                    dve.memset(carrier[:, :], 0.0)
                    for c in range(4):
                        dve.tensor_tensor_reduce(junk[:, c, :], bank[7 - 3 * (r % 2)][:, c * S:(c + 1) * S], mask_b[:, :],
                                                 1.0, -3e38, ALU.add, ALU.max, m2[:, half, c0 + c:c0 + c + 1])\
                            .then_inc(c_jk, 1)

                if tail:
                    need(dve, c_o, e + 1)
                    need(dve, c_xb, e + 1)
                    need(dve, c_y, e)
                    need(dve, c_sq, e)
                    dve.tensor_tensor(x3[:, :], bank[0][:, 384:512], xb2[:, :], ALU.add).then_inc(c_x3, 1)
                if front:
                    rotate(0)
                if att:
                    masked(0)
                if front:
                    rotate(1)
                if att:
                    masked(1)
                if tail:
                    need(dve, c_sq, e + 1)
                    dve.tensor_reduce(ss3[:, :], sq3[:, :], AX, ALU.add).then_inc(c_ss, 1)
                if lead:
                    statistics(g)
                if front:
                    rounded(0)
                if tail:
                    need(dve, c_ss, e + 1)
                    need(dve, c_r3, e)
                    dve.tensor_scalar(ms3[:, :], ss3[:, :], 1.0 / D, 1e-6, ALU.mult, ALU.add).then_inc(c_ms, 1)
                if lead:
                    aggregated(g)
                if att:
                    normalised(0)
                if front:
                    rotate(2)
                if att:
                    masked(2)
                if front:
                    rounded(1)
                if att:
                    normalised(1)
                if front:
                    rotate(3)
                if att:
                    masked(3)
                if lead:
                    centred(g)
                if front:
                    if isinstance(f, int) and f == 0:
                        dve.wait_ge(d_mn, 16)
                    need(dve, c_jk, 16 * f)
                    dve.tensor_copy(mask_b[:, :], maskN[:, f, :]).then_inc(c_mk, 1)
                    rounded(2)
                if att:
                    normalised(2)
                if front:
                    maxima(0)
                if att:
                    normalised(3)
                if front:
                    rounded(3)
                    maxima(1)
                if lead:
                    units_low(g, u)
                if front:
                    maxima(2)
                if tail:
                    if isinstance(e, int) and e == 0:
                        dve.wait_ge(d_ab3, 16)
                    need(dve, c_r3, e + 1)
                    need(dve, c_out, e)
                    dve.scalar_tensor_tensor(out=y3[:, :], in0=x3[:, :], scalar=rs3[:, :], in1=AB3[:, e, 0:D],
                                             op0=ALU.mult, op1=ALU.mult).then_inc(c_y, 1)
                if front:
                    maxima(3)
                    parts = nm2[:, :].rearrange("p (h n) -> p h n", h=2)
                    need(dve, c_jk, 16 * f + 16)
                    need(dve, c_mT, f)
                    dve.tensor_scalar(parts[:, :, 0:8], m2[:, :, :], -1.0, None, ALU.mult).then_inc(c_nm, 1)
                    need(dve, c_gel, f + 1)
                    need(dve, c_pj, 8 * f + 8)
                    need(dve, c_o, f - 1)
                    dve.scalar_tensor_tensor(out=ffT[:, v, :, :].rearrange("p c s -> p (c s)"), in0=bank[2][:, :],
                                             scalar=inv_s, in1=gel[:, :, :].rearrange("p c s -> p (c s)"),
                                             op0=ALU.mult, op1=ALU.mult).then_inc(c_ff, 1)
                    need(dve, c_nm, 5 * f + 1)
                    dve.scalar_tensor_tensor(out=mr2[:, 0, :, :], in0=m2[:, :, :], scalar=-1.0,
                                             in1=parts[:, :, 0:8], op0=ALU.mult, op1=ALU.subtract).then_inc(c_nm, 1)
                    need(dve, c_nm, 5 * f + 2)
                    dve.tensor_copy(parts[:, :, 8:16], mr2[:, 0, :, :]).then_inc(c_nm, 1)
                    need(dve, c_nm, 5 * f + 3)
                    dve.tensor_tensor(mr2[:, 1, :, :], mr2[:, 0, :, :], parts[:, :, 8:16], ALU.subtract)\
                        .then_inc(c_nm, 1)
                    need(dve, c_nm, 5 * f + 4)
                    dve.tensor_copy(parts[:, :, 16:24], mr2[:, 1, :, :]).then_inc(c_nm, 1)
                if tail:
                    need(dve, c_y, e + 1)
                    dve.tensor_tensor(X[:, e, :], y3[:, :], AB3[:, e, D:2 * D], ALU.add).then_inc(c_out, 1)

            slots(dve, l2_slot, 4, NB, NB + 3, begin=1)

        @block.scalar
        def _(act):
            act.wait_ge(d_cond, 64)
            act.activation(siluT[:, :], condT[:, :], ACT.Silu).then_inc(s_act, 1)
            act.activation(cabs[:, :], condR[:, :], ACT.Abs).then_inc(s_act, 1)
            act.activation(wabs[:, :], wcc("proj"), ACT.Abs).then_inc(s_act, 1)
            act.wait_ge(d_cst, 16)
            act.activation(identB[:, :], ident, ACT.Copy).then_inc(s_sel, 1)
            act.activation(sel0[:, :, :], cst("sel4").unsqueeze(2).to_broadcast([P, NC0, P]), ACT.Copy)\
                .then_inc(s_sel, 1)
            act.activation(sel12[:, :, :], cst("sel4")[0:3 * NC0, :].unsqueeze(2).to_broadcast([3 * NC0, NC0, S]),
                           ACT.Copy).then_inc(s_sel, 1)
            act.wait_ge(s_R0T, 1)
            act.activation(AB0T[:, :, :], bank[6][:, 0:2 * NB].rearrange("p (n b) -> p n b", n=2), ACT.Copy)\
                .then_inc(s_AB0T, 1)
            act.wait_ge(s_AB0T, 1)
            act.wait_ge(d_bc, 32)

            def l0_slot(t, u):
                g, f, e = t, t - 1, t - 2

                def exps(r):
                    need(act, a_ST, NC0 * f + r + 1)
                    need(act, a_PV, NC0 * f + r - 1)
                    act.activation(P0[:, r % 2, :], bank[3 + (r + 1) % 3][:, :], ACT.Exp).then_inc(a_P, 1)

                def rounded(n):
                    need(act, a_qk, 2 * g + 1 + n)
                    need(act, a_pack, 2 * g - 1 + n)
                    c0 = COL_COLS[("part_q", "part_k")[n]][0]
                    act.activation(rnd[:, n, :], bank[1 + n][:, :], ACT.Copy, scale=cols_sb[:, c0:c0 + 1])\
                        .then_inc(a_rnd, 1)

                if live(g):
                    need(act, a_xnT, g + 1)
                    need(act, a_v, g)
                    need(act, a_qk, 2 * g)
                    act.activation(ut[:, :], bank[0][:, 0:S], ACT.Identity, bias=AB0T[:, 1, one(g)],
                                   scale=AB0T[:, 0, one(g)]).then_inc(a_u, 1)
                if live(e):
                    need(act, a_atT, e + 1)
                    need(act, a_o, e)
                    act.activation(at0T[:, :], bank[7][:, 256:384], ACT.Copy).then_inc(a_atS, 1)
                if live(e):
                    if isinstance(e, int) and e == 0:
                        act.wait_ge(d_adj, 16 * (NB // GM) * (GM + 1))
                    need(act, g_cnt, 2 * e)
                    need(act, g_lab, 2 * e)
                    act.activation(labF0[:, :], adj0[:, e, :], ACT.Copy).then_inc(g_flt, 1)
                    act.activation(labF1[:, :], adj1[:, e, :], ACT.Copy).then_inc(g_flt, 1)
                if live(g):
                    rounded(0)
                if live(f):
                    need(act, a_mT, f + 1)
                    need(act, a_ST, NC0 * f)
                    act.activation(mT0[:, :], bank[7][:, 128:256], ACT.Copy).then_inc(a_mTs, 1)
                    exps(0)
                    exps(1)
                if live(g):
                    rounded(1)
                if live(f):
                    exps(2)
                    exps(3)

            slots(act, l0_slot, 4, NB - 2, NB + 2)
            def l1_slot(t, u):
                g, f, a, e = t, t - 1, t - 2, t - 3
                v = 1 - u

                def exps(d):
                    need(act, b_sub, 2 * a + 1 + d)
                    need(act, b_eT, 2 * a - 1 + d)
                    act.activation(ex1[:, d, 0:H0 * NG], aff[:, d, :], ACT.Exp).then_inc(b_ex, 1)

                if live(g):
                    need(act, b_xT, g + 1)
                    need(act, b_sf, g)
                    act.activation(xT1[:, :], bank[0][:, 0:S], ACT.Copy).then_inc(b_xTs, 1)
                if live(e):
                    for d in range(2):
                        need(act, b_eT, 2 * e + 1 + d)
                        need(act, b_PV, 2 * e - 1 + d)
                        act.activation(exT[:, d, :], bank[5 + d][0:HC * NG, 0:NC1 * S], ACT.Copy).then_inc(b_eTs, 1)
                if live(f):
                    need(act, b_q, f + 1)
                    need(act, b_S, 2 * (f - 1))
                    need(act, b_kbd, 2 * f)
                    for d in range(2):
                        c0 = COL_COLS["bk1"][0] + d
                        act.activation(kT1[:, d, :], bank[1][:, 256 + NG * d:256 + NG * (d + 1)], ACT.Identity,
                                       bias=cols_sb[:, c0:c0 + 1]).then_inc(b_kT, 1)
                    for d in range(2):
                        c0 = COL_COLS["bq1"][0] + d
                        act.activation(qT1[:, v, d, :], bank[1][:, d * S:(d + 1) * S], ACT.Identity,
                                       bias=cols_sb[:, c0:c0 + 1]).then_inc(b_qs, 1)
                if live(a):
                    exps(0)
                    exps(1)
                if live(g):
                    cs = bass.ds(g * W2P, W2P)
                    act.activation(w2h[:, cs], w2raw[:, cs], ACT.Copy).then_inc(e_h, 1)
                    need(act, b_sT, g + 1)
                    need(act, b_q, g - 1)
                    act.activation(selfT[:, u, :], bank[0][:, 256:384], ACT.Copy).then_inc(b_sTs, 1)
                    act.activation(selfR[:, u, :, :],
                                   bank[0][:, 256:256 + NG].unsqueeze(1).to_broadcast([P, HC, NG]), ACT.Copy)\
                        .then_inc(b_sTs, 1)
                if isinstance(t, int) and t == NB + 1:
                    act.wait_ge(s_cqT, 2)
                    units(0, 0)

            def units(g, u):
                need(act, c_xT, g + 1)
                need(act, c_pj, 8 * (g - 1))
                need(act, c_ul, g - 1)
                act.activation(uT2[:, u, :], bank[0][:, 0:S], ACT.Identity, bias=AB2T[:, 1, one(g)],
                               scale=AB2T[:, 0, one(g)]).then_inc(c_u, 1)
                act.activation(uTh[:, u, :], bank[0][:, 0:S], ACT.Identity, bias=AB2T[:, 1, one(g)],
                               scale=AB2T[:, 0, one(g)]).then_inc(c_u, 1)

            act.wait_ge(d_w2, 16)
            slots(act, l1_slot, 4, NB, NB + 3)
            act.wait_ge(b_x2, NB)

            def l2_slot(t, u):
                g, f, a, e = t, t - 1, t - 2, t - 3
                lead, front, att, tail = live(g), live(f), live(a), live(e)
                v = 1 - u

                def exps(r):
                    need(act, c_SM, 4 * a + r + 1)
                    act.activation(P2[:, r % 2, :], P2[:, r % 2, :], ACT.Exp).then_inc(c_P, 1)

                def taken(j):
                    need(act, c_pj, 8 * f + j + 1)
                    need(act, c_T, 4 * f + j - 1)
                    act.activation(qkt[:, j % 2, :], bank[1 + j % 2][:, :], ACT.Copy, scale=HD2 ** -0.5)\
                        .then_inc(c_cp, 1)

                def turned(j):
                    need(act, c_T, 4 * f + j + 1)
                    need(act, c_ST, 4 * (f - 1))
                    act.activation(qkT[:, v, j % 2, 4 * (j // 2):4 * (j // 2) + 4, :],
                                   bank[3][:, :].rearrange("p (c s) -> p c s", s=S), ACT.Copy).then_inc(c_Ts, 1)

                def val(n):
                    need(act, c_pj, 8 * f + 5 + n)
                    need(act, c_PV, 4 * (f - 1))
                    act.activation(V2[:, v, 8 * n:8 * n + 8, 0:HD2],
                                   bank[1 + n][:, :].rearrange("p (h d) -> p h d", d=HD2), ACT.Copy).then_inc(c_V, 1)

                def results(n):
                    need(act, c_OT, 2 * a + n + 1)
                    need(act, c_o, a)
                    act.activation(OT2[:, 4 * n:4 * n + 4, :],
                                   bank[3][:, :].rearrange("p (c s) -> p c s", s=S),
                                   ACT.Copy).then_inc(c_OTs, 1)

                if front:
                    taken(0)
                    taken(1)
                if att:
                    exps(0)
                if tail:
                    need(act, c_x3, e + 1)
                    need(act, c_ss, e)
                    act.activation(sq3[:, :], x3[:, :], ACT.Square).then_inc(c_sq, 1)
                if front:
                    turned(0)
                if att:
                    exps(1)
                if front:
                    taken(2)
                    turned(1)
                if att:
                    exps(2)
                if front:
                    taken(3)
                    turned(2)
                if att:
                    exps(3)
                if front:
                    val(0)
                    turned(3)
                    val(1)
                if att:
                    results(0)
                if lead:
                    units(g, u)
                if front:
                    need(act, c_pj, 8 * f + 7)
                    need(act, c_ff, f)
                    act.activation(gel[:, :, :].rearrange("p c s -> p (c s)"), bank[1][:, :], ACT.Gelu,
                                   scale=2.0 ** 0.5 / 1.41421).then_inc(c_gel, 1)
                if att:
                    results(1)
                    need(act, c_tab, a)
                    act.activation(tab[:, :], eps_c[:, :], ACT.Exp).then_inc(c_tab, 1)
                if front:
                    need(act, c_mT, f + 1)
                    need(act, c_ST, 4 * f)
                    act.activation(mT2[:, :], bank[7][:, 0:128], ACT.Copy).then_inc(c_mTs, 1)

            slots(act, l2_slot, 4, NB, NB + 3, begin=1)

        @block.gpsimd
        def _(pool):
            pool.memset(onesP[:, :], 1.0).then_inc(s_one, 1)
            pool.memset(eps_c[:, :], EPS).then_inc(s_const, 1)
            pool.memset(neg_half[:, :], -0.5).then_inc(s_const, 1)
            pool.memset(nm0[:, :], 0.0).then_inc(s_const, 1)
            for n in range(2):
                pool.memset(V0[:, n, :, HD0], 1.0)
                pool.memset(V0[:, n, :, HD0 + 1:VW0], 0.0).then_inc(s_const, 1)
            pool.wait_ge(s_const, 5)

            def deviations(first, end):
                pool.wait_ge(s_mean0, end)
                pool.tensor_tensor(rstd0[:, first:end], mean0[:, first:end, 1],
                                   eps_c[:, :].to_broadcast([P, end - first]), ALU.add).then_inc(s_ve, 1)
                pool.wait_ge(s_ve, 1 if first == 0 else 2)
                pool.tensor_tensor(rstd0[:, first:end], rstd0[:, first:end], neg_half[:, first:end], ALU.pow)\
                    .then_inc(s_rstd0, 1)

            deviations(0, 1)
            deviations(1, NB)
            pool.wait_ge(d_bc, 32)
            w_lab = bcv("w_bias")

            def l0_slot(t, u):
                f, e = t - 1, t - 2
                if live(e):
                    need(pool, a_h1, e)
                    pool.tensor_tensor(xb0[:, :], X[:, e, :], bcv("bp0"), ALU.add).then_inc(a_xb, 1)
                if live(e):
                    for n, (flt, lab, parts, m) in enumerate(((labF0, lab0, P, NG), (labF1, lab1, GM * NG, GN))):
                        need(pool, g_flt, 2 * e + 1 + n)
                        need(pool, g_vb, 2 * e - 1 + n)
                        pool.tensor_tensor(lab[:, :].rearrange("p (m l) -> p m l", l=NL),
                                           flt[:, :].rearrange("p (m l) -> p m l", l=NL),
                                           w_lab[0:parts, :].unsqueeze(1).to_broadcast([parts, m, NL]),
                                           ALU.mult).then_inc(g_lab, 1)
                if live(e):
                    need(pool, a_bn, 2 * e + 2)
                    pool.tensor_tensor(ve0[:, :], mv0[:, u, 1:2], eps_c[:, :], ALU.add).then_inc(a_ve, 1)
                    need(pool, a_ve, e + 1)
                    need(pool, a_x1, e - 1)
                    pool.tensor_tensor(rs0[:, u, :], ve0[:, :], neg_half[:, 0:1], ALU.pow).then_inc(a_rs, 1)
                    if isinstance(e, int) and e == 0:
                        pool.wait_ge(d_ab0, 16)
                    pool.tensor_tensor(hb0[:, u, :], h1[:, u, :], AB0[:, e, D:2 * D], ALU.add).then_inc(a_hb, 1)

            slots(pool, l0_slot, 4, NB - 2, NB + 2)
            pool.wait_ge(a_x1, NB)
            pool.memset(ex1[:, :, H0 * NG:H1P * NG], 0.0).then_inc(g_pad, 1)
            for n in range(2):
                pool.tensor_copy(VW[:, n, :, :, HD0],
                                 cst("bd_v")[0:HC * NG, :].rearrange("p (h d) -> p h d", d=HD0)[:, :, 0].unsqueeze(1)
                                 .to_broadcast([HC * NG, 2, H1P])).then_inc(g_pad, 1)

            pool.memset(V2[:, 0, :, HD2], 1.0).then_inc(c_const, 1)
            pool.memset(V2[:, 1, :, HD2], 1.0).then_inc(c_const, 1)
            pool.tensor_copy(sel2[:, :, :], cst("sel8").unsqueeze(2).to_broadcast([P, HC2, P])).then_inc(c_const, 1)

            def l1_slot(t, u):
                f, a = t - 1, t - 2
                for d in range(2):
                    if live(a):
                        need(pool, b_mx, 2 * a + 1 + d)
                        pool.tensor_tensor(aff[:, d, :].rearrange("p (h m) -> p h m", m=NG),
                                           aff[:, d, :].rearrange("p (h m) -> p h m", m=NG),
                                           mx1[:, d, :].unsqueeze(2).to_broadcast([P, H0, NG]), ALU.subtract)\
                            .then_inc(b_sub, 1)
                    if live(f):
                        need(pool, b_kT, 2 * f + 1 + d)
                        need(pool, b_S, 2 * (f - 1))
                        pool.tensor_tensor(kbd[:, 1 - u, d, :].rearrange("p (h m) -> p h m", m=NG),
                                           kT1[:, d, :].unsqueeze(1).to_broadcast([P, H0, NG]),
                                           cst("bd_k").rearrange("p (h m) -> p h m", m=NG), ALU.mult)\
                            .then_inc(b_kbd, 1)
                if live(t):
                    need(pool, b_self, t + 1)
                    pool.tensor_tensor(selfB[:, t, :], selfTok[:, :], bout1[:, :], ALU.add).then_inc(b_sB, 1)
                    cs = bass.ds(t * W2P, W2P)
                    need(pool, e_h, t + 1)
                    pool.tensor_tensor(w2l[:, cs], w2raw[:, cs], w2h[:, cs].bitcast(F32), ALU.subtract)\
                        .then_inc(e_l, 1)
                if isinstance(t, int) and t == NB:
                    deviation(0)

            def deviation(g):
                need(pool, c_bn, 2 * g + 2)
                pool.tensor_tensor(ve2[:, :], mv2[:, 1:2], eps_c[:, :], ALU.add).then_inc(c_ve, 1)
                need(pool, c_ve, g + 1)
                need(pool, c_xn, g)
                pool.tensor_tensor(rs2[:, :], ve2[:, :], neg_half[:, 0:1], ALU.pow).then_inc(c_rs, 1)

            pool.wait_ge(g_bc, 1)
            slots(pool, l1_slot, 4, NB, NB + 2)
            pool.wait_ge(b_x2, NB)
            pool.wait_ge(c_const, 5)

            def l2_slot(t, u):
                g, f, a, e = t, t - 1, t - 2, t - 3
                lead, front, att, tail = live(g), live(f), live(a), live(e)

                def rotated(j):
                    need(pool, c_rope, 8 * f + 2 * j + 2)
                    pool.tensor_tensor(qkt[:, j % 2, :].rearrange("p (h d) -> p h d", d=HD2)[:, :, 0:ROT],
                                       rcos[:, :, :], rsin[:, :, :], ALU.add).then_inc(c_rot, 1)

                if front:
                    rotated(0)
                    rotated(1)
                if tail:
                    need(pool, c_ms, e + 1)
                    need(pool, c_y, e)
                    pool.tensor_tensor(rs3[:, :], ms3[:, :], neg_half[:, 0:1], ALU.pow).then_inc(c_r3, 1)
                if lead:
                    deviation(g)
                if front:
                    rotated(2)
                    rotated(3)
                if att:
                    need(pool, c_x3, a)
                    pool.tensor_tensor(xb2[:, :], X[:, a, :], bsum2[:, :], ALU.add).then_inc(c_xb, 1)

            slots(pool, l2_slot, 4, NB, NB + 3, begin=1)


def bf16_rounded(table):
    import numpy as np
    bits = table.astype(np.float32).view(np.uint32)
    return ((bits + 0x7FFF + (bits >> 16 & 1)) & 0xFFFF0000).astype(np.uint32).view(np.float32)


def laid_out(inputs):
    import numpy as np
    g = {k: np.ascontiguousarray(v) for k, v in inputs.items()}

    def per_head(t):
        return np.ascontiguousarray(g["L0_cond_Wqkv"].reshape(H0, HD0, 3, D)[:, :, t]), \
            np.ascontiguousarray(g["L0_cond_bqkv"].reshape(H0, HD0, 3)[:, :, t])

    def packed(w):
        return np.repeat(w.reshape(H0, 1, HD0, -1), 4, axis=1).reshape(H0 * 4 * HD0, -1)

    (wq, bq), (wk, bk), (wv, bv) = (per_head(t) for t in range(3))
    def placed(w):
        return w.reshape(NC0, G, HD0, -1).transpose(1, 0, 2, 3).reshape(D, -1)

    w0 = np.concatenate([packed(wq).T, packed(wk).T, placed(wv).T], axis=1)
    bias_qk0 = np.concatenate([packed(bq[..., None]).reshape(NC0, P), packed(bk[..., None]).reshape(NC0, P)], axis=1)
    w_self = g["L1_cond_W_self"]
    wout = g["L1_cond_Wout"].reshape(2, D, D)
    pad = np.zeros((2, (H1P - H0) * HD0, D), np.float32)
    wout = np.concatenate([wout, pad], axis=1)
    w1 = np.concatenate([placed(g["L0_cond_Wp"].T), w_self[:, :D].T, g["L1_cond_Wq"][0].T, g["L1_cond_Wq"][1].T,
                         g["L1_cond_Wk"][0].T, g["L1_cond_Wk"][1].T, wout[0].T, wout[1].T], axis=1)
    wc = np.concatenate([g["L0_cond_Wg"].T, g["L0_cond_Wb"].T, w_self[:, D:].T, g["L2_cond_cond_w"],
                         g["L3_cond_w_proj"].T], axis=1)
    rows = np.concatenate([g[k].reshape(-1) for k in (
        "L0_cond_bg", "L0_cond_bb", "L0_cond_ln_g", "L0_cond_ln_b", "L2_cond_cond_b", "L2_cond_ln_w",
        "L2_cond_ln_b", "L3_cond_b_proj", "L3_cond_rms_weight")])[None]
    bc = np.concatenate([placed(bv).reshape(-1)] + [g[k].reshape(-1) for k in (
        "L0_cond_bp", "L1_cond_b_self", "L1_cond_bout", "L2_cond_attn_proj_b", "L2_cond_ff_proj_b",
        "L1_cond_w_bias", "L1_cond_b_bias")])[None]
    part = np.arange(P) % 32 // HD0
    part_q, part_k = np.array([0, 1, 0, 1], np.float32)[part], np.array([0, 0, 1, 1], np.float32)[part]
    cols = np.stack([*g["L1_cond_bq"], *g["L1_cond_bk"], part_q, part_k], axis=1)
    bd_k = (np.arange(P)[:, None] // HD0 == np.arange(H0 * NG)[None] // NG).astype(np.float32)
    bd_v = (np.arange(P)[:, None] // NG == np.arange(HC * HD0)[None] // HD0).astype(np.float32)
    inv_freq = np.float32(1.0) / np.float32(10000.0) ** (np.arange(0, ROT, 2, dtype=np.float32) / np.float32(ROT))
    freqs = np.arange(S, dtype=np.float32)[:, None] * inv_freq[None]
    cos, sin = bf16_rounded(np.cos(freqs)), bf16_rounded(np.sin(freqs))
    cst = np.concatenate([np.eye(P, dtype=np.float32), bd_k, np.tile(bd_v, (1, NC1)), cos, cos, -sin, sin,
                          (np.arange(P)[:, None] % NC0 == np.arange(NC0)[None]).astype(np.float32),
                          (np.arange(P)[:, None] % 8 == np.arange(8)[None]).astype(np.float32)], axis=1)
    return {
        "x": g["x"], "cond_t": g["cond_1024"].T, "cond_r": g["cond_1024"], "w0": w0, "bias_qk0": bias_qk0,
        "w1": w1, "wc": wc, "rows": rows, "bc": bc, "cols": cols, "cst_d": cst, "adj": g["mask_BxSxSx11_ik0"],
        "w2": g["L2_cond_proj_in_w"],
        "attn_w": g["L2_cond_attn_proj_w"], "ff_w": g["L2_cond_ff_proj_w"],
        "mask": g["mask_Bx1xSxS_ff0"].reshape(NB, S, S),
        "mask_t": g["mask_Bx1xSxS_ff0"].reshape(NB, S, S).transpose(0, 2, 1),
    }


def kernel(**inputs):
    import numpy as np
    import concourse.bacc as bacc
    from concourse.bass_utils import run_bass_kernel_spmd

    nc = bacc.Bacc("TRN2", target_bir_lowering=False, num_devices=1)
    arrays, args = {}, {}
    for name, a in laid_out(inputs).items():
        a = np.ascontiguousarray(a)
        arrays[f"in_{name}"] = a
        args[name] = nc.dram_tensor(f"in_{name}", a.shape, mybir.dt.from_np(a.dtype), kind="ExternalInput").ap()
    args["out"] = nc.dram_tensor("out_0", (NB, S, D), F32, kind="ExternalOutput").ap()
    build(nc, **args)
    got = run_bass_kernel_spmd(nc, [arrays], core_ids=[0])
    return got.results[0]["out_0"]
```
